# Optimizing a Trainium2 kernel written in Bass

```python
import numpy as np
import jax
import jax.numpy as jnp

def _softmax(x, axis=-1):
    return jax.nn.softmax(x, axis=axis)

def _gelu(x):
    return jax.nn.gelu(x, approximate=True)

def _silu(x):
    return jax.nn.silu(x)

def _sigmoid(x):
    return jax.nn.sigmoid(x)

def _layernorm(x, axis=-1, eps=1e-05):
    m = jnp.mean(x, axis=axis, keepdims=True)
    v = jnp.var(x, axis=axis, keepdims=True)
    return (x - m) / jnp.sqrt(v + eps)

def _scatter_add(tgt, idx, src, axis=0):
    return tgt.at[idx].add(src)

def _segment_sum(src, seg, n):
    return jax.ops.segment_sum(src, seg, n)
kernel_name = 'mk_hybrid_d1_jaxref_r8_1b6fe1'

def setup_inputs(seed: int=0):
    np.random.seed(seed)
    _w = jnp.asarray

    def _L0_attn_a_setup():
        import jax, jax.numpy as jnp
        import numpy as np
        import math
        D_MODEL = 256
        N_HEADS = 16
        Q_LORA = 192
        KV_LORA = 64
        D_NOPE = 128
        D_ROPE = 64
        D_V = 128
        EPS = 1e-05

        def _layernorm(x, w, b):
            mu = jnp.mean(x, axis=-1, keepdims=True)
            var = jnp.mean(jnp.square(x - mu), axis=-1, keepdims=True)
            return (x - mu) * jax.lax.rsqrt(var + EPS) * w + b

        def _rope_tables(seq_len, dim, dtype):
            inv_freq = 1.0 / 10000.0 ** (np.arange(0, dim, 2, dtype=np.float32) / dim)
            t = np.arange(seq_len, dtype=np.float32)
            freqs = np.outer(t, inv_freq)
            emb = np.concatenate([freqs, freqs], -1)
            return (jnp.asarray(np.cos(emb), dtype), jnp.asarray(np.sin(emb), dtype))

        def _rotate_half(x):
            x1, x2 = jnp.split(x, 2, axis=-1)
            return jnp.concatenate([-x2, x1], axis=-1)

        def _apply_rope(x, cos, sin):
            c = cos[None, :, None, :]
            s = sin[None, :, None, :]
            return x * c + _rotate_half(x) * s
        key = jax.random.key(seed)
        ks = jax.random.split(key, 8)

        def lin(k, out_d, in_d):
            return jax.random.normal(k, (out_d, in_d), jnp.float32) * (1.0 / math.sqrt(in_d))
        B, S = (2, 256)
        return {'hidden_states': jax.random.normal(ks[0], (B, S, D_MODEL), jnp.float32), 'q_a_w': lin(ks[1], Q_LORA, D_MODEL), 'q_a_ln_w': jnp.ones((Q_LORA,), jnp.float32), 'q_a_ln_b': jnp.zeros((Q_LORA,), jnp.float32), 'q_b_w': lin(ks[2], N_HEADS * D_NOPE, Q_LORA), 'q_rope_w': lin(ks[3], N_HEADS * D_ROPE, Q_LORA), 'kv_a_w': lin(ks[4], KV_LORA + D_ROPE, D_MODEL), 'kv_a_ln_w': jnp.ones((KV_LORA,), jnp.float32), 'kv_a_ln_b': jnp.zeros((KV_LORA,), jnp.float32), 'kv_b_w': lin(ks[5], N_HEADS * (D_NOPE + D_V), KV_LORA), 'o_w': lin(ks[6], D_MODEL, N_HEADS * D_V)}
    _L0_attn_a_in = _L0_attn_a_setup()

    def _L0_attn_b_setup():
        import jax, jax.numpy as jnp
        import numpy as np
        HIDDEN = 256
        INTER = 512
        KCONV = 512
        DT_RANK = 128
        SSM_N = 16
        B_SZ, SEQ = (2, 512)
        key = jax.random.key(seed)
        ks = jax.random.split(key, 8)
        s = 0.02
        return {'hidden_states': jax.random.normal(ks[0], (B_SZ, SEQ, HIDDEN), jnp.float32), 'W_in': jax.random.normal(ks[1], (2 * INTER, HIDDEN), jnp.float32) * s, 'conv_w': jax.random.normal(ks[2], (INTER, KCONV), jnp.float32) * s, 'W_x': jax.random.normal(ks[3], (DT_RANK + 2 * SSM_N, INTER), jnp.float32) * s, 'W_dt': jax.random.normal(ks[4], (INTER, DT_RANK), jnp.float32) * s, 'b_dt': jax.random.normal(ks[5], (INTER,), jnp.float32) * s, 'D': jnp.ones((INTER,), jnp.float32), 'W_out': jax.random.normal(ks[6], (HIDDEN, INTER), jnp.float32) * s}
    _L0_attn_b_in = _L0_attn_b_setup()

    def _L0_ffn_setup():
        import jax, jax.numpy as jnp
        import numpy as np
        HIDDEN = 256
        INTER = 1024
        COMPRESSION = 128.9

        def _n_ctrl(out_size, in_size):
            return max(16, int(out_size * in_size / COMPRESSION))

        def _catmull_rom_grid(n_ctrl, n_samples):
            t = np.linspace(0.0, n_ctrl - 1.0, n_samples, dtype=np.float64)
            i = np.clip(np.floor(t).astype(np.int64), 0, n_ctrl - 2)
            f = (t - i).astype(np.float32)
            idx = np.stack([np.clip(i + k, 0, n_ctrl - 1) for k in (-1, 0, 1, 2)], axis=0)
            return (jnp.asarray(idx.astype(np.int32)), jnp.asarray(f))

        def spline_reconstruct(control_points, out_size, in_size):
            n = out_size * in_size
            idx, f = _catmull_rom_grid(control_points.shape[0], n)
            p0, p1, p2, p3 = (control_points[idx[0]], control_points[idx[1]], control_points[idx[2]], control_points[idx[3]])
            f2 = f * f
            f3 = f2 * f
            w = 0.5 * (2.0 * p1 + (p2 - p0) * f + (2.0 * p0 - 5.0 * p1 + 4.0 * p2 - p3) * f2 + (3.0 * p1 - p0 - 3.0 * p2 + p3) * f3)
            return w.reshape(out_size, in_size)
        key = jax.random.key(seed)
        k0, k1, k2, k3 = jax.random.split(key, 4)
        hidden_states = jax.random.normal(k0, (4, 256, HIDDEN), dtype=jnp.float32)
        gate_cp = jax.random.normal(k1, (_n_ctrl(INTER, HIDDEN),), dtype=jnp.float32) * 0.02
        up_cp = jax.random.normal(k2, (_n_ctrl(INTER, HIDDEN),), dtype=jnp.float32) * 0.02
        down_cp = jax.random.normal(k3, (_n_ctrl(HIDDEN, INTER),), dtype=jnp.float32) * 0.02
        return {'hidden_states': hidden_states, 'gate_cp': gate_cp, 'up_cp': up_cp, 'down_cp': down_cp}
    _L0_ffn_in = _L0_ffn_setup()
    _d = {'L0_attn_a_hidden_states': _L0_attn_a_in['hidden_states'], 'L0_attn_a_q_a_w': _L0_attn_a_in['q_a_w'], 'L0_attn_a_q_a_ln_w': _L0_attn_a_in['q_a_ln_w'], 'L0_attn_a_q_a_ln_b': _L0_attn_a_in['q_a_ln_b'], 'L0_attn_a_q_b_w': _L0_attn_a_in['q_b_w'], 'L0_attn_a_q_rope_w': _L0_attn_a_in['q_rope_w'], 'L0_attn_a_kv_a_w': _L0_attn_a_in['kv_a_w'], 'L0_attn_a_kv_a_ln_w': _L0_attn_a_in['kv_a_ln_w'], 'L0_attn_a_kv_a_ln_b': _L0_attn_a_in['kv_a_ln_b'], 'L0_attn_a_kv_b_w': _L0_attn_a_in['kv_b_w'], 'L0_attn_a_o_w': _L0_attn_a_in['o_w'], 'L0_attn_b_W_in': _L0_attn_b_in['W_in'], 'L0_attn_b_conv_w': _L0_attn_b_in['conv_w'], 'L0_attn_b_W_x': _L0_attn_b_in['W_x'], 'L0_attn_b_W_dt': _L0_attn_b_in['W_dt'], 'L0_attn_b_b_dt': _L0_attn_b_in['b_dt'], 'L0_attn_b_D': _L0_attn_b_in['D'], 'L0_attn_b_W_out': _L0_attn_b_in['W_out'], 'L0_ffn_gate_cp': _L0_ffn_in['gate_cp'], 'L0_ffn_up_cp': _L0_ffn_in['up_cp'], 'L0_ffn_down_cp': _L0_ffn_in['down_cp']}
    _x0 = _d['L0_attn_a_hidden_states']
    _d['L0_attn_a_hidden_states'] = jax.random.normal(jax.random.fold_in(jax.random.key(seed), 1), (8, 256, 256), dtype=_x0.dtype)
    del _x0
    return _d

def reference(L0_attn_a_hidden_states, L0_attn_a_q_a_w, L0_attn_a_q_a_ln_w, L0_attn_a_q_a_ln_b, L0_attn_a_q_b_w, L0_attn_a_q_rope_w, L0_attn_a_kv_a_w, L0_attn_a_kv_a_ln_w, L0_attn_a_kv_a_ln_b, L0_attn_a_kv_b_w, L0_attn_a_o_w, L0_attn_b_W_in, L0_attn_b_conv_w, L0_attn_b_W_x, L0_attn_b_W_dt, L0_attn_b_b_dt, L0_attn_b_D, L0_attn_b_W_out, L0_ffn_gate_cp, L0_ffn_up_cp, L0_ffn_down_cp):

    def _L0_attn_a_ref(hidden_states, q_a_w, q_a_ln_w, q_a_ln_b, q_b_w, q_rope_w, kv_a_w, kv_a_ln_w, kv_a_ln_b, kv_b_w, o_w):
        import jax, jax.numpy as jnp
        import numpy as np
        import math
        D_MODEL = 256
        N_HEADS = 16
        Q_LORA = 192
        KV_LORA = 64
        D_NOPE = 128
        D_ROPE = 64
        D_V = 128
        EPS = 1e-05

        def _layernorm(x, w, b):
            mu = jnp.mean(x, axis=-1, keepdims=True)
            var = jnp.mean(jnp.square(x - mu), axis=-1, keepdims=True)
            return (x - mu) * jax.lax.rsqrt(var + EPS) * w + b

        def _rope_tables(seq_len, dim, dtype):
            inv_freq = 1.0 / 10000.0 ** (np.arange(0, dim, 2, dtype=np.float32) / dim)
            t = np.arange(seq_len, dtype=np.float32)
            freqs = np.outer(t, inv_freq)
            emb = np.concatenate([freqs, freqs], -1)
            return (jnp.asarray(np.cos(emb), dtype), jnp.asarray(np.sin(emb), dtype))

        def _rotate_half(x):
            x1, x2 = jnp.split(x, 2, axis=-1)
            return jnp.concatenate([-x2, x1], axis=-1)

        def _apply_rope(x, cos, sin):
            c = cos[None, :, None, :]
            s = sin[None, :, None, :]
            return x * c + _rotate_half(x) * s
        B, S, _ = hidden_states.shape
        cos, sin = _rope_tables(S, D_ROPE, hidden_states.dtype)
        q_latent = _layernorm(hidden_states @ q_a_w.T, q_a_ln_w, q_a_ln_b)
        q_nope = (q_latent @ q_b_w.T).reshape(B, S, N_HEADS, D_NOPE)
        q_rope = (q_latent @ q_rope_w.T).reshape(B, S, N_HEADS, D_ROPE)
        kv_mixed = hidden_states @ kv_a_w.T
        kv_latent, k_rope = (kv_mixed[..., :KV_LORA], kv_mixed[..., KV_LORA:])
        kv_latent = _layernorm(kv_latent, kv_a_ln_w, kv_a_ln_b)
        kv_dec = (kv_latent @ kv_b_w.T).reshape(B, S, N_HEADS, D_NOPE + D_V)
        k_nope, v = (kv_dec[..., :D_NOPE], kv_dec[..., D_NOPE:])
        k_rope = k_rope[:, :, None, :]
        q_rope = _apply_rope(q_rope, cos, sin)
        k_rope = _apply_rope(k_rope, cos, sin)
        q = jnp.concatenate([q_nope, q_rope], axis=-1)
        k = jnp.concatenate([k_nope, jnp.broadcast_to(k_rope, (B, S, N_HEADS, D_ROPE))], axis=-1)
        scale = 1.0 / math.sqrt(D_NOPE + D_ROPE)
        scores = jnp.einsum('bqhd,bkhd->bhqk', q, k) * scale
        probs = jax.nn.softmax(scores, axis=-1)
        attn = jnp.einsum('bhqk,bkhd->bqhd', probs, v)
        attn = attn.reshape(B, S, N_HEADS * D_V)
        return attn @ o_w.T

    def _L0_attn_b_ref(hidden_states, W_in, conv_w, W_x, W_dt, b_dt, D, W_out):
        import jax, jax.numpy as jnp
        import numpy as np
        HIDDEN = 256
        INTER = 512
        KCONV = 512
        DT_RANK = 128
        SSM_N = 16
        B_SZ, SEQ = (2, 512)
        xz = jnp.einsum('bsh,ih->bsi', hidden_states, W_in)
        x, z = jnp.split(xz, 2, axis=-1)
        x = jnp.einsum('bsk,ik->bsi', x, conv_w)
        x_proj = jnp.einsum('bsi,pi->bsp', x, W_x)
        delta_raw = x_proj[..., :DT_RANK]
        B = x_proj[..., DT_RANK:DT_RANK + SSM_N]
        C = x_proj[..., DT_RANK + SSM_N:]
        delta = jax.nn.softplus(jnp.einsum('bsr,ir->bsi', delta_raw, W_dt))
        y = x * D
        z = jax.nn.silu(z)
        return jnp.einsum('bsi,hi->bsh', y * z, W_out)

    def _L0_ffn_ref(hidden_states, gate_cp, up_cp, down_cp):
        import jax, jax.numpy as jnp
        import numpy as np
        HIDDEN = 256
        INTER = 1024
        COMPRESSION = 128.9

        def _n_ctrl(out_size, in_size):
            return max(16, int(out_size * in_size / COMPRESSION))

        def _catmull_rom_grid(n_ctrl, n_samples):
            t = np.linspace(0.0, n_ctrl - 1.0, n_samples, dtype=np.float64)
            i = np.clip(np.floor(t).astype(np.int64), 0, n_ctrl - 2)
            f = (t - i).astype(np.float32)
            idx = np.stack([np.clip(i + k, 0, n_ctrl - 1) for k in (-1, 0, 1, 2)], axis=0)
            return (jnp.asarray(idx.astype(np.int32)), jnp.asarray(f))

        def spline_reconstruct(control_points, out_size, in_size):
            n = out_size * in_size
            idx, f = _catmull_rom_grid(control_points.shape[0], n)
            p0, p1, p2, p3 = (control_points[idx[0]], control_points[idx[1]], control_points[idx[2]], control_points[idx[3]])
            f2 = f * f
            f3 = f2 * f
            w = 0.5 * (2.0 * p1 + (p2 - p0) * f + (2.0 * p0 - 5.0 * p1 + 4.0 * p2 - p3) * f2 + (3.0 * p1 - p0 - 3.0 * p2 + p3) * f3)
            return w.reshape(out_size, in_size)
        gate_w = spline_reconstruct(gate_cp, INTER, HIDDEN)
        up_w = spline_reconstruct(up_cp, INTER, HIDDEN)
        down_w = spline_reconstruct(down_cp, HIDDEN, INTER)
        gate = jnp.einsum('bsh,ih->bsi', hidden_states, gate_w)
        up = jnp.einsum('bsh,ih->bsi', hidden_states, up_w)
        inter = jax.nn.silu(gate) * up
        return jnp.einsum('bsi,hi->bsh', inter, down_w)
    x = L0_attn_a_hidden_states
    x = x + _L0_attn_a_ref(_layernorm(x, axis=-1), L0_attn_a_q_a_w, L0_attn_a_q_a_ln_w, L0_attn_a_q_a_ln_b, L0_attn_a_q_b_w, L0_attn_a_q_rope_w, L0_attn_a_kv_a_w, L0_attn_a_kv_a_ln_w, L0_attn_a_kv_a_ln_b, L0_attn_a_kv_b_w, L0_attn_a_o_w)
    x = x + _L0_ffn_ref(_layernorm(x, axis=-1), L0_ffn_gate_cp, L0_ffn_up_cp, L0_ffn_down_cp)
    x = x + _L0_attn_b_ref(_layernorm(x, axis=-1), L0_attn_b_W_in, L0_attn_b_conv_w, L0_attn_b_W_x, L0_attn_b_W_dt, L0_attn_b_b_dt, L0_attn_b_D, L0_attn_b_W_out)
    x = x + _L0_ffn_ref(_layernorm(x, axis=-1), L0_ffn_gate_cp, L0_ffn_up_cp, L0_ffn_down_cp)
    return x

_drawn_inputs = setup_inputs


def setup_inputs(seed=0):
    import zlib

    import numpy as np

    out = dict(_drawn_inputs(seed))
    spreads = {'L0_attn_a_q_a_ln_w': (1.0, 0.2),
     'L0_attn_a_q_a_ln_b': (0.0, 0.574),
     'L0_attn_a_kv_a_ln_w': (1.0, 0.2),
     'L0_attn_a_kv_a_ln_b': (0.0, 0.1),
     'L0_attn_b_D': (1.0, 0.6)}
    factors = {'L0_attn_b_W_in': 4.577, 'L0_attn_b_conv_w': 4.135, 'L0_attn_b_W_out': 4.15}
    for name, (base, spread) in spreads.items():
        noise = np.random.default_rng([zlib.crc32(name.encode()), seed]).standard_normal(out[name].shape)
        drawn = base * np.exp(spread * noise) if base else spread * noise
        out[name] = jnp.asarray(drawn.astype(out[name].dtype))
    for name, factor in factors.items():
        out[name] = (out[name] * factor).astype(out[name].dtype)
    return out
```

```python
from contextlib import ExitStack

import numpy as np
import concourse.bass as bass
from concourse import mybir

F32 = mybir.dt.float32
F32R = mybir.dt.float32r
ALU = mybir.AluOpType
ACT = mybir.ActivationFunctionType
AX = mybir.AxisListType

P = 128
NB, SEQ, HID = 8, 256, 256
NH, NOPE, ROPE, DV = 16, 128, 64, 128
QL, KVL = 192, 64
QK2 = QL - P
FFN, CONV = 1024, 512
CTRL = 2033
TAPS = 6
EPS = 1e-5
SCALE = 1.0 / float(np.sqrt(NOPE + ROPE))
KT = HID // P
TT = SEQ // P
NTILE = NB * TT
PAIRS = NH // 2
ROWS = FFN * HID // HID
RT = ROWS // P
CHUNK = 512
NCH = NB * SEQ // CHUNK
CT = CHUNK // P
G4 = 4


class Step:

    def __init__(self, b, least):
        self.b, self.least = b, least

    def need(self, eng, sem, per, const):
        if per * self.least + const > 0:
            eng.wait_ge(sem, self.b * per + const)

    def has(self, per, const):
        return per * self.least + const >= 0


def f32r_matmul3(pe, out, hi, lo, whi, wlo, first, last):
    pe.matmul(out, lhsT=hi, rhs=whi, start=first, stop=False, skip_group_check=True)
    pe.matmul(out, lhsT=hi, rhs=wlo, start=False, stop=False, skip_group_check=True)
    return pe.matmul(out, lhsT=lo, rhs=whi, start=False, stop=last, skip_group_check=True)


def build(nc, x, wa, lnw, lnb, wqb, wk, wv, wqr1, wqr2, wo, cos, sin, ident_in, basis, ctrl,
          w_inx, w_inz, w_conv, w_out, d_in, out):
    top = ExitStack()
    with top:
        def sem(name):
            return top.enter_context(nc.semaphore(name))

        def sb_in(stack, name, shape, dt=F32):
            return stack.enter_context(nc.sbuf_tensor(name, shape, dt))

        def sb(name, shape, dt=F32):
            return sb_in(top, name, shape, dt)

        ps = top.enter_context(nc.psum_tensor("ps", [P, 8, 512], F32))

        X = sb("X", [P, NTILE * HID])
        ident = sb("ident", [P, P])
        half = sb("half", [P, 8])
        Wn = sb("Wn", [P, 3, RT, HID])

        attn = ExitStack()
        Wq1 = [sb_in(attn, f"Wq1_{p}", [P, NH, P], F32R) for p in ("hi", "lo")]
        Wq2s = sb_in(attn, "Wq2s", [P, NH, P], F32R)
        Wq2l = sb_in(attn, "Wq2l", [QK2, NH, P], F32R)
        Bo = [sb_in(attn, f"Bo_{p}", [P, PAIRS, HID], F32R) for p in ("hi", "lo")]
        Wa = [sb_in(attn, f"Wa_{p}", [P, KT, QL + P], F32R) for p in ("hi", "lo")]
        lnws = sb_in(attn, "lnws", [P, QL + KVL])
        lnbs = sb_in(attn, "lnbs", [P, QL + KVL])
        cosT = sb_in(attn, "cosT", [P, TT, ROPE])
        sinT = sb_in(attn, "sinT", [P, TT, ROPE])
        cpad = [sb_in(attn, f"cpad_{p}", [P, TT, 3 * KVL], F32R) for p in ("hi", "lo")]

        prep = ExitStack()
        wqb_s = sb_in(prep, "wqb_s", [P, NH, QL])
        wk_s = sb_in(prep, "wk_s", [P, NH, KVL])
        wv_s = sb_in(prep, "wv_s", [P, NH, KVL])
        wqr1_s = sb_in(prep, "wqr1_s", [P, NH, ROPE])
        wqr2_s = sb_in(prep, "wqr2_s", [QK2, NH, ROPE])
        wo_s = sb_in(prep, "wo_s", [P, NH, HID])
        wa_s = sb_in(prep, "wa_s", [P, KT, QL + P])
        Ws1 = sb_in(prep, "Ws1", [P, NH, P])
        Ws2 = sb_in(prep, "Ws2", [QK2, NH, P])
        prep.close()

        QT = [sb_in(attn, f"QT_{p}", [P, NH, SEQ], F32R) for p in ("hi", "lo")]
        kT = [sb_in(attn, f"kT_{p}", [P, NB * SEQ], F32R) for p in ("hi", "lo")]
        zc = sb_in(attn, "zc", [P, NTILE * KVL])
        zkn = sb_in(attn, "zkn", [P, TT, P])
        zq = sb_in(attn, "zq", [P, TT, QL])
        xn = sb_in(attn, "xn", [P, TT, HID])
        xaT = [sb_in(attn, f"xaT_{p}", [P, KT, SEQ], F32R) for p in ("hi", "lo")]
        ql1 = [sb_in(attn, f"ql1_{p}", [P, SEQ], F32R) for p in ("hi", "lo")]
        ql2 = sb_in(attn, "ql2", [P, SEQ], F32R)
        E = sb_in(attn, "E", [P, 2, 4, SEQ])
        PT = [sb_in(attn, f"PT_{p}", [P, 2, 4, SEQ], F32R) for p in ("hi", "lo")]
        Qt = sb_in(attn, "Qt", [P, 2, G4, P])
        rtmp = sb_in(attn, "rtmp", [P, G4, ROPE])
        Us = [sb_in(attn, f"Us_{p}", [P, 2, SEQ], F32R) for p in ("hi", "lo")]
        basis_s = sb_in(attn, "basis_s", [P, TAPS, HID])
        ctrl_s = sb_in(attn, "ctrl_s", [P, 3, TAPS])
        rows_s = sb_in(attn, "rows_s", [P, 3, HID])
        sptmp = sb_in(attn, "sptmp", [P, 2, HID])
        negmax = sb_in(attn, "negmax", [P, 2, 4])
        rowsum = sb_in(attn, "rowsum", [P, 2, 4])
        rinv = sb_in(attn, "rinv", [P, 2, 4])
        st6 = sb_in(attn, "st6", [P, 2, 6])
        mv = sb_in(attn, "mv", [P, 2, 2])
        vare = sb_in(attn, "vare", [P, 2])
        rstd = sb_in(attn, "rstd", [P, 2])
        zst6 = sb_in(attn, "zst6", [P, 2, 6])
        zmv = sb_in(attn, "zmv", [P, 2, 2])
        zvare = sb_in(attn, "zvare", [P, 2])
        zrstd = sb_in(attn, "zrstd", [P, 2])
        attn.close()

        Wg = [sb(f"Wg_{p}", [P, KT, FFN], F32R) for p in ("hi", "lo")]
        Wu = [sb(f"Wu_{p}", [P, KT, FFN], F32R) for p in ("hi", "lo")]
        Wd = [sb(f"Wd_{p}", [P, FFN // P, HID], F32R) for p in ("hi", "lo")]
        Cz = [sb(f"Cz_{p}", [P, KT, CONV], F32R) for p in ("hi", "lo")]
        Cx = [sb(f"Cx_{p}", [P, KT, CONV], F32R) for p in ("hi", "lo")]
        Co = [sb(f"Co_{p}", [P, CONV // P, HID], F32R) for p in ("hi", "lo")]
        xT = [sb(f"xT_{p}", [P, KT, NB * SEQ], F32R) for p in ("hi", "lo")]
        H = [sb(f"H_{p}", [P, 4, CHUNK], F32R) for p in ("hi", "lo")]
        htmp = sb("htmp", [P, 2, CHUNK])
        silu = sb("silu", [P, 2, CHUNK])
        xnm = sb("xnm", [P, CT, HID])
        mst6 = sb("mst6", [P, CT, 6])
        mmv = sb("mmv", [P, CT, 2])
        mvare = sb("mvare", [P, CT])
        mrstd = sb("mrstd", [P, CT])
        wconv_s = sb("wconv_s", [P, 4, CONV])
        winx_s = sb("winx_s", [P, 4, HID])
        winz_s = sb("winz_s", [P, KT, CONV])
        wout_s = sb("wout_s", [P, CONV // P, HID])
        d_s = sb("d_s", [P, CONV // P])

        x_loaded = sem("x_loaded")
        conv_loaded = sem("conv_loaded")
        prep_weights(nc, sem, ps, locals())
        attention(nc, sem, ps, locals())
        spline_turn(nc, sem, ps, Wn, ident, Wg, Wu, Wd)
        names = dict(ps=ps, X=X, ident=ident, half=half, xT=xT, H=H, htmp=htmp, silu=silu, xnm=xnm,
                     mst6=mst6, mmv=mmv, mvare=mvare, mrstd=mrstd, out=out)
        loads = [(wconv_s, w_conv), (winx_s, w_inx), (winz_s, w_inz), (wout_s, w_out), (d_s, d_in)]
        gated_block(nc, sem, "f1", names, Wg, Wu, Wd, FFN // P, None, loads, conv_loaded, False)
        conv_weights(nc, sem, ps, conv_loaded, wconv_s, winx_s, winz_s, wout_s, Cz, Cx, Co)
        gated_block(nc, sem, "cb", names, Cz, Cx, Co, CONV // P, d_s, [], None, False)
        gated_block(nc, sem, "f2", names, Wg, Wu, Wd, FFN // P, None, [], None, True)


def prep_weights(nc, sem, ps, v):
    X, ident, half = v["X"], v["ident"], v["half"]
    Wq1, Wq2s, Wq2l, Bo, Wa, cpad = v["Wq1"], v["Wq2s"], v["Wq2l"], v["Bo"], v["Wa"], v["cpad"]
    wqb_s, wk_s, wv_s, wo_s, wa_s = v["wqb_s"], v["wk_s"], v["wv_s"], v["wo_s"], v["wa_s"]
    wqr1_s, wqr2_s, Ws1, Ws2 = v["wqr1_s"], v["wqr2_s"], v["Ws1"], v["Ws2"]
    q_loaded, o_loaded, small_loaded = sem("q_loaded"), sem("o_loaded"), sem("small_loaded")
    join_q, join_o = sem("join_q"), sem("join_o")
    scaled = sem("scaled")
    hi_set, lo_set = sem("hi_set"), sem("lo_set")
    zeroed = sem("zeroed")
    HG = 8

    with nc.Block() as block:
        @block.sync
        def _(sp):
            for dst, src in ((wqb_s, v["wqb"]), (wk_s, v["wk"]), (wqr1_s, v["wqr1"]), (wqr2_s, v["wqr2"])):
                sp.dma_start(dst[:], src).then_inc(q_loaded, 16)
            sp.dma_start(X[:, :].rearrange("p (t d) -> p t d", d=HID), v["x"].rearrange("t p d -> p t d")) \
                .then_inc(v["x_loaded"], 16)

        @block.scalar
        def _(act):
            for dst, src in ((wv_s, v["wv"]), (wo_s, v["wo"])):
                act.dma_start(dst[:], src).then_inc(o_loaded, 16)
            for dst, src in ((wa_s, v["wa"]), (v["lnws"], v["lnw"]), (v["lnbs"], v["lnb"]), (v["cosT"], v["cos"]),
                             (v["sinT"], v["sin"]), (ident, v["ident_in"])):
                act.dma_start(dst[:], src).then_inc(small_loaded, 16)
            act.wait_ge(q_loaded, 64)
            act.activation(Ws1[:, :, KVL:P], wqr1_s[:], ACT.Copy, scale=SCALE)
            act.activation(Ws2[:, :, KVL:P], wqr2_s[:], ACT.Copy, scale=SCALE)
            for g in range(NH // HG):
                heads = slice(g * HG, (g + 1) * HG)
                act.wait_ge(join_q, g + 1)
                act.activation(Ws1[:, heads, 0:KVL], ps[:, 2 * g, :].rearrange("p (h c) -> p h c", c=KVL),
                               ACT.Copy, scale=SCALE)
                act.activation(Ws2[:, heads, 0:KVL], ps[0:QK2, 2 * g + 1, :].rearrange("p (h c) -> p h c", c=KVL),
                               ACT.Copy, scale=SCALE).then_inc(scaled, 1)

        @block.tensor
        def _(pe):
            pe.wait_ge(q_loaded, 64)
            for g in range(NH // HG):
                for i in range(HG):
                    h = g * HG + i
                    cols = slice(i * KVL, (i + 1) * KVL)
                    pe.matmul(ps[:, 2 * g, cols], lhsT=wqb_s[:, h, 0:P], rhs=wk_s[:, h, :], start=True, stop=True)
                    last = pe.matmul(ps[0:QK2, 2 * g + 1, cols], lhsT=wqb_s[:, h, P:QL], rhs=wk_s[:, h, :],
                                     start=True, stop=True)
                last.then_inc(join_q, 1)
            pe.wait_ge(o_loaded, 32)
            for s in range(PAIRS):
                if s >= 4:
                    pe.wait_ge(lo_set, 3 + s - 3)
                for j in range(2):
                    last = pe.matmul(ps[0:KVL, 4 + s % 4, j * HID:(j + 1) * HID], lhsT=wv_s[:, 2 * s + j, :],
                                     rhs=wo_s[:, 2 * s + j, :], start=True, stop=True)
                last.then_inc(join_o, 1)

        @block.vector
        def _(dve):
            dve.wait_ge(small_loaded, 6 * 16)
            dve.tensor_copy(Wa[0][:], wa_s[:]).then_inc(hi_set, 1)
            dve.wait_ge(hi_set, 1)
            dve.tensor_tensor(Wa[1][:], wa_s[:], Wa[0][:].bitcast(F32), ALU.subtract).then_inc(lo_set, 1)
            for g in range(NH // HG):
                heads = slice(g * HG, (g + 1) * HG)
                dve.wait_ge(scaled, g + 1)
                dve.tensor_copy(Wq1[0][:, heads, :], Ws1[:, heads, :])
                dve.tensor_copy(Wq2s[0:QK2, heads, :], Ws2[:, heads, :])
                dve.tensor_copy(Wq2s[QK2:P, heads, :], Ws2[:, heads, :]).then_inc(hi_set, 1)
                dve.wait_ge(hi_set, 2 + g)
                dve.tensor_tensor(Wq1[1][:, heads, :], Ws1[:, heads, :], Wq1[0][:, heads, :].bitcast(F32), ALU.subtract)
                dve.tensor_tensor(Wq2l[:, heads, :], Ws2[:, heads, :], Wq2s[0:QK2, heads, :].bitcast(F32),
                                  ALU.subtract).then_inc(lo_set, 1)
            for s in range(PAIRS):
                dve.wait_ge(join_o, s + 1)
                for j in range(2):
                    last = dve.tensor_copy(Bo[0][j * KVL:(j + 1) * KVL, s, :], ps[0:KVL, 4 + s % 4, j * HID:(j + 1) * HID])
                last.then_inc(hi_set, 1)
                dve.wait_ge(hi_set, 4 + s)
                for j in range(2):
                    rows = slice(j * KVL, (j + 1) * KVL)
                    last = dve.tensor_tensor(Bo[1][rows, s, :], ps[0:KVL, 4 + s % 4, j * HID:(j + 1) * HID],
                                             Bo[0][rows, s, :].bitcast(F32), ALU.subtract)
                last.then_inc(lo_set, 1)

        @block.gpsimd
        def _(pool):
            pool.memset(half[:], -0.5)
            pool.memset(cpad[0][:].bitcast(F32), 0.0)
            pool.memset(cpad[1][:].bitcast(F32), 0.0).then_inc(zeroed, 1)
            pool.wait_ge(zeroed, 1)
            pool.wait_ge(v["x_loaded"], 16)


def attention(nc, sem, ps, v):
    X, ident, half = v["X"], v["ident"], v["half"]
    Wq1, Wq2s, Wq2l, Bo, Wa, cpad = v["Wq1"], v["Wq2s"], v["Wq2l"], v["Bo"], v["Wa"], v["cpad"]
    QT, kT, zc, zq, xn, xaT, ql1, ql2 = (v[k] for k in ("QT", "kT", "zc", "zq", "xn", "xaT", "ql1", "ql2"))
    E, PT, Qt, rtmp, Us = v["E"], v["PT"], v["Qt"], v["rtmp"], v["Us"]
    lnws, lnbs, cosT, sinT = v["lnws"], v["lnbs"], v["cosT"], v["sinT"]
    basis_s, ctrl_s, rows_s, sptmp, Wn = (v[k] for k in ("basis_s", "ctrl_s", "rows_s", "sptmp", "Wn"))
    negmax, rowsum, rinv = v["negmax"], v["rowsum"], v["rinv"]
    zkn = v["zkn"]
    ztmp, krtmp, krtmp2 = xn[:, 0, :], xn[:, 1, 0:ROPE], xn[:, 1, ROPE:2 * ROPE]

    S = ps[:, 0:2, :]
    ET, U, O, Q, QTp, F = (ps[:, 2 + i, :] for i in range(6))

    scores_full, et_full, u_full, o_added = sem("scores_full"), sem("et_full"), sem("u_full"), sem("o_added")
    q_full, qt_full, f_full = sem("q_full"), sem("qt_full"), sem("f_full")
    max_done, exp_done, rinv_done, norm_done = sem("max_done"), sem("exp_done"), sem("rinv_done"), sem("norm_done")
    pt_hi, pt_lo, u_hi, u_lo = sem("pt_hi"), sem("pt_lo"), sem("u_hi"), sem("u_lo")
    qnope_done, rope_mul, qtok_done = sem("qnope_done"), sem("rope_mul"), sem("qtok_done")
    qT_hi, qT_lo = sem("qT_hi"), sem("qT_lo")
    f_hi, f_lo = sem("f_hi"), sem("f_lo")
    fe_chain = sem("fe_chain")
    xvar_done, xrstd_done, xn_done = sem("xvar_done"), sem("xrstd_done"), sem("xn_done")
    zvar_done, zrstd_done, z_done = sem("zvar_done"), sem("zrstd_done"), sem("z_done")
    c_hi, c_lo, x_added = sem("c_hi"), sem("c_lo"), sem("x_added")
    basis_loaded, rows_kept = sem("basis_loaded"), sem("rows_kept")
    sp_chain, spd_chain = sem("sp_chain"), sem("spd_chain")

    SP_LINKS = 2 * (2 * TAPS - 1)
    FE_X, FE_Z = 2, 4
    FE_LINKS = FE_X + TT * FE_Z

    def run(body):
        def whole(eng):
            body(0, 0)
            with eng.Fori(1, NB - 2) as b:
                body(b, 1)
            body(NB - 2, NB - 2)
            body(NB - 1, NB - 1)
            body(NB, NB)
        return whole

    with nc.Block() as block:
        @block.tensor
        def _(pe):
            def turn_x(t, j, dj):
                pe.wait_ge(xn_done, j + dj + 1)
                t.need(pe, f_lo, 5, 5 * dj)
                for k in range(KT):
                    for i in range(TT):
                        c = (k * TT + i) * P
                        last = pe.matmul(F[:, c:c + P], lhsT=xn[:, i, k * P:(k + 1) * P], rhs=ident[:],
                                         is_transpose=True, start=True, stop=True)
                last.then_inc(f_full, 1)

            def latents(t, j, dj, i):
                if i == 0:
                    t.need(pe, f_lo, 5, 5 * dj + 1)
                else:
                    t.need(pe, f_lo, 5, 5 * dj + 2)
                rows = slice(i * P, (i + 1) * P)
                for k in range(KT):
                    last = f32r_matmul3(pe, F[:, 0:QL + P], xaT[0][:, k, rows], xaT[1][:, k, rows],
                                        Wa[0][:, k, :], Wa[1][:, k, :], k == 0, k == KT - 1)
                last.then_inc(f_full, 1)

            def turn_k(t, j, dj):
                t.need(pe, z_done, 2, 2 * dj + 2)
                t.need(pe, f_lo, 5, 5 * dj + 3)
                for i in range(TT):
                    last = pe.matmul(F[:, i * P:(i + 1) * P], lhsT=zkn[:, i, :], rhs=ident[:], is_transpose=True, start=True, stop=True)
                last.then_inc(f_full, 1)

            def turn_q(t, j, dj):
                t.need(pe, z_done, 2, 2 * dj + 2)
                t.need(pe, f_lo, 5, 5 * dj + 4)
                for i in range(TT):
                    pe.matmul(F[:, i * P:(i + 1) * P], lhsT=zq[:, i, 0:P], rhs=ident[:],
                              is_transpose=True, start=True, stop=True)
                    last = pe.matmul(F[0:QK2, SEQ + i * P:SEQ + (i + 1) * P], lhsT=zq[:, i, P:QL], rhs=ident[:],
                                     is_transpose=True, start=True, stop=True)
                last.then_inc(f_full, 1)

            def query(t, idx, dq):
                i, g = idx % 2, idx // 2
                if idx == 0:
                    t.need(pe, f_lo, 5, 5 * (dq // 8) + 5)
                t.need(pe, rope_mul, 8, dq)
                rows, heads = slice(i * P, (i + 1) * P), slice(g * G4, (g + 1) * G4)

                def w(a):
                    return a[:, heads, :].rearrange("p h f -> p (h f)")
                f32r_matmul3(pe, Q, ql1[0][:, rows], ql1[1][:, rows], w(Wq1[0]), w(Wq1[1]), True, False)
                pe.matmul(Q, lhsT=ql2[:, rows], rhs=w(Wq2s), start=False, stop=False, skip_group_check=True)
                pe.matmul(Q, lhsT=ql2[0:QK2, rows], rhs=w(Wq2l), start=False, stop=True,
                          skip_group_check=True).then_inc(q_full, 1)

            def turn_query(t, par, dq):
                t.need(pe, qtok_done, 8, dq + 1)
                t.need(pe, qT_lo, 8, dq)
                for j in range(G4):
                    last = pe.matmul(QTp[:, j * P:(j + 1) * P], lhsT=Qt[:, par, j, :], rhs=ident[:],
                                     is_transpose=True, start=True, stop=True)
                last.then_inc(qt_full, 1)

            def scores(t, s):
                t.need(pe, qT_lo, 8, 2 * (s // 2) + 2)
                if s == 0:
                    t.need(pe, f_lo, 5, 4)
                t.need(pe, exp_done, 8, s)
                for i in range(TT):
                    for j in range(2):
                        rows = slice(i * P, (i + 1) * P)
                        last = f32r_matmul3(pe, S[:, i, j * SEQ:(j + 1) * SEQ], QT[0][:, 2 * s + j, rows],
                                            QT[1][:, 2 * s + j, rows], kT[0][:, bass.ds(t.b * SEQ, SEQ)],
                                            kT[1][:, bass.ds(t.b * SEQ, SEQ)], True, True)
                last.then_inc(scores_full, 1)

            def turn_probs(t, s, i):
                t.need(pe, norm_done, 8, s)
                t.need(pe, pt_lo, 16, 2 * (s - 1) + i)
                for k in range(TT):
                    for j in range(2):
                        c = (k * 2 + j) * P
                        last = pe.matmul(ET[:, c:c + P], lhsT=E[:, (s - 1) % 2, 2 * i + j, k * P:(k + 1) * P],
                                         rhs=ident[:], is_transpose=True, start=True, stop=True)
                last.then_inc(et_full, 1)

            def values(t, s):
                par = s % 2
                t.need(pe, pt_lo, 16, 2 * (s - 2) + 2)
                t.need(pe, u_lo, 8, s - 2)
                if s == 2:
                    t.need(pe, c_lo, 1, 1)
                first = True
                for k in range(TT):
                    for j in range(2):
                        cols = slice(KVL, 3 * KVL) if j == 0 else slice(0, 2 * KVL)
                        hi, lo = cpad[0][:, k, cols], cpad[1][:, k, cols]
                        phi, plo = PT[0][:, par, 2 * k + j, :], PT[1][:, par, 2 * k + j, :]
                        last = f32r_matmul3(pe, U[:, 0:SEQ], hi, lo, phi, plo, first, k == 1 and j == 1)
                        first = False
                last.then_inc(u_full, 1)

            def output(t, s):
                pair = (s - 3) % 8
                t.need(pe, u_lo, 8, s - 2)
                if pair == 0:
                    t.need(pe, x_added, 1, 0)
                for i in range(TT):
                    rows = slice(i * P, (i + 1) * P)
                    last = f32r_matmul3(pe, O[:, i * HID:(i + 1) * HID], Us[0][:, (s - 3) % 2, rows],
                                        Us[1][:, (s - 3) % 2, rows], Bo[0][:, pair, :], Bo[1][:, pair, :],
                                        pair == 0 and i == 0, pair == PAIRS - 1)
                last.then_inc(o_added, 1)

            def body(b, least):
                t = Step(b, least)
                for s in range(8 if least < NB else 3):
                    n = 8 * least + s
                    if n < 64:
                        scores(t, s)
                    if 1 <= n <= 64:
                        turn_probs(t, s, 0)
                    if 2 <= n <= 65:
                        values(t, s)
                    if 1 <= n <= 64:
                        turn_probs(t, s, 1)
                    if n + 6 < 64:
                        query(t, (s + 6) % 8, s + 6)
                    if 3 <= n <= 66:
                        output(t, s)
                    if n + 5 < 64:
                        turn_query(t, (s + 5) % 2, s + 5)
                    if s == 1 and least + 1 < NB:
                        turn_q(t, b, 1)
                    if least + 2 < NB:
                        if s == 2:
                            turn_x(t, b, 2)
                        if s in (3, 5):
                            latents(t, b, 2, (s - 3) // 2)
                        if s == 7:
                            turn_k(t, b, 2)

            t0 = Step(0, 0)
            turn_x(t0, 0, 0)
            latents(t0, 0, 0, 0)
            latents(t0, 0, 0, 1)
            turn_k(t0, 0, 0)
            turn_q(t0, 0, 0)
            for q in range(6):
                query(t0, q, q)
                if q >= 1:
                    turn_query(t0, (q - 1) % 2, q - 1)
            turn_x(t0, 0, 1)
            latents(t0, 0, 1, 0)
            latents(t0, 0, 1, 1)
            turn_k(t0, 0, 1)
            run(body)(pe)

        @block.scalar
        def _(act):
            def split_x(t, j, dj):
                t.need(act, f_full, 5, 5 * dj + 1)
                act.activation(xaT[0][:].rearrange("p k c -> p (k c)"), F, ACT.Copy).then_inc(f_hi, 1)

            def split_k(t, j, dj):
                t.need(act, f_full, 5, 5 * dj + 4)
                act.activation(kT[0][:, bass.ds((j + dj) * SEQ, SEQ)], F[:, 0:SEQ], ACT.Copy).then_inc(f_hi, 1)

            def split_q(t, j, dj):
                t.need(act, f_full, 5, 5 * dj + 5)
                if dj:
                    t.need(act, q_full, 8, 8)
                act.activation(ql1[0][:], F[:, 0:SEQ], ACT.Copy)
                act.activation(ql2[0:QK2, :], F[0:QK2, SEQ:2 * SEQ], ACT.Copy).then_inc(f_hi, 1)

            def probs(t, s, i):
                t.need(act, et_full, 16, 2 * (s - 1) + i + 1)
                t.need(act, u_full, 8, s - 2)
                act.activation(PT[0][:, (s - 1) % 2, :, i * P:(i + 1) * P],
                               ET.rearrange("p (a q) -> p a q", q=P), ACT.Copy).then_inc(pt_hi, 1)

            def exps(t, s):
                par = s % 2
                t.need(act, max_done, 8, s + 1)
                t.need(act, et_full, 16, 2 * s - 2)
                t.need(act, rinv_done, 8, s - 1)
                for a in range(4):
                    last = act.activation(E[:, par, a, :], S[:, a // 2, (a % 2) * SEQ:(a % 2 + 1) * SEQ], ACT.Exp,
                                          bias=negmax[:, par, a:a + 1], accum_out=rowsum[:, par, a:a + 1])
                last.then_inc(exp_done, 1)

            def u_split(t, s):
                t.need(act, u_full, 8, s - 1)
                t.need(act, o_added, 8, s - 3)
                act.activation(Us[0][:, s % 2, :], U[:, 0:SEQ], ACT.Copy).then_inc(u_hi, 1)

            def q_nope(t, dq):
                t.need(act, q_full, 8, dq + 1)
                t.need(act, qt_full, 8, dq - 1)
                act.activation(Qt[:, dq % 2, :, 0:KVL], Q.rearrange("p (h f) -> p h f", f=P)[:, :, 0:KVL],
                               ACT.Copy).then_inc(qnope_done, 1)

            def q_turned(t, dq):
                idx = dq % 8
                g, i = idx // 2, idx % 2
                t.need(act, qt_full, 8, dq + 1)
                t.need(act, scores_full, 8, 8 * (dq // 8 - 1) + 2 * g + 2)
                act.activation(QT[0][:, g * G4:(g + 1) * G4, i * P:(i + 1) * P],
                               QTp.rearrange("p (h q) -> p h q", q=P), ACT.Copy).then_inc(qT_hi, 1)

            def body(b, least):
                t = Step(b, least)
                for s in range(8 if least < NB else 3):
                    n = 8 * least + s
                    if 1 <= n <= 64:
                        probs(t, s, 0)
                    if n < 64:
                        exps(t, s)
                    if 2 <= n <= 65:
                        u_split(t, s)
                    if 1 <= n <= 64:
                        probs(t, s, 1)
                    if n + 6 < 64:
                        q_nope(t, s + 6)
                    if n + 5 < 64:
                        q_turned(t, s + 5)
                    if s == 1 and least < NB:
                        t.need(act, u_full, 8, 0)
                        t.need(act, z_done, 2, 2)
                        act.activation(cpad[0][:, :, KVL:2 * KVL],
                                       zc[:, bass.ds(b * TT * KVL, TT * KVL)].rearrange("p (i f) -> p i f", f=KVL),
                                       ACT.Copy).then_inc(c_hi, 1)
                    if s == 1 and least + 1 < NB:
                        split_q(t, b, 1)
                    if least + 2 < NB:
                        if s == 2:
                            split_x(t, b, 2)
                        if s == 7:
                            split_k(t, b, 2)

            t0 = Step(0, 0)
            split_x(t0, 0, 0)
            split_k(t0, 0, 0)
            split_q(t0, 0, 0)
            for q in range(6):
                q_nope(t0, q)
                if q >= 1:
                    q_turned(t0, q - 1)
            split_x(t0, 0, 1)
            split_k(t0, 0, 1)
            run(body)(act)

        @block.vector
        def _(dve):
            def x_stats(t, j, dj):
                for i in range(TT):
                    last = dve.bn_stats(v["st6"][:, i, :], X[:, bass.ds((j + dj) * TT * HID + i * HID, HID)])
                last.then_inc(fe_chain, 1)

            def x_aggregate(t, j, dj, between):
                t.need(dve, fe_chain, FE_LINKS, FE_LINKS * dj + 1)
                if between is not None:
                    between()
                for i in range(TT):
                    last = dve.bn_aggr(v["mv"][:, i, :], v["st6"][:, i, :])
                last.then_inc(fe_chain, 1)
                t.need(dve, fe_chain, FE_LINKS, FE_LINKS * dj + 2)
                t.need(dve, xrstd_done, 1, dj)
                dve.tensor_scalar(v["vare"][:], v["mv"][:, :, 1], EPS, None, ALU.add).then_inc(xvar_done, 1)

            def x_norm(t, j, dj):
                t.need(dve, xrstd_done, 1, dj + 1)
                t.need(dve, f_full, 5, 5 * dj - 4)
                for i in range(TT):
                    last = dve.tensor_scalar(xn[:, i, :], X[:, bass.ds((j + dj) * TT * HID + i * HID, HID)],
                                             v["mv"][:, i, 0:1], v["rstd"][:, i:i + 1], ALU.subtract, ALU.mult)
                last.then_inc(xn_done, 1)

            def split_x(t, j, dj):
                t.need(dve, f_hi, 3, 3 * dj + 1)
                dve.tensor_tensor(xaT[1][:].rearrange("p k c -> p (k c)"), F,
                                  xaT[0][:].rearrange("p k c -> p (k c)").bitcast(F32), ALU.subtract).then_inc(f_lo, 1)

            def z_stats(t, j, dj, i):
                c0 = FE_LINKS * dj + FE_X + FE_Z * i
                t.need(dve, f_full, 5, 5 * dj + 2 + i)
                dve.bn_stats(v["zst6"][:, 0, :], F[:, 0:QL])
                dve.bn_stats(v["zst6"][:, 1, :], F[:, QL:QL + KVL]).then_inc(fe_chain, 1)
                t.need(dve, fe_chain, FE_LINKS, c0 + 1)
                dve.tensor_tensor(krtmp, F[:, QL + KVL:QL + P], cosT[:, i, :], ALU.mult)
                for a in range(2):
                    last = dve.bn_aggr(v["zmv"][:, a, :], v["zst6"][:, a, :])
                last.then_inc(fe_chain, 1)
                t.need(dve, fe_chain, FE_LINKS, c0 + 2)
                dve.tensor_scalar(v["zvare"][:], v["zmv"][:, :, 1], EPS, None, ALU.add).then_inc(zvar_done, 1)

            def z_norm(t, j, dj, i):
                c0 = FE_LINKS * dj + FE_X + FE_Z * i + 2
                t.need(dve, zrstd_done, 2, 2 * dj + i + 1)
                dve.tensor_scalar(ztmp[:, 0:QL], F[:, 0:QL], v["zmv"][:, 0, 0:1], v["zrstd"][:, 0:1],
                                  ALU.subtract, ALU.mult)
                dve.tensor_scalar(ztmp[:, QL:], F[:, QL:QL + KVL], v["zmv"][:, 1, 0:1], v["zrstd"][:, 1:2],
                                  ALU.subtract, ALU.mult)
                kr = F[:, QL + KVL:QL + P]
                dve.tensor_tensor(krtmp2.rearrange("p (z e) -> p z e", z=2),
                                  kr.rearrange("p (z e) -> p z e", z=2)[:, ::-1, :],
                                  sinT[:, i, :].rearrange("p (z e) -> p z e", z=2), ALU.mult).then_inc(f_lo, 1)
                t.need(dve, f_lo, 5, 5 * dj + 2 + i)
                dve.tensor_tensor(ztmp, ztmp, lnws[:], ALU.mult).then_inc(fe_chain, 1)
                t.need(dve, fe_chain, FE_LINKS, c0 + 1)
                zs = bass.ds((j + dj) * TT * KVL + i * KVL, KVL)
                if i == 0:
                    t.need(dve, f_full, 5, 5 * dj)
                dve.tensor_tensor(zq[:, i, :], ztmp[:, 0:QL], lnbs[:, 0:QL], ALU.add)
                dve.tensor_tensor(zkn[:, i, 0:KVL], ztmp[:, QL:], lnbs[:, QL:], ALU.add)
                dve.tensor_tensor(zkn[:, i, KVL:P], krtmp, krtmp2, ALU.add).then_inc(fe_chain, 1)
                t.need(dve, fe_chain, FE_LINKS, c0 + 2)
                dve.tensor_copy(zc[:, zs], zkn[:, i, 0:KVL]).then_inc(z_done, 1)

            def split_k(t, j, dj):
                t.need(dve, f_hi, 3, 3 * dj + 2)
                cols = bass.ds((j + dj) * SEQ, SEQ)
                dve.tensor_tensor(kT[1][:, cols], F[:, 0:SEQ], kT[0][:, cols].bitcast(F32), ALU.subtract) \
                    .then_inc(f_lo, 1)

            def split_q(t, j, dj):
                t.need(dve, f_hi, 3, 3 * dj + 3)
                dve.tensor_tensor(ql1[1][:], F[:, 0:SEQ], ql1[0][:].bitcast(F32), ALU.subtract)
                dve.tensor_tensor(ql2[QK2:P, :], F[0:QK2, SEQ:2 * SEQ], ql2[0:QK2, :].bitcast(F32),
                                  ALU.subtract).then_inc(f_lo, 1)

            def maxima(t, s):
                t.need(dve, scores_full, 8, s + 1)
                t.need(dve, exp_done, 8, s - 1)
                dve.tensor_reduce(negmax[:, s % 2, :], S.rearrange("p i (j k) -> p (i j) k", k=SEQ), AX.X, ALU.max,
                                  negate=True).then_inc(max_done, 1)

            def inverse(t, s):
                t.need(dve, exp_done, 8, s + 1)
                t.need(dve, norm_done, 8, s - 1)
                dve.reciprocal(rinv[:, s % 2, :], rowsum[:, s % 2, :]).then_inc(rinv_done, 1)

            def probs(t, s, i):
                t.need(dve, pt_hi, 16, 2 * (s - 1) + i + 1)
                cols = slice(i * P, (i + 1) * P)
                dve.tensor_tensor(PT[1][:, (s - 1) % 2, :, cols], ET.rearrange("p (a q) -> p a q", q=P),
                                  PT[0][:, (s - 1) % 2, :, cols].bitcast(F32), ALU.subtract).then_inc(pt_lo, 1)

            def u_split(t, s):
                t.need(dve, u_hi, 8, s - 1)
                dve.tensor_tensor(Us[1][:, s % 2, :], U[:, 0:SEQ], Us[0][:, s % 2, :].bitcast(F32),
                                  ALU.subtract).then_inc(u_lo, 1)

            def rope(t, dq):
                i = (dq % 8) % 2
                t.need(dve, qnope_done, 8, dq + 1)
                t.need(dve, qtok_done, 8, dq)
                r = Q.rearrange("p (h f) -> p h f", f=P)[:, :, KVL:P]
                dst = Qt[:, dq % 2, :, KVL:P]
                dve.tensor_tensor(dst, r, cosT[:, i, :].unsqueeze(1).broadcast_to([P, G4, ROPE]), ALU.mult)
                dve.tensor_tensor(rtmp[:].rearrange("p h (z e) -> p h z e", z=2),
                                  r.rearrange("p h (z e) -> p h z e", z=2)[:, :, ::-1, :],
                                  sinT[:, i, :].rearrange("p (z e) -> p z e", z=2).unsqueeze(1)
                                  .broadcast_to([P, G4, 2, ROPE // 2]), ALU.mult).then_inc(rope_mul, 1)
                t.need(dve, rope_mul, 8, dq + 1)
                dve.tensor_tensor(dst, dst, rtmp[:], ALU.add).then_inc(qtok_done, 1)

            def q_turned(t, dq):
                idx = dq % 8
                g, i = idx // 2, idx % 2
                t.need(dve, qT_hi, 8, dq + 1)
                heads, cols = slice(g * G4, (g + 1) * G4), slice(i * P, (i + 1) * P)
                dve.tensor_tensor(QT[1][:, heads, cols], QTp.rearrange("p (h q) -> p h q", q=P),
                                  QT[0][:, heads, cols].bitcast(F32), ALU.subtract).then_inc(qT_lo, 1)

            def spline_tap(t, m):
                row, w = rows_s[:, 2, :], ctrl_s[:, 2, m:m + 1]
                if m == 0:
                    t.need(dve, basis_loaded, 32, 32)
                    t.need(dve, rows_kept, 16, 0)
                    last = dve.tensor_scalar(row, basis_s[:, 0, :], w, None, ALU.mult)
                else:
                    t.need(dve, spd_chain, TAPS, m)
                    last = dve.scalar_tensor_tensor(row, basis_s[:, m, :], w, row, ALU.mult, ALU.add)
                last.then_inc(spd_chain, 1)

            def body(b, least):
                t = Step(b, least)
                for s in range(8 if least < NB else 3):
                    n = 8 * least + s
                    if n < 64:
                        maxima(t, s)
                    if 1 <= n <= 64:
                        probs(t, s, 0)
                    if n < 64:
                        inverse(t, s)
                    if 2 <= n <= 65:
                        u_split(t, s)
                    if 1 <= n <= 64:
                        probs(t, s, 1)
                    if n + 6 < 64:
                        rope(t, s + 6)
                    if n + 5 < 64:
                        q_turned(t, s + 5)
                    if s == 1 and least < NB:
                        t.need(dve, c_hi, 1, 1)
                        dve.tensor_tensor(cpad[1][:, :, KVL:2 * KVL],
                                          zc[:, bass.ds(b * TT * KVL, TT * KVL)].rearrange("p (i f) -> p i f", f=KVL),
                                          cpad[0][:, :, KVL:2 * KVL].bitcast(F32), ALU.subtract).then_inc(c_lo, 1)
                    if s == 1 and least + 1 < NB:
                        split_q(t, b, 1)
                    if s == 2 and least >= 1:
                        t.need(dve, o_added, 8, 0)
                        rows = X[:, bass.ds(b * TT * HID - TT * HID, TT * HID)]
                        dve.tensor_tensor(rows, O, rows, ALU.add).then_inc(x_added, 1)
                    if least + 2 < NB:
                        if s == 0:
                            x_stats(t, b, 2)
                        if s == 1:
                            x_norm(t, b, 2)
                        if s == 2:
                            split_x(t, b, 2)
                        if s in (3, 5):
                            z_stats(t, b, 2, (s - 3) // 2)
                        if s in (4, 6):
                            z_norm(t, b, 2, (s - 4) // 2)
                        if s == 7:
                            split_k(t, b, 2)
                    if s == 0 and least + 2 < NB:
                        x_aggregate(t, b, 2, lambda: spline_tap(t, 0))
                    elif s < TAPS and least < NB:
                        spline_tap(t, s)

            t0 = Step(0, 0)
            x_stats(t0, 0, 0)
            x_aggregate(t0, 0, 0, None)
            x_norm(t0, 0, 0)
            split_x(t0, 0, 0)
            for i in range(TT):
                z_stats(t0, 0, 0, i)
                z_norm(t0, 0, 0, i)
            split_k(t0, 0, 0)
            split_q(t0, 0, 0)
            x_stats(t0, 0, 1)
            x_aggregate(t0, 0, 1, None)
            x_norm(t0, 0, 1)
            for q in range(6):
                rope(t0, q)
                if q >= 1:
                    q_turned(t0, q - 1)
            split_x(t0, 0, 1)
            for i in range(TT):
                z_stats(t0, 0, 1, i)
                z_norm(t0, 0, 1, i)
            split_k(t0, 0, 1)
            run(body)(dve)

        @block.gpsimd
        def _(pool):
            def x_rsqrt(t, dj):
                t.need(pool, xvar_done, 1, dj + 1)
                t.need(pool, xn_done, 1, dj)
                pool.tensor_tensor(v["rstd"][:], v["vare"][:], half[:, 0:TT], ALU.pow).then_inc(xrstd_done, 1)

            def z_rsqrt(t, dj, i):
                t.need(pool, zvar_done, 2, 2 * dj + i + 1)
                pool.tensor_tensor(v["zrstd"][:], v["zvare"][:], half[:, 0:2], ALU.pow).then_inc(zrstd_done, 1)

            def normalise(t, s):
                t.need(pool, rinv_done, 8, s + 1)
                e = E[:, s % 2, :, :]
                pool.tensor_tensor(e, e, rinv[:, s % 2, :].unsqueeze(2).broadcast_to([P, 4, SEQ]), ALU.mult) \
                    .then_inc(norm_done, 1)

            def spline_ops(t, first, count):
                for link in range(first, min(first + count, SP_LINKS)):
                    w, k = link % 2, link // 2
                    m = (k + 1) // 2
                    row, cp = rows_s[:, w, :], ctrl_s[:, w, m:m + 1].broadcast_to([P, HID])
                    if link == 0:
                        t.need(pool, basis_loaded, 32, 32)
                        t.need(pool, rows_kept, 16, 0)
                    if link >= 2:
                        t.need(pool, sp_chain, SP_LINKS, link - 1)
                    else:
                        t.need(pool, sp_chain, SP_LINKS, 0)
                    if k == 0:
                        last = pool.tensor_tensor(row, basis_s[:, 0, :], cp, ALU.mult)
                    elif k % 2 == 1:
                        last = pool.tensor_tensor(sptmp[:, w, :], basis_s[:, m, :], cp, ALU.mult)
                    else:
                        last = pool.tensor_tensor(row, row, sptmp[:, w, :], ALU.add)
                    last.then_inc(sp_chain, 1)

            def body(b, least):
                if least >= NB:
                    return
                t = Step(b, least)
                for s in range(8):
                    normalise(t, s)
                    if least + 2 < NB and s == 0:
                        x_rsqrt(t, 2)
                    if least + 2 < NB and s in (3, 5):
                        z_rsqrt(t, 2, (s - 3) // 2)
                    spline_ops(t, 3 * s, 3)

            t0 = Step(0, 0)
            for dj in range(2):
                x_rsqrt(t0, dj)
                if dj == 0:
                    for i in range(TT):
                        z_rsqrt(t0, dj, i)
            for i in range(TT):
                z_rsqrt(t0, 1, i)
            run(body)(pool)

        @block.sync
        def _(sp):
            for b in range(NB):
                if b >= 1:
                    sp.wait_ge(sp_chain, b * SP_LINKS)
                    sp.wait_ge(spd_chain, b * TAPS)
                    sp.dma_start(Wn[:, :, b - 1, :], rows_s[:]).then_inc(rows_kept, 16)
                sp.dma_start(basis_s[:].rearrange("p m c -> p (m c)"), v["basis"][b]).then_inc(basis_loaded, 16)
                sp.dma_start(ctrl_s[:], v["ctrl"][b]).then_inc(basis_loaded, 16)
            sp.wait_ge(sp_chain, NB * SP_LINKS)
            sp.wait_ge(spd_chain, NB * TAPS)
            sp.dma_start(Wn[:, :, NB - 1, :], rows_s[:]).then_inc(rows_kept, 16)
            sp.wait_ge(rows_kept, 16 * NB)


def spline_turn(nc, sem, ps, Wn, ident, Wg, Wu, Wd):
    turned, hi_cut, lo_cut = sem("sw_turned"), sem("sw_hi"), sem("sw_lo")
    units = [(w, r) for r in range(RT // 2) for w in range(3)]

    def views(w, r):
        u = units.index((w, r))
        bank = ps[:, u % 4, :]
        if w < 2:
            dst = (Wg, Wu)[w]
            return [(bank.rearrange("p (k c) -> p k c", k=KT), [d[:, :, r * 2 * P:(r + 1) * 2 * P] for d in dst])]
        return [(bank[:, k * 2 * P:(k + 1) * 2 * P].rearrange("p (o a) -> p a o", a=4),
                 [d[:].rearrange("p (a k) o -> p a k o", k=KT)[:, :, k, r * 64:(r + 1) * 64] for d in Wd])
                for k in range(KT)]

    with nc.Block() as block:
        @block.tensor
        def _(pe):
            for u, (w, r) in enumerate(units):
                if u >= 4:
                    pe.wait_ge(lo_cut, u - 3)
                for k in range(KT):
                    for i in range(2):
                        c = (2 * k + i) * P
                        last = pe.matmul(ps[:, u % 4, c:c + P], lhsT=Wn[:, w, 2 * r + i, k * P:(k + 1) * P],
                                         rhs=ident[:], is_transpose=True, start=True, stop=True)
                last.then_inc(turned, 1)

        @block.scalar
        def _(act):
            for u, (w, r) in enumerate(units):
                act.wait_ge(turned, u + 1)
                for src, (hi, lo) in views(w, r):
                    last = act.activation(hi, src, ACT.Copy)
                last.then_inc(hi_cut, 1)

        @block.vector
        def _(dve):
            for u, (w, r) in enumerate(units):
                dve.wait_ge(hi_cut, u + 1)
                for src, (hi, lo) in views(w, r):
                    last = dve.tensor_tensor(lo, src, hi.bitcast(F32), ALU.subtract)
                last.then_inc(lo_cut, 1)


def conv_weights(nc, sem, ps, loaded, wconv_s, winx_s, winz_s, wout_s, Cz, Cx, Co):
    joined, hi_cut = sem("cw_joined"), sem("cw_hi")
    with nc.Block() as block:
        @block.tensor
        def _(pe):
            for m in range(KT):
                for k in range(4):
                    last = pe.matmul(ps[:, m, :], lhsT=winx_s[:, k, m * P:(m + 1) * P], rhs=wconv_s[:, k, :],
                                     start=k == 0, stop=k == 3)
                last.then_inc(joined, 1)

        @block.vector
        def _(dve):
            dve.tensor_copy(Cz[0][:], winz_s[:])
            dve.tensor_copy(Co[0][:], wout_s[:])
            dve.wait_ge(joined, KT)
            dve.tensor_copy(Cx[0][:], ps[:, 0:KT, :]).then_inc(hi_cut, 1)
            dve.wait_ge(hi_cut, 1)
            dve.tensor_tensor(Cz[1][:], winz_s[:], Cz[0][:].bitcast(F32), ALU.subtract)
            dve.tensor_tensor(Co[1][:], wout_s[:], Co[0][:].bitcast(F32), ALU.subtract)
            dve.tensor_tensor(Cx[1][:], ps[:, 0:KT, :], Cx[0][:].bitcast(F32), ALU.subtract)


def gated_block(nc, sem, tag, names, Wg, Wu, Wd, NF, d_s, loads, loaded, store):
    ps, X, ident, half, xT, H, htmp, silu, xnm = (names[k] for k in (
        "ps", "X", "ident", "half", "xT", "H", "htmp", "silu", "xnm"))
    mst6, mmv, mvare, mrstd, out = (names[k] for k in ("mst6", "mmv", "mvare", "mrstd", "out"))
    G, UP, O, XT = ps[:, 0:2, :], ps[:, 2:4, :], ps[:, 4:6, :], ps[:, 6:8, :]
    gate_full, up_full, down_done = sem(tag + "_gate_full"), sem(tag + "_up_full"), sem(tag + "_down_done")
    silu_done, h_done, h_hi, h_lo = sem(tag + "_silu"), sem(tag + "_h"), sem(tag + "_h_hi"), sem(tag + "_h_lo")
    chain, var_done, rstd_done = sem(tag + "_chain"), sem(tag + "_var"), sem(tag + "_rstd")
    xn_done, xt_full, x_hi, x_lo = sem(tag + "_xn"), sem(tag + "_xt_full"), sem(tag + "_x_hi"), sem(tag + "_x_lo")
    x_added, stored = sem(tag + "_x_added"), sem(tag + "_stored")
    TOT = NF * NCH

    def run(eng, body):
        body(0, 0)
        with eng.Fori(1, NCH - 1) as c:
            body(c, 1)
        body(NCH - 1, NCH - 1)
        body(NCH, NCH)

    with nc.Block() as block:
        @block.tensor
        def _(pe):
            def turn_x(t, dc):
                t.need(pe, xn_done, 1, dc + 1)
                t.need(pe, x_lo, KT, KT * dc)
                for k in range(KT):
                    for i in range(CT):
                        last = pe.matmul(XT[:, k, i * P:(i + 1) * P], lhsT=xnm[:, i, k * P:(k + 1) * P],
                                         rhs=ident[:], is_transpose=True, start=True, stop=True)
                    last.then_inc(xt_full, 1)

            def inner(t, j, W, bank, full):
                cols = bass.ds(t.b * CHUNK, CHUNK)
                for k in range(KT):
                    w = [a[:, k, j * P:(j + 1) * P] for a in W]
                    last = f32r_matmul3(pe, bank, w[0], w[1], xT[0][:, k, cols], xT[1][:, k, cols],
                                        k == 0, k == KT - 1)
                last.then_inc(full, 1)

            def down(t, j):
                f = (j - 2) % NF
                t.need(pe, h_lo, NF, j - 1)
                if f == 0:
                    t.need(pe, x_added, 1, 0)
                for i in range(CT):
                    rows = slice(i * P, (i + 1) * P)
                    last = f32r_matmul3(pe, O[:, i // 2, (i % 2) * HID:(i % 2 + 1) * HID], H[0][:, (j - 2) % 4, rows],
                                        H[1][:, (j - 2) % 4, rows], Wd[0][:, f, :], Wd[1][:, f, :],
                                        f == 0 and i % 2 == 0, f == NF - 1)
                last.then_inc(down_done, 1)

            def body(c, least):
                t = Step(c, least)
                for j in range(NF if least < NCH else 2):
                    m = NF * least + j
                    if m < TOT:
                        if j == 0:
                            t.need(pe, x_lo, KT, KT)
                        t.need(pe, silu_done, NF, j - 1)
                        inner(t, j, Wg, G[:, j % 2, :], gate_full)
                        t.need(pe, h_done, NF, j - 1)
                        inner(t, j, Wu, UP[:, j % 2, :], up_full)
                    if m >= 2:
                        down(t, j)
                    if j == 2 and least + 1 < NCH:
                        turn_x(t, 1)

            turn_x(Step(0, 0), 0)
            run(pe, body)

        @block.scalar
        def _(act):
            for dst, src in loads:
                act.dma_start(dst[:], src).then_inc(loaded, 16)

            def split_x(t, dc):
                for k in range(KT):
                    t.need(act, xt_full, KT, KT * dc + k + 1)
                    act.activation(xT[0][:, k, bass.ds((t.b + dc) * CHUNK, CHUNK)], XT[:, k, :], ACT.Copy) \
                        .then_inc(x_hi, 1)

            def body(c, least):
                t = Step(c, least)
                for j in range(NF if least < NCH else 0):
                    t.need(act, gate_full, NF, j + 1)
                    t.need(act, h_done, NF, j - 1)
                    act.activation(silu[:, j % 2, :], G[:, j % 2, :], ACT.Silu).then_inc(silu_done, 1)
                    t.need(act, h_done, NF, j + 1)
                    t.need(act, down_done, NF, j - 3)
                    act.activation(H[0][:, j % 4, :], htmp[:, j % 2, :], ACT.Copy).then_inc(h_hi, 1)
                    if j == 2 and least + 1 < NCH:
                        split_x(t, 1)

            split_x(Step(0, 0), 0)
            run(act, body)
            if loads:
                act.wait_ge(loaded, 16 * len(loads))

        @block.vector
        def _(dve):
            def x_stats(t, dc):
                base = t.b + dc
                for i in range(CT):
                    last = dve.bn_stats(mst6[:, i, :], X[:, bass.ds(base * CT * HID + i * HID, HID)])
                last.then_inc(chain, 1)

            def x_aggregate(t, dc, between):
                t.need(dve, chain, 2, 2 * dc + 1)
                if between is not None:
                    between()
                for i in range(CT):
                    last = dve.bn_aggr(mmv[:, i, :], mst6[:, i, :])
                last.then_inc(chain, 1)
                t.need(dve, chain, 2, 2 * dc + 2)
                t.need(dve, rstd_done, 1, dc)
                dve.tensor_scalar(mvare[:], mmv[:, :, 1], EPS, None, ALU.add).then_inc(var_done, 1)

            def x_norm(t, dc):
                t.need(dve, rstd_done, 1, dc + 1)
                t.need(dve, xt_full, KT, KT * dc)
                for i in range(CT):
                    last = dve.tensor_scalar(xnm[:, i, :], X[:, bass.ds((t.b + dc) * CT * HID + i * HID, HID)],
                                             mmv[:, i, 0:1], mrstd[:, i:i + 1], ALU.subtract, ALU.mult)
                last.then_inc(xn_done, 1)

            def split_x(t, dc):
                for k in range(KT):
                    t.need(dve, x_hi, KT, KT * dc + k + 1)
                    cols = bass.ds((t.b + dc) * CHUNK, CHUNK)
                    dve.tensor_tensor(xT[1][:, k, cols], XT[:, k, :], xT[0][:, k, cols].bitcast(F32),
                                      ALU.subtract).then_inc(x_lo, 1)

            def product(t, j):
                t.need(dve, silu_done, NF, j + 1)
                t.need(dve, up_full, NF, j + 1)
                t.need(dve, h_lo, NF, j - 1)
                dve.scalar_tensor_tensor(htmp[:, j % 2, :], UP[:, j % 2, :], d_s[:, j:j + 1] if d_s is not None else 1.0,
                                         silu[:, j % 2, :], ALU.mult, ALU.mult).then_inc(h_done, 1)

            def h_split(t, j):
                t.need(dve, h_hi, NF, j)
                dve.tensor_tensor(H[1][:, (j - 1) % 4, :], htmp[:, (j - 1) % 2, :],
                                  H[0][:, (j - 1) % 4, :].bitcast(F32), ALU.subtract).then_inc(h_lo, 1)

            def body(c, least):
                t = Step(c, least)
                for j in range(NF if least < NCH else 2):
                    m = NF * least + j
                    if j == 0 and least + 1 < NCH:
                        x_stats(t, 1)
                        x_aggregate(t, 1, lambda: product(t, 0))
                    elif m < TOT:
                        product(t, j)
                    if 1 <= m <= TOT:
                        h_split(t, j)
                    if j == 1 and least >= 1:
                        t.need(dve, down_done, NF, 0)
                        rows = X[:, bass.ds(c * CT * HID - CT * HID, CT * HID)]
                        dve.tensor_tensor(rows, O.rearrange("p a b -> p (a b)"), rows, ALU.add).then_inc(x_added, 1)
                    if least + 1 < NCH:
                        if j == 1:
                            x_norm(t, 1)
                        if j == 2:
                            split_x(t, 1)

            t0 = Step(0, 0)
            x_stats(t0, 0)
            x_aggregate(t0, 0, None)
            x_norm(t0, 0)
            split_x(t0, 0)
            run(dve, body)

        @block.gpsimd
        def _(pool):
            for c in range(NCH):
                pool.wait_ge(var_done, c + 1)
                if c >= 1:
                    pool.wait_ge(xn_done, c)
                pool.tensor_tensor(mrstd[:], mvare[:], half[:, 0:CT], ALU.pow).then_inc(rstd_done, 1)

        @block.sync
        def _(sp):
            if store:
                for c in range(NCH):
                    sp.wait_ge(x_added, c + 1)
                    sp.dma_start(out[c * CT:(c + 1) * CT].rearrange("t p d -> p t d"),
                                 X[:, c * CT * HID:(c + 1) * CT * HID].rearrange("p (t d) -> p t d", d=HID)) \
                        .then_inc(stored, 16)
                sp.wait_ge(stored, 16 * NCH)


def spline_basis():
    n = ROWS * HID
    t = np.linspace(0.0, CTRL - 1.0, n, dtype=np.float64)
    i = np.clip(np.floor(t).astype(np.int64), 0, CTRL - 2)
    f = (t - i).astype(np.float32).astype(np.float64)
    first = np.clip(i.reshape(ROWS, HID)[:, 0] - 1, 0, CTRL - TAPS)
    f2, f3 = f * f, f * f * f
    parts = [0.5 * (-f + 2 * f2 - f3), 0.5 * (2 - 5 * f2 + 3 * f3), 0.5 * (f + 4 * f2 - 3 * f3), 0.5 * (f3 - f2)]
    basis = np.zeros((ROWS, TAPS, HID))
    row, col = np.divmod(np.arange(n), HID)
    for k, part in enumerate(parts):
        tap = np.clip(i + k - 1, 0, CTRL - 1) - first[row]
        np.add.at(basis, (row, tap, col), part)
    return basis.astype(np.float32).reshape(RT, P, TAPS * HID), first


def rope_tables():
    inv = 1.0 / 10000.0 ** (np.arange(0, ROPE, 2, dtype=np.float32) / ROPE)
    a = np.outer(np.arange(SEQ, dtype=np.float32), inv)
    cos = np.concatenate([np.cos(a), np.cos(a)], 1).astype(np.float32)
    sin = np.concatenate([-np.sin(a), np.sin(a)], 1).astype(np.float32)
    return [t.reshape(TT, P, ROPE).transpose(1, 0, 2) for t in (cos, sin)]


def kernel(**inputs):
    import concourse.bacc as bacc
    from concourse.bass_utils import run_bass_kernel_spmd

    a = {k: np.asarray(w) for k, w in inputs.items()}
    A, C, FN = "L0_attn_a_", "L0_attn_b_", "L0_ffn_"
    kvb = a[A + "kv_b_w"].reshape(NH, NOPE + DV, KVL)
    qr = a[A + "q_rope_w"].T
    basis, first = spline_basis()
    cos, sin = rope_tables()
    win = first[:, None] + np.arange(TAPS)
    ctrl = np.stack([a[FN + n][win].reshape(RT, P, TAPS) for n in ("gate_cp", "up_cp", "down_cp")], 2)
    w_in = a[C + "W_in"]
    wide = lambda w: np.broadcast_to(w, (P, w.shape[0]))
    arrays = {
        "x": a[A + "hidden_states"].reshape(NTILE, P, HID),
        "wa": np.concatenate([a[A + "q_a_w"], a[A + "kv_a_w"]], 0).T.reshape(KT, P, QL + P).transpose(1, 0, 2),
        "lnw": wide(np.concatenate([a[A + "q_a_ln_w"], a[A + "kv_a_ln_w"]])),
        "lnb": wide(np.concatenate([a[A + "q_a_ln_b"], a[A + "kv_a_ln_b"]])),
        "wqb": a[A + "q_b_w"].reshape(NH, NOPE, QL).transpose(1, 0, 2),
        "wk": kvb[:, :NOPE].transpose(1, 0, 2),
        "wv": kvb[:, NOPE:].transpose(1, 0, 2),
        "wqr1": qr[:P].reshape(P, NH, ROPE),
        "wqr2": qr[P:].reshape(QK2, NH, ROPE),
        "wo": a[A + "o_w"].T.reshape(NH, DV, HID).transpose(1, 0, 2),
        "cos": cos, "sin": sin, "ident_in": np.eye(P, dtype=np.float32),
        "basis": basis, "ctrl": ctrl,
        "w_inx": w_in[:CONV].reshape(4, P, HID).transpose(1, 0, 2),
        "w_inz": w_in[CONV:].T.reshape(KT, P, CONV).transpose(1, 0, 2),
        "w_conv": a[C + "conv_w"].T.reshape(4, P, CONV).transpose(1, 0, 2),
        "w_out": a[C + "W_out"].T.reshape(4, P, HID).transpose(1, 0, 2),
        "d_in": a[C + "D"].reshape(4, P).T,
    }
    nc = bacc.Bacc("TRN2", target_bir_lowering=False, num_devices=1)
    feeds, aps = {}, {}
    for name, w in arrays.items():
        w = np.ascontiguousarray(w)
        feeds["in_" + name] = w
        aps[name] = nc.dram_tensor("in_" + name, w.shape, mybir.dt.from_np(w.dtype), kind="ExternalInput").ap()
    aps["out"] = nc.dram_tensor("out_x", (NTILE, P, HID), F32, kind="ExternalOutput").ap()
    build(nc, **aps)
    r = run_bass_kernel_spmd(nc, [feeds], core_ids=[0])
    return r.results[0]["out_x"].reshape(NB, SEQ, HID)
```

```python
from contextlib import ExitStack

import numpy as np
import concourse.bass as bass
from concourse import mybir

F32 = mybir.dt.float32
F32R = mybir.dt.float32r
ALU = mybir.AluOpType
ACT = mybir.ActivationFunctionType
AX = mybir.AxisListType

P = 128
NB, SEQ, HID = 8, 256, 256
NH, NOPE, ROPE, DV = 16, 128, 64, 128
QL, KVL = 192, 64
QK2 = QL - P
FFN, CONV = 1024, 512
CTRL = 2033
TAPS = 6
EPS = 1e-5
SCALE = 1.0 / float(np.sqrt(NOPE + ROPE))
KT = HID // P
TT = SEQ // P
NTILE = NB * TT
PAIRS = NH // 2
ROWS = FFN * HID // HID
RT = ROWS // P
CHUNK = 512
NCH = NB * SEQ // CHUNK
CT = CHUNK // P
G4 = 4
HG = 8
LEAD = 4
LAST = NB * PAIRS


class Step:

    def __init__(self, b, least):
        self.b, self.least = b, least

    def need(self, eng, sem, per, const):
        if per * self.least + const > 0:
            eng.wait_ge(sem, self.b * per + const)

    def has(self, per, const):
        return per * self.least + const >= 0


def f32r_matmul3(pe, out, hi, lo, whi, wlo, first, last):
    pe.matmul(out, lhsT=hi, rhs=whi, start=first, stop=False, skip_group_check=True)
    pe.matmul(out, lhsT=hi, rhs=wlo, start=False, stop=False, skip_group_check=True)
    return pe.matmul(out, lhsT=lo, rhs=whi, start=False, stop=last, skip_group_check=True)


def build(nc, x, wa, lnw, lnb, wqb, wk, wv, wqr1, wqr2, wo, cos, sin, ident_in, basis, ctrl,
          w_inx, w_inz, w_conv, w_out, d_in, out):
    top = ExitStack()
    with top:
        def sem(name):
            return top.enter_context(nc.semaphore(name))

        def one(stack, name, shape, dt=F32):
            return stack.enter_context(nc.sbuf_tensor(name, shape, dt))

        def pair(stack, name, shape):
            return [one(stack, f"{name}_{p}", shape, F32R) for p in ("hi", "lo")]

        ps = top.enter_context(nc.psum_tensor("ps", [P, 8, 512], F32))

        X = one(top, "X", [P, NTILE * HID])
        ident = one(top, "ident", [P, P])
        half = one(top, "half", [P, CT])
        early = ExitStack()
        wo_s = one(early, "wo_s", [P, NH, HID])
        wv_s = one(early, "wv_s", [P, NH, KVL])
        wk_s = one(early, "wk_s", [P, NH, KVL])
        early.close()
        Wn = one(top, "Wn", [P, 3, RT, HID])

        attn = ExitStack()
        Wq1 = pair(attn, "Wq1", [P, NH, P])
        Wq2s = one(attn, "Wq2s", [P, NH, P], F32R)
        Wq2l = one(attn, "Wq2l", [QK2, NH, P], F32R)
        QT = pair(attn, "QT", [P, NH, SEQ])
        kT = pair(attn, "kT", [P, NB * SEQ])
        Bo = pair(attn, "Bo", [P, PAIRS, HID])
        Wa = pair(attn, "Wa", [P, KT, QL + P])
        lnws = one(attn, "lnws", [P, QL + KVL])
        lnbs = one(attn, "lnbs", [P, QL + KVL])
        cosT = one(attn, "cosT", [P, TT, ROPE])
        sinT = one(attn, "sinT", [P, TT, ROPE])
        cpad = pair(attn, "cpad", [P, TT, 3 * KVL])
        zc = one(attn, "zc", [P, NTILE * KVL])
        zkn = one(attn, "zkn", [P, TT, P])
        zq = one(attn, "zq", [P, TT, QL])
        xn = one(attn, "xn", [P, TT, HID])
        xaT = pair(attn, "xaT", [P, KT, SEQ])
        ql1 = pair(attn, "ql1", [P, SEQ])
        ql2 = one(attn, "ql2", [P, SEQ], F32R)
        raw = ExitStack()
        wqb_s = one(raw, "wqb_s", [P, NH, QL])
        wqr1_s = one(raw, "wqr1_s", [P, NH, ROPE])
        wqr2_s = one(raw, "wqr2_s", [QK2, NH, ROPE])
        wa_s = one(raw, "wa_s", [P, KT, QL + P])
        raw.close()
        E = one(attn, "E", [P, 2, 4, SEQ])
        PT = pair(attn, "PT", [P, 2, 4, SEQ])
        Qt = one(attn, "Qt", [P, 2, G4, P])
        rtmp = one(attn, "rtmp", [P, G4, ROPE])
        Us = pair(attn, "Us", [P, 2, SEQ])
        basis_s = one(attn, "basis_s", [P, TAPS, HID])
        ctrl_s = one(attn, "ctrl_s", [P, 3, TAPS])
        rows_s = one(attn, "rows_s", [P, 3, HID])
        sptmp = one(attn, "sptmp", [P, 2, HID])
        negmax = one(attn, "negmax", [P, 2, 4])
        rowsum = one(attn, "rowsum", [P, 2, 4])
        rinv = one(attn, "rinv", [P, 2, 4])
        st6, mv = one(attn, "st6", [P, TT, 6]), one(attn, "mv", [P, TT, 2])
        vare, rstd = one(attn, "vare", [P, TT]), one(attn, "rstd", [P, TT])
        zst6, zmv = one(attn, "zst6", [P, 2, 6]), one(attn, "zmv", [P, 2, 2])
        zvare, zrstd = one(attn, "zvare", [P, 2]), one(attn, "zrstd", [P, 2])
        ztmp, krtmp, krtmp2 = xn[:, 0, :], xn[:, 1, 0:ROPE], xn[:, 1, ROPE:2 * ROPE]
        attn.close()

        Wg = pair(top, "Wg", [P, KT, FFN])
        Wu = pair(top, "Wu", [P, KT, FFN])
        Wd = pair(top, "Wd", [P, FFN // P, HID])
        xT = pair(top, "xT", [P, KT, NB * SEQ])
        wconv_s = one(top, "wconv_s", [P, 4, CONV])
        winx_s = one(top, "winx_s", [P, 4, HID])
        winz_s = one(top, "winz_s", [P, KT, CONV])
        wout_s = one(top, "wout_s", [P, CONV // P, HID])
        d_s = one(top, "d_s", [P, CONV // P])
        htmp = one(top, "htmp", [P, 2, CHUNK])
        silu = one(top, "silu", [P, 2, CHUNK])
        mst6, mmv = one(top, "mst6", [P, CT, 6]), one(top, "mmv", [P, CT, 2])
        mvare, mrstd = one(top, "mvare", [P, CT]), one(top, "mrstd", [P, CT])
        xnm = one(top, "xnm", [P, CT, HID])
        Co = pair(top, "Co", [P, CONV // P, HID])
        H = pair(top, "H", [P, 4, CHUNK])
        Cz = pair(top, "Cz", [P, KT, CONV])
        Cx = pair(top, "Cx", [P, KT, CONV])

        S = ps[:, 0:2, :]
        ET, U, O, Q, QTp, F = (ps[:, 2 + i, :] for i in range(6))
        mXT, mG, mUP, mO = (ps[:, 2 * i:2 * i + 2, :] for i in range(4))

        x0_loaded, wa_loaded, first_loaded, q_loaded, o_loaded, x_loaded = (sem(n) for n in (
            "x0_loaded", "wa_loaded", "first_loaded", "q_loaded", "o_loaded", "x_loaded"))
        zeroed, wa_hi, wa_lo = sem("zeroed"), sem("wa_hi"), sem("wa_lo")
        join_q, wq_hi, wq_lo = sem("join_q"), sem("wq_hi"), sem("wq_lo")
        join_o, bo_hi, bo_lo = sem("join_o"), sem("bo_hi"), sem("bo_lo")
        scores_full, et_full, u_full, o_added = sem("scores_full"), sem("et_full"), sem("u_full"), sem("o_added")
        q_full, qt_full, f_full = sem("q_full"), sem("qt_full"), sem("f_full")
        max_done, exp_done, rinv_done, norm_done = (sem(n) for n in ("max_done", "exp_done", "rinv_done", "norm_done"))
        pt_hi, pt_lo, u_hi, u_lo = sem("pt_hi"), sem("pt_lo"), sem("u_hi"), sem("u_lo")
        qnope_done, rope_mul, qtok_done = sem("qnope_done"), sem("rope_mul"), sem("qtok_done")
        qT_hi, qT_lo = sem("qT_hi"), sem("qT_lo")
        f_hi, f_lo = sem("f_hi"), sem("f_lo")
        fe_chain = sem("fe_chain")
        xvar_done, xrstd_done, xn_done = sem("xvar_done"), sem("xrstd_done"), sem("xn_done")
        zvar_done, zrstd_done = sem("zvar_done"), sem("zrstd_done")
        zscaled, z_done = sem("zscaled"), sem("z_done")
        c_hi, c_lo, x_added = sem("c_hi"), sem("c_lo"), sem("x_added")
        basis_loaded, rows_kept = sem("basis_loaded"), sem("rows_kept")
        sp_chain, spd_chain = sem("sp_chain"), sem("spd_chain")
        sw_turned, sw_hi, sw_lo = sem("sw_turned"), sem("sw_hi"), sem("sw_lo")
        cw_loaded, cw_joined, cw_hi, cw_lo = sem("cw_loaded"), sem("cw_joined"), sem("cw_hi"), sem("cw_lo")
        gate_full, up_full, down_done = sem("gate_full"), sem("up_full"), sem("down_done")
        silu_done, h_done, h_hi, h_lo = sem("silu_done"), sem("h_done"), sem("h_hi"), sem("h_lo")
        m_chain, m_var, m_rstd, m_xn = sem("m_chain"), sem("m_var"), sem("m_rstd"), sem("m_xn")
        xt_full, xt_hi, xt_lo = sem("xt_full"), sem("xt_hi"), sem("xt_lo")
        m_added, stored = sem("m_added"), sem("stored")

        SP_LINKS = 2 * (2 * TAPS - 1)
        FE_X, FE_Z = 2, 2
        FE_LINKS = FE_X + TT * FE_Z

        def entries(eng, body):
            body(0, 0)
            with eng.Fori(1, NB - 2) as b:
                body(b, 1)
            body(NB - 2, NB - 2)
            body(NB - 1, NB - 1)
            body(NB, NB)

        BLOCKS = [(Wg, Wu, Wd, FFN // P, 0, 0), (Cz, Cx, Co, CONV // P, NCH, NCH * FFN // P),
                  (Wg, Wu, Wd, FFN // P, 2 * NCH, NCH * (FFN + CONV) // P)]
        M_ALL = NCH * (2 * FFN + CONV) // P

        def chunks(eng, body):
            for k in range(len(BLOCKS)):
                body(k, 0, 0)
                with eng.Fori(1, NCH - 1) as c:
                    body(k, c, 1)
                body(k, NCH - 1, NCH - 1)
            body(len(BLOCKS), 0, 0)

        UNITS = [(0, 0), (1, 0), (0, 1), (1, 1), (0, 2), (1, 2), (2, 0), (2, 1), (2, 2), (0, 3), (1, 3), (2, 3)]
        SWB = [7, 5, 6]

        def unit_views(u):
            w, r = UNITS[u]
            bank = ps[:, SWB[u % 3], :]
            if w < 2:
                dst = (Wg, Wu)[w]
                return [(bank.rearrange("p (k c) -> p k c", k=KT), [d[:, :, r * 2 * P:(r + 1) * 2 * P] for d in dst])]
            return [(bank[:, k * 2 * P:(k + 1) * 2 * P].rearrange("p (o a) -> p a o", a=4),
                     [d[:].rearrange("p (a k) o -> p a k o", k=KT)[:, :, k, r * 64:(r + 1) * 64] for d in Wd])
                    for k in range(KT)]

        def units_at(least, s):
            if least == NB - 1:
                return {4: [0], 5: [1], 6: [2, 3], 7: [4, 5]}.get(s, [])
            return {0: [6, 7, 8], 1: [9, 10], 2: [11]}[s] if least == NB else []

        OB = [4, 6, 0, 1, 2, 3, 4, 0]

        block = top.enter_context(nc.Block())

        @block.tensor
        def _(pe):
            def turn(dst, src):
                return pe.matmul(dst, lhsT=src, rhs=ident[:], is_transpose=True, start=True, stop=True)

            def join_query(g, half):
                for i in range(half * HG // 2, (half + 1) * HG // 2):
                    h = g * HG + i
                    cols = slice(i * KVL, (i + 1) * KVL)
                    pe.matmul(ps[:, 2 * g, cols], lhsT=wqb_s[:, h, 0:P], rhs=wk_s[:, h, :], start=True, stop=True)
                    last = pe.matmul(ps[0:QK2, 2 * g + 1, cols], lhsT=wqb_s[:, h, P:QL], rhs=wk_s[:, h, :],
                                     start=True, stop=True)
                if half == 1:
                    last.then_inc(join_q, 1)

            def join_output(s):
                if s in (2, 4):
                    pe.wait_ge(wq_lo, s // 2)
                if s >= 6:
                    pe.wait_ge(bo_lo, 1 if s == 6 else 3)
                for j in range(2):
                    last = pe.matmul(ps[0:KVL, OB[s], j * HID:(j + 1) * HID], lhsT=wv_s[:, 2 * s + j, :],
                                     rhs=wo_s[:, 2 * s + j, :], start=True, stop=True)
                last.then_inc(join_o, 1)

            def turn_x(t, dj):
                t.need(pe, xn_done, 1, dj + 1)
                t.need(pe, f_lo, 5, 5 * dj)
                for k in range(KT):
                    for i in range(TT):
                        c = (k * TT + i) * P
                        last = turn(F[:, c:c + P], xn[:, i, k * P:(k + 1) * P])
                last.then_inc(f_full, 1)

            def latents(t, dj, i):
                t.need(pe, f_lo, 5, 5 * dj + 1 + i)
                rows = slice(i * P, (i + 1) * P)
                for k in range(KT):
                    last = f32r_matmul3(pe, F[:, 0:QL + P], xaT[0][:, k, rows], xaT[1][:, k, rows],
                                        Wa[0][:, k, :], Wa[1][:, k, :], k == 0, k == KT - 1)
                last.then_inc(f_full, 1)

            def turn_k(t, dj):
                t.need(pe, z_done, 2, 2 * dj + 2)
                t.need(pe, f_lo, 5, 5 * dj + 3)
                for i in range(TT):
                    last = turn(F[:, i * P:(i + 1) * P], zkn[:, i, :])
                last.then_inc(f_full, 1)

            def turn_q(t, dj):
                t.need(pe, z_done, 2, 2 * dj + 2)
                t.need(pe, f_lo, 5, 5 * dj + 4)
                for i in range(TT):
                    turn(F[:, i * P:(i + 1) * P], zq[:, i, 0:P])
                    last = turn(F[0:QK2, SEQ + i * P:SEQ + (i + 1) * P], zq[:, i, P:QL])
                last.then_inc(f_full, 1)

            def query(t, dq):
                idx = dq % 8
                i, g = idx % 2, idx // 2
                if idx == 0:
                    t.need(pe, f_lo, 5, 5 * (dq // 8) + 5)
                t.need(pe, rope_mul, 8, dq)
                rows, heads = slice(i * P, (i + 1) * P), slice(g * G4, (g + 1) * G4)
                w1h, w1l, w2s, w2l = (a[:, heads, :].rearrange("p h f -> p (h f)") for a in (*Wq1, Wq2s, Wq2l))
                f32r_matmul3(pe, Q, ql1[0][:, rows], ql1[1][:, rows], w1h, w1l, True, False)
                pe.matmul(Q, lhsT=ql2[:, rows], rhs=w2s, start=False, stop=False, skip_group_check=True)
                pe.matmul(Q, lhsT=ql2[0:QK2, rows], rhs=w2l, start=False, stop=True,
                          skip_group_check=True).then_inc(q_full, 1)

            def turn_query(t, dq):
                t.need(pe, qtok_done, 8, dq + 1)
                t.need(pe, qT_lo, 8, dq)
                for j in range(G4):
                    last = turn(QTp[:, j * P:(j + 1) * P], Qt[:, dq % 2, j, :])
                last.then_inc(qt_full, 1)

            def scores(t, s, i):
                t.need(pe, qT_lo, 8, 2 * (s // 2) + i + 1)
                if s == 0 and i == 0:
                    t.need(pe, f_lo, 5, 4)
                t.need(pe, exp_done, 16, 2 * s + i - 1)
                rows, keys = slice(i * P, (i + 1) * P), bass.ds(t.b * SEQ, SEQ)
                for j in range(2):
                    last = f32r_matmul3(pe, S[:, i, j * SEQ:(j + 1) * SEQ], QT[0][:, 2 * s + j, rows],
                                        QT[1][:, 2 * s + j, rows], kT[0][:, keys], kT[1][:, keys], True, True)
                last.then_inc(scores_full, 1)

            def turn_probs(t, s, i):
                t.need(pe, norm_done, 16, 2 * (s - 1) + i + 1)
                t.need(pe, pt_lo, 16, 2 * (s - 1) + i)
                for k in range(TT):
                    for j in range(2):
                        c = (k * 2 + j) * P
                        last = turn(ET[:, c:c + P], E[:, (s - 1) % 2, 2 * i + j, k * P:(k + 1) * P])
                last.then_inc(et_full, 1)

            def values(t, s):
                t.need(pe, pt_lo, 16, 2 * (s - 2) + 2)
                t.need(pe, u_lo, 8, s - 2)
                if s == 2:
                    t.need(pe, c_lo, 1, 1)
                for k in range(TT):
                    for j in range(2):
                        cols = slice(KVL, 3 * KVL) if j == 0 else slice(0, 2 * KVL)
                        last = f32r_matmul3(pe, U[:, 0:SEQ], cpad[0][:, k, cols], cpad[1][:, k, cols],
                                            PT[0][:, s % 2, 2 * k + j, :], PT[1][:, s % 2, 2 * k + j, :],
                                            k == 0 and j == 0, k == 1 and j == 1)
                last.then_inc(u_full, 1)

            def output(t, s):
                p = (s - 3) % PAIRS
                t.need(pe, u_lo, 8, s - 2)
                if p == 0:
                    t.need(pe, x_added, 1, 0)
                for i in range(TT):
                    rows = slice(i * P, (i + 1) * P)
                    last = f32r_matmul3(pe, O[:, i * HID:(i + 1) * HID], Us[0][:, (s - 3) % 2, rows],
                                        Us[1][:, (s - 3) % 2, rows], Bo[0][:, p, :], Bo[1][:, p, :],
                                        p == 0 and i == 0, p == PAIRS - 1)
                last.then_inc(o_added, 1)

            def turn_unit(u):
                w, r = UNITS[u]
                pe.wait_ge(rows_kept, 16 * (2 * r + 2))
                if u == 0:
                    pe.wait_ge(rope_mul, LAST)
                if u == 2:
                    pe.wait_ge(qT_lo, LAST)
                if u >= 3:
                    pe.wait_ge(sw_lo, u - 2)
                for k in range(KT):
                    for i in range(2):
                        c = (2 * k + i) * P
                        last = turn(ps[:, SWB[u % 3], c:c + P], Wn[:, w, 2 * r + i, k * P:(k + 1) * P])
                last.then_inc(sw_turned, 1)

            def entry(b, least):
                t = Step(b, least)
                for s in range(8 if least < NB else 3):
                    n = PAIRS * least + s
                    if n < LAST:
                        scores(t, s, 0)
                        scores(t, s, 1)
                    if 1 <= n <= LAST:
                        turn_probs(t, s, 0)
                    if 2 <= n <= LAST + 1:
                        values(t, s)
                    if n + LEAD < LAST:
                        query(t, s + LEAD)
                    if 1 <= n <= LAST:
                        turn_probs(t, s, 1)
                    if s == 1 and least + 1 < NB:
                        turn_k(t, 1)
                    if s == 3 and least + 1 < NB:
                        turn_q(t, 1)
                    if s == 4 and least + 2 < NB:
                        turn_x(t, 2)
                    if 3 <= n <= LAST + 2:
                        output(t, s)
                    if n + LEAD - 1 < LAST:
                        turn_query(t, s + LEAD - 1)
                    if s in (5, 7) and least + 2 < NB:
                        latents(t, 2, (s - 5) // 2)
                    for u in units_at(least, s):
                        turn_unit(u)
                    if least == NB and s == 0:
                        pe.wait_ge(exp_done, 2 * LAST)
                        turn_mx(Step(0, 0), 0)

            def turn_mx(t, gc):
                t.need(pe, m_xn, 1, gc + 1)
                t.need(pe, xt_lo, KT, KT * gc)
                for k in range(KT):
                    for i in range(CT):
                        last = turn(mXT[:, k, i * P:(i + 1) * P], xnm[:, i, k * P:(k + 1) * P])
                    last.then_inc(xt_full, 1)

            def inner(t, j, W, bank, full):
                cols = bass.ds(t.b * CHUNK, CHUNK)
                for k in range(KT):
                    last = f32r_matmul3(pe, bank, W[0][:, k, j * P:(j + 1) * P], W[1][:, k, j * P:(j + 1) * P],
                                        xT[0][:, k, cols], xT[1][:, k, cols], k == 0, k == KT - 1)
                last.then_inc(full, 1)

            def down(t, nf, m, j, f, W, closes, before=None):
                t.need(pe, h_lo, nf, m - 1)
                if before is not None:
                    t.need(pe, m_added, 1, before)
                for i in range(CT):
                    rows = slice(i * P, (i + 1) * P)
                    last = f32r_matmul3(pe, mO[:, i // 2, (i % 2) * HID:(i % 2 + 1) * HID], H[0][:, (j - 2) % 4, rows],
                                        H[1][:, (j - 2) % 4, rows], W[0][:, f, :], W[1][:, f, :],
                                        f == 0 and i % 2 == 0, closes)
                last.then_inc(down_done, 1)

            def chunk(k, c, least):
                t = Step(c, least)
                if k == len(BLOCKS):
                    _, _, pd, pnf, pc0, pm0 = BLOCKS[k - 1]
                    for j in range(2):
                        down(t, 0, M_ALL + j, j, pnf - 2 + j, pd, j == 1)
                    return
                Wa_, Wb_, Wc_, nf, c0, m0 = BLOCKS[k]
                for j in range(nf):
                    m = m0 + j
                    if j == 0:
                        t.need(pe, xt_lo, KT, KT * (c0 + 1))
                    if k == 1 and least == 0 and j == 0:
                        pe.wait_ge(cw_lo, 1)
                    if k == 0 and least == 0 and j == 0:
                        pe.wait_ge(sw_lo, len(UNITS))
                        pe.wait_ge(x_added, NB)
                    t.need(pe, silu_done, nf, m - 1)
                    inner(t, j, Wa_, mG[:, j % 2, :], gate_full)
                    t.need(pe, h_done, nf, m - 1)
                    inner(t, j, Wb_, mUP[:, j % 2, :], up_full)
                    if j >= 2:
                        down(t, nf, m, j, j - 2, Wc_, False, c0 if j == 2 else None)
                    elif least >= 1:
                        down(t, nf, m, j, nf - 2 + j, Wc_, j == 1)
                    elif k >= 1:
                        down(t, nf, m, j, BLOCKS[k - 1][3] - 2 + j, BLOCKS[k - 1][2], j == 1)
                    if j == 2 and not (k == len(BLOCKS) - 1 and least == NCH - 1):
                        turn_mx(t, c0 + 1)
                    if k == 0 and least == NCH - 1 and j == 4:
                        join_conv()

            def join_conv():
                pe.wait_ge(cw_loaded, 16 * 5)
                pe.wait_ge(xt_lo, KT * (NCH + 1))
                for m in range(KT):
                    for k in range(4):
                        last = pe.matmul(mXT[:, m, :], lhsT=winx_s[:, k, m * P:(m + 1) * P], rhs=wconv_s[:, k, :],
                                         start=k == 0, stop=k == 3)
                    last.then_inc(cw_joined, 1)

            t0 = Step(0, 0)
            pe.wait_ge(x0_loaded, 32)
            turn_x(t0, 0)
            pe.wait_ge(wa_lo, 1)
            latents(t0, 0, 0)
            pe.wait_ge(q_loaded, 16 * 4)
            join_query(0, 0)
            latents(t0, 0, 1)
            join_query(0, 1)
            join_query(1, 0)
            join_query(1, 1)
            pe.wait_ge(o_loaded, 32)
            join_output(0)
            turn_k(t0, 0)
            join_output(1)
            turn_q(t0, 0)
            join_output(2)
            turn_x(t0, 1)
            for q in range(LEAD):
                if q == 0:
                    pe.wait_ge(wq_lo, 1)
                query(t0, q)
                join_output(q + 3)
                if q == 1:
                    latents(t0, 1, 0)
                if q == 3:
                    latents(t0, 1, 1)
                if q >= 1:
                    if q == 1:
                        pe.wait_ge(bo_lo, 2)
                    turn_query(t0, q - 1)
            join_output(PAIRS - 1)
            pe.wait_ge(bo_lo, PAIRS)
            entries(pe, entry)
            chunks(pe, chunk)

        @block.scalar
        def _(act):
            def copy(dst, src, **kw):
                return act.activation(dst, src, ACT.Copy, **kw)

            def split_x(t, dj):
                t.need(act, f_full, 5, 5 * dj + 1)
                copy(xaT[0][:].rearrange("p k c -> p (k c)"), F).then_inc(f_hi, 1)

            def split_k(t, dj):
                t.need(act, f_full, 5, 5 * dj + 4)
                copy(kT[0][:, bass.ds((t.b + dj) * SEQ, SEQ)], F[:, 0:SEQ]).then_inc(f_hi, 1)

            def split_q(t, dj):
                t.need(act, f_full, 5, 5 * dj + 5)
                if dj:
                    t.need(act, q_full, 8, 8)
                copy(ql1[0][:], F[:, 0:SEQ])
                copy(ql2[0:QK2, :], F[0:QK2, SEQ:2 * SEQ]).then_inc(f_hi, 1)

            def query_weights(g):
                heads = slice(g * HG, (g + 1) * HG)
                copy(Wq1[0][:, heads, KVL:P], wqr1_s[:, heads, :], scale=SCALE)
                for rows in (slice(0, QK2), slice(QK2, P)):
                    copy(Wq2s[rows, heads, KVL:P], wqr2_s[:, heads, :], scale=SCALE)
                act.wait_ge(join_q, g + 1)
                copy(Wq1[0][:, heads, 0:KVL], ps[:, 2 * g, :].rearrange("p (h c) -> p h c", c=KVL), scale=SCALE)
                for rows in (slice(0, QK2), slice(QK2, P)):
                    last = copy(Wq2s[rows, heads, 0:KVL],
                                ps[0:QK2, 2 * g + 1, :].rearrange("p (h c) -> p h c", c=KVL), scale=SCALE)
                last.then_inc(wq_hi, 1)

            def output_weights(s):
                act.wait_ge(join_o, s + 1)
                for j in range(2):
                    last = copy(Bo[0][j * KVL:(j + 1) * KVL, s, :], ps[0:KVL, OB[s], j * HID:(j + 1) * HID])
                last.then_inc(bo_hi, 1)

            def probs(t, s, i):
                t.need(act, et_full, 16, 2 * (s - 1) + i + 1)
                t.need(act, u_full, 8, s - 2)
                copy(PT[0][:, (s - 1) % 2, :, i * P:(i + 1) * P], ET.rearrange("p (a q) -> p a q", q=P)) \
                    .then_inc(pt_hi, 1)

            def exps(t, s, i):
                par = s % 2
                t.need(act, max_done, 16, 2 * s + i + 1)
                t.need(act, et_full, 16, 2 * (s - 2) + i + 1)
                t.need(act, rinv_done, 16, 2 * (s - 2) + i + 1)
                for j in range(2):
                    a = 2 * i + j
                    last = act.activation(E[:, par, a, :], S[:, i, j * SEQ:(j + 1) * SEQ], ACT.Exp,
                                          bias=negmax[:, par, a:a + 1], accum_out=rowsum[:, par, a:a + 1])
                last.then_inc(exp_done, 1)

            def u_split(t, s):
                t.need(act, u_full, 8, s - 1)
                t.need(act, o_added, 8, s - 3)
                copy(Us[0][:, s % 2, :], U[:, 0:SEQ]).then_inc(u_hi, 1)

            def q_nope(t, dq):
                t.need(act, q_full, 8, dq + 1)
                t.need(act, qt_full, 8, dq - 1)
                copy(Qt[:, dq % 2, :, 0:KVL], Q.rearrange("p (h f) -> p h f", f=P)[:, :, 0:KVL]).then_inc(qnope_done, 1)

            def q_turned(t, dq):
                idx = dq % 8
                g, i = idx // 2, idx % 2
                t.need(act, qt_full, 8, dq + 1)
                t.need(act, scores_full, 16, 16 * (dq // 8 - 1) + 4 * g + 2 + i + 1)
                copy(QT[0][:, g * G4:(g + 1) * G4, i * P:(i + 1) * P], QTp.rearrange("p (h q) -> p h q", q=P)) \
                    .then_inc(qT_hi, 1)

            def unit_hi(u):
                act.wait_ge(sw_turned, u + 1)
                if u == 6:
                    act.wait_ge(scores_full, 2 * LAST)
                for src, (hi, lo) in unit_views(u):
                    last = copy(hi, src)
                last.then_inc(sw_hi, 1)

            def entry(b, least):
                t = Step(b, least)
                for s in range(8 if least < NB else 3):
                    n = PAIRS * least + s
                    if 1 <= n <= LAST:
                        probs(t, s, 0)
                    if n < LAST:
                        exps(t, s, 0)
                    if 2 <= n <= LAST + 1:
                        u_split(t, s)
                    if n < LAST:
                        exps(t, s, 1)
                    if n + LEAD < LAST:
                        q_nope(t, s + LEAD)
                    if s == 1 and least < NB:
                        t.need(act, u_full, 8, 0)
                        t.need(act, z_done, 2, 2)
                        copy(cpad[0][:, :, KVL:2 * KVL],
                             zc[:, bass.ds(b * TT * KVL, TT * KVL)].rearrange("p (i f) -> p i f", f=KVL)).then_inc(c_hi, 1)
                    if 1 <= n <= LAST:
                        probs(t, s, 1)
                    if s == 1 and least + 1 < NB:
                        split_k(t, 1)
                    if s == 3 and least + 1 < NB:
                        split_q(t, 1)
                    if s == 4 and least + 2 < NB:
                        split_x(t, 2)
                    if n + LEAD - 1 < LAST:
                        q_turned(t, s + LEAD - 1)
                    for u in units_at(least, s):
                        unit_hi(u)
                    if least == NB and s == 0:
                        split_mx(Step(0, 0), 0, 0)

            def split_mx(t, gc, slot):
                for k in range(KT):
                    t.need(act, xt_full, KT, KT * gc + k + 1)
                    copy(xT[0][:, k, bass.ds(slot * CHUNK, CHUNK)], mXT[:, k, :]).then_inc(xt_hi, 1)

            def chunk(k, c, least):
                if k == len(BLOCKS):
                    return
                t = Step(c, least)
                nf, c0, m0 = BLOCKS[k][3:]
                for j in range(nf):
                    m = m0 + j
                    t.need(act, gate_full, nf, m + 1)
                    t.need(act, h_done, nf, m - 1)
                    act.activation(silu[:, j % 2, :], mG[:, j % 2, :], ACT.Silu).then_inc(silu_done, 1)
                    t.need(act, h_done, nf, m + 1)
                    t.need(act, down_done, nf, m - 3)
                    copy(H[0][:, j % 4, :], htmp[:, j % 2, :]).then_inc(h_hi, 1)
                    if j == 2 and not (k == len(BLOCKS) - 1 and least == NCH - 1):
                        split_mx(t, c0 + 1, 0 if least == NCH - 1 else c + 1)

            act.dma_start(wa_s[:], wa).then_inc(wa_loaded, 16)
            for dst, src in ((wk_s, wk), (wqb_s, wqb), (wqr1_s, wqr1), (wqr2_s, wqr2)):
                act.dma_start(dst[:], src).then_inc(q_loaded, 16)
            t0 = Step(0, 0)
            act.wait_ge(wa_loaded, 16)
            copy(Wa[0][:], wa_s[:]).then_inc(wa_hi, 1)
            split_x(t0, 0)
            act.wait_ge(q_loaded, 16 * 4)
            query_weights(0)
            split_k(t0, 0)
            output_weights(0)
            split_q(t0, 0)
            output_weights(1)
            split_x(t0, 1)
            query_weights(1)
            for q in range(LEAD):
                q_nope(t0, q)
                output_weights(q + 2)
                if q >= 1:
                    q_turned(t0, q - 1)
            output_weights(PAIRS - 2)
            output_weights(PAIRS - 1)
            entries(act, entry)
            chunks(act, chunk)

        @block.vector
        def _(dve):
            def minus(dst, src, hi):
                return dve.tensor_tensor(dst, src, hi.bitcast(F32), ALU.subtract)

            def x_stats(t, dj):
                for i in range(TT):
                    last = dve.bn_stats(st6[:, i, :], X[:, bass.ds((t.b + dj) * TT * HID + i * HID, HID)])
                last.then_inc(fe_chain, 1)

            def x_aggregate(t, dj, between):
                t.need(dve, fe_chain, FE_LINKS, FE_LINKS * dj + 1)
                if between is not None:
                    between()
                for i in range(TT):
                    last = dve.bn_aggr(mv[:, i, :], st6[:, i, :])
                last.then_inc(fe_chain, 1)
                t.need(dve, fe_chain, FE_LINKS, FE_LINKS * dj + 2)
                t.need(dve, xrstd_done, 1, dj)
                dve.tensor_scalar(vare[:], mv[:, :, 1], EPS, None, ALU.add).then_inc(xvar_done, 1)

            def x_norm(t, dj):
                t.need(dve, xrstd_done, 1, dj + 1)
                t.need(dve, z_done, 2, 2 * dj)
                for i in range(TT):
                    last = dve.tensor_scalar(xn[:, i, :], X[:, bass.ds((t.b + dj) * TT * HID + i * HID, HID)],
                                             mv[:, i, 0:1], rstd[:, i:i + 1], ALU.subtract, ALU.mult)
                last.then_inc(xn_done, 1)

            def split_x(t, dj):
                t.need(dve, f_hi, 3, 3 * dj + 1)
                minus(xaT[1][:].rearrange("p k c -> p (k c)"), F, xaT[0][:].rearrange("p k c -> p (k c)")) \
                    .then_inc(f_lo, 1)

            def z_stats(t, dj, i):
                c0 = FE_LINKS * dj + FE_X + FE_Z * i
                t.need(dve, f_full, 5, 5 * dj + 2 + i)
                dve.bn_stats(zst6[:, 0, :], F[:, 0:QL])
                dve.bn_stats(zst6[:, 1, :], F[:, QL:QL + KVL]).then_inc(fe_chain, 1)
                t.need(dve, z_done, 2, 2 * dj + i)
                t.need(dve, fe_chain, FE_LINKS, c0 + 1)
                dve.tensor_tensor(krtmp, F[:, QL + KVL:QL + P], cosT[:, i, :], ALU.mult)
                for a in range(2):
                    last = dve.bn_aggr(zmv[:, a, :], zst6[:, a, :])
                last.then_inc(fe_chain, 1)
                t.need(dve, fe_chain, FE_LINKS, c0 + 2)
                dve.tensor_scalar(zvare[:], zmv[:, :, 1], EPS, None, ALU.add).then_inc(zvar_done, 1)

            def z_norm(t, dj, i):
                t.need(dve, zrstd_done, 2, 2 * dj + i + 1)
                for a, cols in enumerate((slice(0, QL), slice(QL, QL + KVL))):
                    dve.tensor_scalar(ztmp[:, cols], F[:, cols], zmv[:, a, 0:1], zrstd[:, a:a + 1],
                                      ALU.subtract, ALU.mult)
                dve.tensor_tensor(krtmp2.rearrange("p (z e) -> p z e", z=2),
                                  F[:, QL + KVL:QL + P].rearrange("p (z e) -> p z e", z=2)[:, ::-1, :],
                                  sinT[:, i, :].rearrange("p (z e) -> p z e", z=2), ALU.mult).then_inc(f_lo, 1)

            def split_k(t, dj):
                t.need(dve, f_hi, 3, 3 * dj + 2)
                cols = bass.ds((t.b + dj) * SEQ, SEQ)
                minus(kT[1][:, cols], F[:, 0:SEQ], kT[0][:, cols]).then_inc(f_lo, 1)

            def split_q(t, dj):
                t.need(dve, f_hi, 3, 3 * dj + 3)
                minus(ql1[1][:], F[:, 0:SEQ], ql1[0][:])
                minus(ql2[QK2:P, :], F[0:QK2, SEQ:2 * SEQ], ql2[0:QK2, :]).then_inc(f_lo, 1)

            def query_weights(g):
                heads = slice(g * HG, (g + 1) * HG)
                dve.wait_ge(wq_hi, g + 1)
                for dst, hi, src in (
                        (Wq1[1][:, heads, KVL:P], Wq1[0][:, heads, KVL:P], wqr1_s[:, heads, :]),
                        (Wq2l[:, heads, KVL:P], Wq2s[0:QK2, heads, KVL:P], wqr2_s[:, heads, :]),
                        (Wq1[1][:, heads, 0:KVL], Wq1[0][:, heads, 0:KVL],
                         ps[:, 2 * g, :].rearrange("p (h c) -> p h c", c=KVL)),
                        (Wq2l[:, heads, 0:KVL], Wq2s[0:QK2, heads, 0:KVL],
                         ps[0:QK2, 2 * g + 1, :].rearrange("p (h c) -> p h c", c=KVL))):
                    last = dve.scalar_tensor_tensor(dst, src, SCALE, hi.bitcast(F32), ALU.mult, ALU.subtract)
                last.then_inc(wq_lo, 1)

            def output_weights(s):
                dve.wait_ge(bo_hi, s + 1)
                for j in range(2):
                    rows = slice(j * KVL, (j + 1) * KVL)
                    last = minus(Bo[1][rows, s, :], ps[0:KVL, OB[s], j * HID:(j + 1) * HID], Bo[0][rows, s, :])
                last.then_inc(bo_lo, 1)

            def maxima(t, s, i):
                t.need(dve, scores_full, 16, 2 * s + i + 1)
                t.need(dve, exp_done, 16, 2 * (s - 2) + i + 1)
                dve.tensor_reduce(negmax[:, s % 2, 2 * i:2 * i + 2], S[:, i, :].rearrange("p (j k) -> p j k", k=SEQ),
                                  AX.X, ALU.max, negate=True).then_inc(max_done, 1)

            def inverse(t, s, i):
                t.need(dve, exp_done, 16, 2 * s + i + 1)
                t.need(dve, norm_done, 16, 2 * (s - 2) + i + 1)
                dve.reciprocal(rinv[:, s % 2, 2 * i:2 * i + 2], rowsum[:, s % 2, 2 * i:2 * i + 2]).then_inc(rinv_done, 1)

            def probs(t, s, i):
                t.need(dve, pt_hi, 16, 2 * (s - 1) + i + 1)
                cols = slice(i * P, (i + 1) * P)
                minus(PT[1][:, (s - 1) % 2, :, cols], ET.rearrange("p (a q) -> p a q", q=P),
                      PT[0][:, (s - 1) % 2, :, cols]).then_inc(pt_lo, 1)

            def u_split(t, s):
                t.need(dve, u_hi, 8, s - 1)
                minus(Us[1][:, s % 2, :], U[:, 0:SEQ], Us[0][:, s % 2, :]).then_inc(u_lo, 1)

            def rope(t, dq):
                i = (dq % 8) % 2
                t.need(dve, qnope_done, 8, dq + 1)
                t.need(dve, qtok_done, 8, dq)
                r = Q.rearrange("p (h f) -> p h f", f=P)[:, :, KVL:P]
                dve.tensor_tensor(Qt[:, dq % 2, :, KVL:P], r,
                                  cosT[:, i, :].unsqueeze(1).broadcast_to([P, G4, ROPE]), ALU.mult)
                dve.tensor_tensor(rtmp[:].rearrange("p h (z e) -> p h z e", z=2),
                                  r.rearrange("p h (z e) -> p h z e", z=2)[:, :, ::-1, :],
                                  sinT[:, i, :].rearrange("p (z e) -> p z e", z=2).unsqueeze(1)
                                  .broadcast_to([P, G4, 2, ROPE // 2]), ALU.mult).then_inc(rope_mul, 1)

            def q_turned(t, dq):
                idx = dq % 8
                g, i = idx // 2, idx % 2
                t.need(dve, qT_hi, 8, dq + 1)
                heads, cols = slice(g * G4, (g + 1) * G4), slice(i * P, (i + 1) * P)
                minus(QT[1][:, heads, cols], QTp.rearrange("p (h q) -> p h q", q=P), QT[0][:, heads, cols]) \
                    .then_inc(qT_lo, 1)

            def spline_tap(t, m):
                row, w = rows_s[:, 2, :], ctrl_s[:, 2, m:m + 1]
                if m == 0:
                    t.need(dve, basis_loaded, 32, 32)
                    t.need(dve, rows_kept, 16, 0)
                    last = dve.tensor_scalar(row, basis_s[:, 0, :], w, None, ALU.mult)
                else:
                    t.need(dve, spd_chain, TAPS, m)
                    last = dve.scalar_tensor_tensor(row, basis_s[:, m, :], w, row, ALU.mult, ALU.add)
                last.then_inc(spd_chain, 1)

            def unit_lo(u):
                dve.wait_ge(sw_hi, u + 1)
                for src, (hi, lo) in unit_views(u):
                    last = minus(lo, src, hi)
                last.then_inc(sw_lo, 1)

            def entry(b, least):
                t = Step(b, least)
                for s in range(8 if least < NB else 3):
                    n = PAIRS * least + s
                    more = least + 2 < NB
                    if n < LAST:
                        maxima(t, s, 0)
                        maxima(t, s, 1)
                    if s == 0 and least + 1 < NB:
                        z_norm(t, 1, 1)
                    if s == 2 and more:
                        x_stats(t, 2)
                    if 1 <= n <= LAST:
                        probs(t, s, 0)
                    if s == 1 and least < NB:
                        spline_tap(t, 1)
                    if s == 4 and more:
                        x_norm(t, 2)
                    if n < LAST:
                        inverse(t, s, 0)
                    if n + LEAD - 2 < LAST:
                        q_turned(t, s + LEAD - 2)
                    if 2 <= n <= LAST + 1:
                        u_split(t, s)
                    if n < LAST:
                        inverse(t, s, 1)
                    if n + LEAD < LAST:
                        rope(t, s + LEAD)
                    if 1 <= n <= LAST:
                        probs(t, s, 1)
                    if s == 1 and least < NB:
                        t.need(dve, c_hi, 1, 1)
                        minus(cpad[1][:, :, KVL:2 * KVL],
                              zc[:, bass.ds(b * TT * KVL, TT * KVL)].rearrange("p (i f) -> p i f", f=KVL),
                              cpad[0][:, :, KVL:2 * KVL]).then_inc(c_lo, 1)
                    if s == 1 and least + 1 < NB:
                        split_k(t, 1)
                    if s == 3 and least + 1 < NB:
                        split_q(t, 1)
                    if s == 2 and least >= 1:
                        t.need(dve, o_added, 8, 0)
                        rows = X[:, bass.ds(b * TT * HID - TT * HID, TT * HID)]
                        dve.tensor_tensor(rows, O, rows, ALU.add).then_inc(x_added, 1)
                    if more:
                        if s == 3:
                            x_aggregate(t, 2, lambda: spline_tap(t, 3))
                        if s == 4:
                            split_x(t, 2)
                        if s in (5, 7):
                            z_stats(t, 2, (s - 5) // 2)
                        if s == 6:
                            z_norm(t, 2, 0)
                    if least < NB and (s in (0, 2, 4, 5) or s == 3 and not more):
                        spline_tap(t, s)
                    if least == NB - 1:
                        if s == 3:
                            mx_stats(Step(0, 0), 0, 0)
                            mx_aggregate(Step(0, 0), 0, None)
                        if s == 5:
                            mx_norm(Step(0, 0), 0, 0)
                    for u in units_at(least, s):
                        unit_lo(u)
                    if least == NB and s == 0:
                        split_mx(Step(0, 0), 0, 0)

            def mx_stats(t, gc, slot):
                for i in range(CT):
                    last = dve.bn_stats(mst6[:, i, :], X[:, bass.ds(slot * CT * HID + i * HID, HID)])
                last.then_inc(m_chain, 1)

            def mx_aggregate(t, gc, between):
                t.need(dve, m_chain, 2, 2 * gc + 1)
                if between is not None:
                    between()
                for i in range(CT):
                    last = dve.bn_aggr(mmv[:, i, :], mst6[:, i, :])
                last.then_inc(m_chain, 1)
                t.need(dve, m_chain, 2, 2 * gc + 2)
                t.need(dve, m_rstd, 1, gc)
                dve.tensor_scalar(mvare[:], mmv[:, :, 1], EPS, None, ALU.add).then_inc(m_var, 1)

            def mx_norm(t, gc, slot):
                t.need(dve, m_rstd, 1, gc + 1)
                t.need(dve, xt_full, KT, KT * gc)
                for i in range(CT):
                    last = dve.tensor_scalar(xnm[:, i, :], X[:, bass.ds(slot * CT * HID + i * HID, HID)],
                                             mmv[:, i, 0:1], mrstd[:, i:i + 1], ALU.subtract, ALU.mult)
                last.then_inc(m_xn, 1)

            def split_mx(t, gc, slot):
                for k in range(KT):
                    t.need(dve, xt_hi, KT, KT * gc + k + 1)
                    cols = bass.ds(slot * CHUNK, CHUNK)
                    minus(xT[1][:, k, cols], mXT[:, k, :], xT[0][:, k, cols]).then_inc(xt_lo, 1)

            def product(t, nf, m, j, scalar):
                t.need(dve, silu_done, nf, m + 1)
                t.need(dve, up_full, nf, m + 1)
                t.need(dve, h_lo, nf, m - 1)
                dve.scalar_tensor_tensor(htmp[:, j % 2, :], mUP[:, j % 2, :], scalar, silu[:, j % 2, :],
                                         ALU.mult, ALU.mult).then_inc(h_done, 1)

            def h_split(t, nf, m, j):
                t.need(dve, h_hi, nf, m)
                minus(H[1][:, (j - 1) % 4, :], htmp[:, (j - 1) % 2, :], H[0][:, (j - 1) % 4, :]).then_inc(h_lo, 1)

            def add_output(t, nf, m, gc, slot):
                t.need(dve, down_done, nf, m)
                rows = X[:, bass.ds(slot * CT * HID, CT * HID)]
                dve.tensor_tensor(rows, mO.rearrange("p a b -> p (a b)"), rows, ALU.add).then_inc(m_added, 1)

            def chunk(k, c, least):
                t = Step(c, least)
                if k == len(BLOCKS):
                    h_split(t, 0, M_ALL, 0)
                    add_output(t, 0, M_ALL, 0, NCH - 1)
                    return
                nf, c0, m0 = BLOCKS[k][3:]
                more = not (k == len(BLOCKS) - 1 and least == NCH - 1)
                slot = 0 if least == NCH - 1 else c + 1
                for j in range(nf):
                    m = m0 + j
                    scalar = d_s[:, j:j + 1] if k == 1 else 1.0
                    if j == 0 and more:
                        mx_stats(t, c0 + 1, slot)
                        mx_aggregate(t, c0 + 1, lambda: product(t, nf, m, j, scalar))
                    else:
                        product(t, nf, m, j, scalar)
                    if j > 0 or k > 0 or least > 0:
                        h_split(t, nf, m, j)
                    if j == 1 and (k > 0 or least > 0):
                        add_output(t, nf, m0, c0, NCH - 1 if least == 0 else c - 1)
                    if more:
                        if j == 1:
                            mx_norm(t, c0 + 1, slot)
                        if j == 2:
                            split_mx(t, c0 + 1, slot)
                    if k == 0 and least == NCH - 1:
                        if j == 5:
                            dve.wait_ge(cw_joined, KT)
                            dve.tensor_copy(Cz[0][:], winz_s[:])
                            dve.tensor_copy(Co[0][:], wout_s[:])
                            dve.tensor_copy(Cx[0][:], mXT).then_inc(cw_hi, 1)
                        if j == 6:
                            dve.wait_ge(cw_hi, 1)
                            minus(Cz[1][:], winz_s[:], Cz[0][:])
                            minus(Co[1][:], wout_s[:], Co[0][:])
                            minus(Cx[1][:], mXT, Cx[0][:]).then_inc(cw_lo, 1)

            t0 = Step(0, 0)
            dve.wait_ge(x0_loaded, 32)
            x_stats(t0, 0)
            x_aggregate(t0, 0, None)
            x_norm(t0, 0)
            dve.wait_ge(wa_hi, 1)
            minus(Wa[1][:], wa_s[:], Wa[0][:]).then_inc(wa_lo, 1)
            split_x(t0, 0)
            dve.wait_ge(first_loaded, 16 * 5)
            z_stats(t0, 0, 0)
            z_norm(t0, 0, 0)
            z_stats(t0, 0, 1)
            x_stats(t0, 1)
            x_aggregate(t0, 1, None)
            z_norm(t0, 0, 1)
            query_weights(0)
            split_k(t0, 0)
            x_norm(t0, 1)
            output_weights(0)
            split_q(t0, 0)
            output_weights(1)
            split_x(t0, 1)
            for q in range(LEAD):
                rope(t0, q)
                if q == 0:
                    query_weights(1)
                output_weights(q + 2)
                if q == 1:
                    z_stats(t0, 1, 0)
                if q == 2:
                    z_norm(t0, 1, 0)
                if q == 3:
                    z_stats(t0, 1, 1)
                if 1 <= q < LEAD - 1:
                    q_turned(t0, q - 1)
            output_weights(PAIRS - 2)
            output_weights(PAIRS - 1)
            dve.wait_ge(x_loaded, 16)
            entries(dve, entry)
            chunks(dve, chunk)

        @block.gpsimd
        def _(pool):
            def x_rsqrt(t, dj):
                t.need(pool, xvar_done, 1, dj + 1)
                t.need(pool, xn_done, 1, dj)
                pool.tensor_tensor(rstd[:], vare[:], half[:, 0:TT], ALU.pow).then_inc(xrstd_done, 1)

            def z_rsqrt(t, dj, i):
                t.need(pool, zvar_done, 2, 2 * dj + i + 1)
                pool.tensor_tensor(zrstd[:], zvare[:], half[:, 0:2], ALU.pow).then_inc(zrstd_done, 1)

            def z_affine(t, dj, i):
                t.need(pool, f_lo, 5, 5 * dj + 2 + i)
                pool.tensor_tensor(ztmp, ztmp, lnws[:], ALU.mult).then_inc(zscaled, 1)
                if i == 0:
                    t.need(pool, f_full, 5, 5 * dj)
                pool.tensor_tensor(zkn[:, i, KVL:P], krtmp, krtmp2, ALU.add)
                t.need(pool, zscaled, 2, 2 * dj + i + 1)
                pool.tensor_tensor(zkn[:, i, 0:KVL], ztmp[:, QL:], lnbs[:, QL:], ALU.add)
                pool.tensor_tensor(zc[:, bass.ds((t.b + dj) * TT * KVL + i * KVL, KVL)], ztmp[:, QL:], lnbs[:, QL:], ALU.add)
                pool.tensor_tensor(zq[:, i, :], ztmp[:, 0:QL], lnbs[:, 0:QL], ALU.add).then_inc(z_done, 1)

            def rope_sum(t, dq):
                t.need(pool, rope_mul, 8, dq + 1)
                dst = Qt[:, dq % 2, :, KVL:P]
                pool.tensor_tensor(dst, dst, rtmp[:], ALU.add).then_inc(qtok_done, 1)

            def normalise(t, s, i):
                t.need(pool, rinv_done, 16, 2 * s + i + 1)
                e = E[:, s % 2, 2 * i:2 * i + 2, :]
                pool.tensor_tensor(e, e, rinv[:, s % 2, 2 * i:2 * i + 2].unsqueeze(2).broadcast_to([P, 2, SEQ]),
                                   ALU.mult).then_inc(norm_done, 1)

            def spline_ops(t, first, count):
                for link in range(first, min(first + count, SP_LINKS)):
                    w, k = link % 2, link // 2
                    m = (k + 1) // 2
                    row, cp = rows_s[:, w, :], ctrl_s[:, w, m:m + 1].broadcast_to([P, HID])
                    if link == 0:
                        t.need(pool, basis_loaded, 32, 32)
                        t.need(pool, rows_kept, 16, 0)
                    t.need(pool, sp_chain, SP_LINKS, max(link - 1, 0))
                    if k == 0:
                        last = pool.tensor_tensor(row, basis_s[:, 0, :], cp, ALU.mult)
                    elif k % 2 == 1:
                        last = pool.tensor_tensor(sptmp[:, w, :], basis_s[:, m, :], cp, ALU.mult)
                    else:
                        last = pool.tensor_tensor(row, row, sptmp[:, w, :], ALU.add)
                    last.then_inc(sp_chain, 1)

            def entry(b, least):
                t = Step(b, least)
                for s in range(8 if least < NB else 0):
                    n = PAIRS * least + s
                    normalise(t, s, 0)
                    normalise(t, s, 1)
                    if n + LEAD < LAST:
                        rope_sum(t, s + LEAD)
                    if s == 0 and least + 1 < NB:
                        z_affine(t, 1, 1)
                    if least + 2 < NB:
                        if s == 3:
                            x_rsqrt(t, 2)
                        if s in (5, 7):
                            z_rsqrt(t, 2, (s - 5) // 2)
                        if s == 6:
                            z_affine(t, 2, 0)
                    if least == NB - 1 and s == 3:
                        m_rsqrt(Step(0, 0), 0)
                    spline_ops(t, 3 * s, 3)

            def m_rsqrt(t, gc):
                t.need(pool, m_var, 1, gc + 1)
                t.need(pool, m_xn, 1, gc)
                pool.tensor_tensor(mrstd[:], mvare[:], half[:, 0:CT], ALU.pow).then_inc(m_rstd, 1)

            t0 = Step(0, 0)
            pool.memset(half[:], -0.5)
            pool.memset(cpad[0][:].bitcast(F32), 0.0)
            pool.memset(cpad[1][:].bitcast(F32), 0.0).then_inc(zeroed, 1)
            pool.wait_ge(zeroed, 1)
            x_rsqrt(t0, 0)
            z_rsqrt(t0, 0, 0)
            z_affine(t0, 0, 0)
            z_rsqrt(t0, 0, 1)
            x_rsqrt(t0, 1)
            z_affine(t0, 0, 1)
            for q in range(LEAD):
                rope_sum(t0, q)
                if q == 1:
                    z_rsqrt(t0, 1, 0)
                if q == 2:
                    z_affine(t0, 1, 0)
            z_rsqrt(t0, 1, 1)
            entries(pool, entry)
            for gc in range(1, NCH * len(BLOCKS)):
                m_rsqrt(t0, gc)

        @block.sync
        def _(sp):
            HALF_X = 2 * TT
            xd = x.rearrange("t p d -> p t d")
            xs = X[:, :].rearrange("p (t d) -> p t d", d=HID)
            sp.dma_start(xs[:, 0:TT, :], xd[:, 0:TT, :]).then_inc(x0_loaded, 16)
            sp.dma_start(ident[:], ident_in).then_inc(x0_loaded, 16)
            sp.dma_start(xs[:, TT:HALF_X, :], xd[:, TT:HALF_X, :]).then_inc(first_loaded, 16)
            for dst, src in ((lnws, lnw), (lnbs, lnb), (cosT, cos), (sinT, sin)):
                sp.dma_start(dst[:], src).then_inc(first_loaded, 16)
            for dst, src in ((wv_s, wv), (wo_s, wo)):
                sp.dma_start(dst[:], src).then_inc(o_loaded, 16)
            sp.dma_start(xs[:, HALF_X:, :], xd[:, HALF_X:, :]).then_inc(x_loaded, 16)
            for b in range(NB):
                if b == 1:
                    sp.wait_ge(bo_lo, PAIRS)
                if b >= 1:
                    sp.wait_ge(sp_chain, b * SP_LINKS)
                    sp.wait_ge(spd_chain, b * TAPS)
                    sp.dma_start(Wn[:, :, b - 1, :], rows_s[:]).then_inc(rows_kept, 16)
                sp.dma_start(basis_s[:].rearrange("p m c -> p (m c)"), basis[b]).then_inc(basis_loaded, 16)
                sp.dma_start(ctrl_s[:], ctrl[b]).then_inc(basis_loaded, 16)
            sp.wait_ge(sp_chain, NB * SP_LINKS)
            sp.wait_ge(spd_chain, NB * TAPS)
            sp.dma_start(Wn[:, :, NB - 1, :], rows_s[:]).then_inc(rows_kept, 16)
            sp.wait_ge(rows_kept, 16 * NB)
            sp.wait_ge(x_added, NB)
            for dst, src in ((wconv_s, w_conv), (winx_s, w_inx), (winz_s, w_inz), (wout_s, w_out), (d_s, d_in)):
                sp.dma_start(dst[:], src).then_inc(cw_loaded, 16)
            for c in range(NCH):
                sp.wait_ge(m_added, 2 * NCH + c + 1)
                sp.dma_start(out[c * CT:(c + 1) * CT].rearrange("t p d -> p t d"),
                             xs[:, c * CT:(c + 1) * CT, :]).then_inc(stored, 16)
            sp.wait_ge(stored, 16 * NCH)


def spline_basis():
    n = ROWS * HID
    t = np.linspace(0.0, CTRL - 1.0, n, dtype=np.float64)
    i = np.clip(np.floor(t).astype(np.int64), 0, CTRL - 2)
    f = (t - i).astype(np.float32).astype(np.float64)
    first = np.clip(i.reshape(ROWS, HID)[:, 0] - 1, 0, CTRL - TAPS)
    f2, f3 = f * f, f * f * f
    parts = [0.5 * (-f + 2 * f2 - f3), 0.5 * (2 - 5 * f2 + 3 * f3), 0.5 * (f + 4 * f2 - 3 * f3), 0.5 * (f3 - f2)]
    basis = np.zeros((ROWS, TAPS, HID))
    row, col = np.divmod(np.arange(n), HID)
    for k, part in enumerate(parts):
        tap = np.clip(i + k - 1, 0, CTRL - 1) - first[row]
        np.add.at(basis, (row, tap, col), part)
    return basis.astype(np.float32).reshape(RT, P, TAPS * HID), first


def rope_tables():
    inv = 1.0 / 10000.0 ** (np.arange(0, ROPE, 2, dtype=np.float32) / ROPE)
    a = np.outer(np.arange(SEQ, dtype=np.float32), inv)
    cos = np.concatenate([np.cos(a), np.cos(a)], 1).astype(np.float32)
    sin = np.concatenate([-np.sin(a), np.sin(a)], 1).astype(np.float32)
    return [t.reshape(TT, P, ROPE).transpose(1, 0, 2) for t in (cos, sin)]


def kernel(**inputs):
    import concourse.bacc as bacc
    from concourse.bass_utils import run_bass_kernel_spmd

    a = {k: np.asarray(w) for k, w in inputs.items()}
    A, C, FN = "L0_attn_a_", "L0_attn_b_", "L0_ffn_"
    kvb = a[A + "kv_b_w"].reshape(NH, NOPE + DV, KVL)
    qr = a[A + "q_rope_w"].T
    basis, first = spline_basis()
    cos, sin = rope_tables()
    win = first[:, None] + np.arange(TAPS)
    ctrl = np.stack([a[FN + n][win].reshape(RT, P, TAPS) for n in ("gate_cp", "up_cp", "down_cp")], 2)
    w_in = a[C + "W_in"]
    wide = lambda w: np.broadcast_to(w, (P, w.shape[0]))
    arrays = {
        "x": a[A + "hidden_states"].reshape(NTILE, P, HID),
        "wa": np.concatenate([a[A + "q_a_w"], a[A + "kv_a_w"]], 0).T.reshape(KT, P, QL + P).transpose(1, 0, 2),
        "lnw": wide(np.concatenate([a[A + "q_a_ln_w"], a[A + "kv_a_ln_w"]])),
        "lnb": wide(np.concatenate([a[A + "q_a_ln_b"], a[A + "kv_a_ln_b"]])),
        "wqb": a[A + "q_b_w"].reshape(NH, NOPE, QL).transpose(1, 0, 2),
        "wk": kvb[:, :NOPE].transpose(1, 0, 2),
        "wv": kvb[:, NOPE:].transpose(1, 0, 2),
        "wqr1": qr[:P].reshape(P, NH, ROPE),
        "wqr2": qr[P:].reshape(QK2, NH, ROPE),
        "wo": a[A + "o_w"].T.reshape(NH, DV, HID).transpose(1, 0, 2),
        "cos": cos, "sin": sin, "ident_in": np.eye(P, dtype=np.float32),
        "basis": basis, "ctrl": ctrl,
        "w_inx": w_in[:CONV].reshape(4, P, HID).transpose(1, 0, 2),
        "w_inz": w_in[CONV:].T.reshape(KT, P, CONV).transpose(1, 0, 2),
        "w_conv": a[C + "conv_w"].T.reshape(4, P, CONV).transpose(1, 0, 2),
        "w_out": a[C + "W_out"].T.reshape(4, P, HID).transpose(1, 0, 2),
        "d_in": a[C + "D"].reshape(4, P).T,
    }
    nc = bacc.Bacc("TRN2", target_bir_lowering=False, num_devices=1)
    feeds, aps = {}, {}
    for name, w in arrays.items():
        w = np.ascontiguousarray(w)
        feeds["in_" + name] = w
        aps[name] = nc.dram_tensor("in_" + name, w.shape, mybir.dt.from_np(w.dtype), kind="ExternalInput").ap()
    aps["out"] = nc.dram_tensor("out_x", (NTILE, P, HID), F32, kind="ExternalOutput").ap()
    build(nc, **aps)
    r = run_bass_kernel_spmd(nc, [feeds], core_ids=[0])
    return r.results[0]["out_x"].reshape(NB, SEQ, HID)
```

```python
from contextlib import ExitStack

import numpy as np
import concourse.bass as bass
from concourse import mybir

F32 = mybir.dt.float32
F32R = mybir.dt.float32r
ALU = mybir.AluOpType
ACT = mybir.ActivationFunctionType
AX = mybir.AxisListType

P = 128
NB, SEQ, HID = 8, 256, 256
NH, NOPE, ROPE, DV = 16, 128, 64, 128
QL, KVL = 192, 64
QK2 = QL - P
FFN, CONV = 1024, 512
CTRL = 2033
TAPS = 6
EPS = 1e-5
SCALE = 1.0 / float(np.sqrt(NOPE + ROPE))
KT = HID // P
TT = SEQ // P
NTILE = NB * TT
PAIRS = NH // 2
ROWS = FFN * HID // HID
RT = ROWS // P
CHUNK = 512
NCH = NB * SEQ // CHUNK
CT = CHUNK // P
G4 = 4
HG = 8
LEAD = 4
LAST = NB * PAIRS


class Step:

    def __init__(self, b, least):
        self.b, self.least = b, least

    def need(self, eng, sem, per, const):
        if per * self.least + const > 0:
            eng.wait_ge(sem, self.b * per + const)

    def has(self, per, const):
        return per * self.least + const >= 0


def f32r_matmul3(pe, out, hi, lo, whi, wlo, first, last):
    pe.matmul(out, lhsT=hi, rhs=whi, start=first, stop=False, skip_group_check=True)
    pe.matmul(out, lhsT=hi, rhs=wlo, start=False, stop=False, skip_group_check=True)
    return pe.matmul(out, lhsT=lo, rhs=whi, start=False, stop=last, skip_group_check=True)


def build(nc, x, wa, lnw, lnb, wqb, wk, wv, wqr1, wqr2, wo, cos, sin, ident_in, basis, ctrl,
          w_inx, w_inz, w_conv, w_out, d_in, out):
    top = ExitStack()
    with top:
        def sem(name):
            return top.enter_context(nc.semaphore(name))

        def one(stack, name, shape, dt=F32):
            return stack.enter_context(nc.sbuf_tensor(name, shape, dt))

        def pair(stack, name, shape):
            return [one(stack, f"{name}_{p}", shape, F32R) for p in ("hi", "lo")]

        ps = top.enter_context(nc.psum_tensor("ps", [P, 8, 512], F32))

        X = one(top, "X", [P, NTILE * HID])
        ident = one(top, "ident", [P, P])
        half = one(top, "half", [P, CT])
        scratch = one(top, "scratch", [P, CT])
        early = ExitStack()
        wo_s = one(early, "wo_s", [P, NH, HID])
        wv_s = one(early, "wv_s", [P, NH, KVL])
        wk_s = one(early, "wk_s", [P, NH, KVL])
        early.close()
        Wn = one(top, "Wn", [P, 3, RT, HID])

        attn = ExitStack()
        Wq1 = pair(attn, "Wq1", [P, NH, P])
        Wq2s = one(attn, "Wq2s", [P, NH, P], F32R)
        Wq2l = one(attn, "Wq2l", [QK2, NH, P], F32R)
        QT = pair(attn, "QT", [P, NH, SEQ])
        kT = pair(attn, "kT", [P, NB * SEQ])
        Bo = pair(attn, "Bo", [P, PAIRS, HID])
        Wa = pair(attn, "Wa", [P, KT, QL + P])
        lnws = one(attn, "lnws", [P, QL + KVL])
        lnbs = one(attn, "lnbs", [P, QL + KVL])
        cosT = one(attn, "cosT", [P, TT, ROPE])
        sinT = one(attn, "sinT", [P, TT, ROPE])
        cs = one(attn, "cs", [P, TT, 2 * KVL], F32R)
        zc = one(attn, "zc", [P, NTILE * KVL])
        zkn = one(attn, "zkn", [P, TT, P])
        zq = one(attn, "zq", [P, TT, QL])
        xn = one(attn, "xn", [P, TT, HID])
        xaT = pair(attn, "xaT", [P, KT, SEQ])
        ql1 = pair(attn, "ql1", [P, SEQ])
        ql2 = one(attn, "ql2", [P, SEQ], F32R)
        raw = ExitStack()
        wqb_s = one(raw, "wqb_s", [P, NH, QL])
        wqr1_s = one(raw, "wqr1_s", [P, NH, ROPE])
        wqr2_s = one(raw, "wqr2_s", [QK2, NH, ROPE])
        wa_s = one(raw, "wa_s", [P, KT, QL + P])
        raw.close()
        E = one(attn, "E", [P, 2, 4, SEQ])
        PT = pair(attn, "PT", [P, 2, 4, SEQ])
        Qt = one(attn, "Qt", [P, 2, G4, P])
        rtmp = one(attn, "rtmp", [P, G4, ROPE])
        usum = one(attn, "usum", [P, SEQ])
        Us = pair(attn, "Us", [P, 2, SEQ])
        basis_s = one(attn, "basis_s", [P, TAPS, HID])
        ctrl_s = one(attn, "ctrl_s", [P, 3, TAPS])
        rows_s = one(attn, "rows_s", [P, 3, HID])
        sprod = one(attn, "sprod", [P, 3, HID])
        negmax = one(attn, "negmax", [P, 2, 4])
        rowsum = one(attn, "rowsum", [P, 2, 4])
        rinv = one(attn, "rinv", [P, 2, 4])
        st6, mv = one(attn, "st6", [P, TT, 6]), one(attn, "mv", [P, TT, 2])
        vare, rstd = one(attn, "vare", [P, TT]), one(attn, "rstd", [P, TT])
        zst6, zmv = one(attn, "zst6", [P, 2, 6]), one(attn, "zmv", [P, 2, 2])
        zvare, zrstd = one(attn, "zvare", [P, 2]), one(attn, "zrstd", [P, 2])
        ztmp, krtmp, krtmp2 = xn[:, 0, :], xn[:, 1, 0:ROPE], xn[:, 1, ROPE:2 * ROPE]
        attn.close()

        Wg = pair(top, "Wg", [P, KT, FFN])
        Wu = pair(top, "Wu", [P, KT, FFN])
        Wd = pair(top, "Wd", [P, FFN // P, HID])
        xT = pair(top, "xT", [P, KT, NB * SEQ])
        wconv_s = one(top, "wconv_s", [P, 4, CONV])
        winx_s = one(top, "winx_s", [P, 4, HID])
        winz_s = one(top, "winz_s", [P, KT, CONV])
        wout_s = one(top, "wout_s", [P, CONV // P, HID])
        d_s = one(top, "d_s", [P, CONV // P])
        htmp = one(top, "htmp", [P, 2, CHUNK])
        silu = one(top, "silu", [P, 2, CHUNK])
        mst6, mmv = one(top, "mst6", [P, CT, 6]), one(top, "mmv", [P, CT, 2])
        mvare, mrstd = one(top, "mvare", [P, CT]), one(top, "mrstd", [P, CT])
        xnm = one(top, "xnm", [P, CT, HID])
        Co = pair(top, "Co", [P, CONV // P, HID])
        H = pair(top, "H", [P, 4, CHUNK])
        Cz = pair(top, "Cz", [P, KT, CONV])
        Cx = pair(top, "Cx", [P, KT, CONV])

        S = ps[:, 0:2, :]
        ET, U, O, Q, QTp, F = (ps[:, 2 + i, :] for i in range(6))
        mXT, mG, mUP, mO = (ps[:, 2 * i:2 * i + 2, :] for i in range(4))

        x0_loaded, x1_loaded, x_loaded, ident_loaded, half_set = (sem(n) for n in (
            "x0_loaded", "x1_loaded", "x_loaded", "ident_loaded", "half_set"))
        wa_loaded, first_loaded, qa_loaded, qb_loaded, r_loaded, o_loaded = (sem(n) for n in (
            "wa_loaded", "first_loaded", "qa_loaded", "qb_loaded", "r_loaded", "o_loaded"))
        zeroed, wa_hi, wa_lo = sem("zeroed"), sem("wa_hi"), sem("wa_lo")
        wqr_hi, join_q, wq_hi, wq_lo = sem("wqr_hi"), sem("join_q"), sem("wq_hi"), sem("wq_lo")
        join_o, bo_hi, bo_lo = sem("join_o"), sem("bo_hi"), sem("bo_lo")
        scores_full, et_full, u_full, o_added = sem("scores_full"), sem("et_full"), sem("u_full"), sem("o_added")
        q_full, qt_full, f_full = sem("q_full"), sem("qt_full"), sem("f_full")
        max_done, exp_done, rinv_done, norm_done = (sem(n) for n in (
            "max_done", "exp_done", "rinv_done", "norm_done"))
        pt_hi, pt_lo = sem("pt_hi"), sem("pt_lo")
        u_copied, u_summed, u_hi, u_lo = sem("u_copied"), sem("u_summed"), sem("u_hi"), sem("u_lo")
        qnope_done, rope_mul, qtok_done = sem("qnope_done"), sem("rope_mul"), sem("qtok_done")
        qT_hi, qT_lo = sem("qT_hi"), sem("qT_lo")
        f_hi, f_lo = sem("f_hi"), sem("f_lo")
        fe_chain = sem("fe_chain")
        xvar_done, xrstd_done, xn_done = sem("xvar_done"), sem("xrstd_done"), sem("xn_done")
        zvar_done, zrstd_done = sem("zvar_done"), sem("zrstd_done")
        zscaled, z_done = sem("zscaled"), sem("z_done")
        c_hi, c_lo, x_added = sem("c_hi"), sem("c_lo"), sem("x_added")
        basis_loaded, rows_kept = sem("basis_loaded"), sem("rows_kept")
        tap_mul, tap_add = sem("tap_mul"), sem("tap_add")
        sw_turned, sw_hi, sw_lo = sem("sw_turned"), sem("sw_hi"), sem("sw_lo")
        cw_loaded, cw_joined, cw_hi, cw_lo = sem("cw_loaded"), sem("cw_joined"), sem("cw_hi"), sem("cw_lo")
        gate_full, up_full, down_done = sem("gate_full"), sem("up_full"), sem("down_done")
        silu_done, h_done, h_hi, h_lo = sem("silu_done"), sem("h_done"), sem("h_hi"), sem("h_lo")
        m_chain, m_var, m_rstd, m_xn = sem("m_chain"), sem("m_var"), sem("m_rstd"), sem("m_xn")
        xt_full, xt_hi, xt_lo = sem("xt_full"), sem("xt_hi"), sem("xt_lo")
        m_added, stored = sem("m_added"), sem("stored")

        FE_X, FE_Z = 2, 2
        FE_LINKS = FE_X + TT * FE_Z

        def entries(eng, body):
            body(0, 0)
            with eng.Fori(1, NB - 2) as b:
                body(b, 1)
            body(NB - 2, NB - 2)
            body(NB - 1, NB - 1)
            body(NB, NB)

        BLOCKS = [(Wg, Wu, Wd, FFN // P, 0, 0), (Cz, Cx, Co, CONV // P, NCH, NCH * FFN // P),
                  (Wg, Wu, Wd, FFN // P, 2 * NCH, NCH * (FFN + CONV) // P)]
        M_ALL = NCH * (2 * FFN + CONV) // P

        def chunks(eng, body):
            for k in range(len(BLOCKS)):
                body(k, 0, 0)
                with eng.Fori(1, NCH - 1) as c:
                    body(k, c, 1)
                body(k, NCH - 1, NCH - 1)
            body(len(BLOCKS), 0, 0)

        UNITS = [(0, 0), (1, 0), (0, 1), (1, 1), (0, 2), (1, 2), (2, 0), (2, 1), (2, 2), (0, 3), (1, 3), (2, 3)]
        SWB = [7, 5, 6]

        def unit_views(u):
            w, r = UNITS[u]
            bank = ps[:, SWB[u % 3], :]
            if w < 2:
                dst = (Wg, Wu)[w]
                return [(bank.rearrange("p (k c) -> p k c", k=KT), [d[:, :, r * 2 * P:(r + 1) * 2 * P] for d in dst])]
            return [(bank[:, k * 2 * P:(k + 1) * 2 * P].rearrange("p (o a) -> p a o", a=4),
                     [d[:].rearrange("p (a k) o -> p a k o", k=KT)[:, :, k, r * 64:(r + 1) * 64] for d in Wd])
                    for k in range(KT)]

        def units_at(least, s):
            if least == NB - 1:
                return {4: [0], 5: [1], 6: [2, 3], 7: [4, 5]}.get(s, [])
            return {0: [6], 1: [7, 8, 9], 2: [10, 11]}[s] if least == NB else []

        OB = [4, 6, 0, 1, 2, 3, 4, 0]

        block = top.enter_context(nc.Block())

        @block.tensor
        def _(pe):
            def turn(dst, src):
                return pe.matmul(dst, lhsT=src, rhs=ident[:], is_transpose=True, start=True, stop=True)

            def keep_warm(count):
                for _ in range(count):
                    pe.matmul(O[:, 0:TT * P], lhsT=cs[:, 0, :], rhs=cs[:], start=True, stop=True)

            def join_query(g, first, count):
                for i in range(first, first + count):
                    h = g * HG + i
                    cols = slice(i * KVL, (i + 1) * KVL)
                    pe.matmul(ps[:, 2 * g, cols], lhsT=wqb_s[:, h, 0:P], rhs=wk_s[:, h, :], start=True, stop=True)
                    last = pe.matmul(ps[0:QK2, 2 * g + 1, cols], lhsT=wqb_s[:, h, P:QL], rhs=wk_s[:, h, :],
                                     start=True, stop=True)
                if first + count == HG:
                    last.then_inc(join_q, 1)

            def join_output(s):
                if s in (2, 4):
                    pe.wait_ge(wq_lo, s // 2)
                if s >= 6:
                    pe.wait_ge(bo_lo, 1 if s == 6 else 3)
                for j in range(2):
                    last = pe.matmul(ps[0:KVL, OB[s], j * HID:(j + 1) * HID], lhsT=wv_s[:, 2 * s + j, :],
                                     rhs=wo_s[:, 2 * s + j, :], start=True, stop=True)
                last.then_inc(join_o, 1)

            def turn_x(t, dj):
                t.need(pe, xn_done, 1, dj + 1)
                t.need(pe, f_lo, 5, 5 * dj)
                for k in range(KT):
                    for i in range(TT):
                        c = (k * TT + i) * P
                        last = turn(F[:, c:c + P], xn[:, i, k * P:(k + 1) * P])
                last.then_inc(f_full, 1)

            def latents(t, dj, i):
                t.need(pe, f_lo, 5, 5 * dj + 1 + i)
                rows = slice(i * P, (i + 1) * P)
                for k in range(KT):
                    last = f32r_matmul3(pe, F[:, 0:QL + P], xaT[0][:, k, rows], xaT[1][:, k, rows],
                                        Wa[0][:, k, :], Wa[1][:, k, :], k == 0, k == KT - 1)
                last.then_inc(f_full, 1)

            def turn_k(t, dj):
                t.need(pe, z_done, 2, 2 * dj + 2)
                t.need(pe, f_lo, 5, 5 * dj + 3)
                for i in range(TT):
                    last = turn(F[:, i * P:(i + 1) * P], zkn[:, i, :])
                last.then_inc(f_full, 1)

            def turn_q(t, dj):
                t.need(pe, z_done, 2, 2 * dj + 2)
                t.need(pe, f_lo, 5, 5 * dj + 4)
                for i in range(TT):
                    turn(F[:, i * P:(i + 1) * P], zq[:, i, 0:P])
                    last = turn(F[0:QK2, SEQ + i * P:SEQ + (i + 1) * P], zq[:, i, P:QL])
                last.then_inc(f_full, 1)

            def query(t, dq):
                idx = dq % 8
                i, g = idx % 2, idx // 2
                if idx == 0:
                    t.need(pe, f_lo, 5, 5 * (dq // 8) + 5)
                t.need(pe, rope_mul, 8, dq)
                rows, heads = slice(i * P, (i + 1) * P), slice(g * G4, (g + 1) * G4)
                w1h, w1l, w2s, w2l = (a[:, heads, :].rearrange("p h f -> p (h f)") for a in (*Wq1, Wq2s, Wq2l))
                f32r_matmul3(pe, Q, ql1[0][:, rows], ql1[1][:, rows], w1h, w1l, True, False)
                pe.matmul(Q, lhsT=ql2[:, rows], rhs=w2s, start=False, stop=False, skip_group_check=True)
                pe.matmul(Q, lhsT=ql2[0:QK2, rows], rhs=w2l, start=False, stop=True,
                          skip_group_check=True).then_inc(q_full, 1)

            def turn_query(t, dq):
                t.need(pe, qtok_done, 8, dq + 1)
                t.need(pe, qT_lo, 8, dq)
                for j in range(G4):
                    last = turn(QTp[:, j * P:(j + 1) * P], Qt[:, dq % 2, j, :])
                last.then_inc(qt_full, 1)

            def scores(t, s, i):
                t.need(pe, qT_lo, 8, 2 * (s // 2) + i + 1)
                if s == 0 and i == 0:
                    t.need(pe, f_lo, 5, 4)
                t.need(pe, exp_done, 16, 2 * s + i - 1)
                rows, keys = slice(i * P, (i + 1) * P), bass.ds(t.b * SEQ, SEQ)
                for j in range(2):
                    last = f32r_matmul3(pe, S[:, i, j * SEQ:(j + 1) * SEQ], QT[0][:, 2 * s + j, rows],
                                        QT[1][:, 2 * s + j, rows], kT[0][:, keys], kT[1][:, keys], True, True)
                last.then_inc(scores_full, 1)

            def turn_probs(t, s, i):
                t.need(pe, norm_done, 16, 2 * (s - 1) + i + 1)
                t.need(pe, pt_lo, 16, 2 * (s - 1) + i)
                for k in range(TT):
                    for j in range(2):
                        c = (k * 2 + j) * P
                        last = turn(ET[:, c:c + P], E[:, (s - 1) % 2, 2 * i + j, k * P:(k + 1) * P])
                last.then_inc(et_full, 1)

            def values(t, s):
                t.need(pe, pt_lo, 16, 2 * (s - 2) + 2)
                t.need(pe, u_summed, 8, s - 2)
                if s == 2:
                    t.need(pe, c_lo, 1, 1)
                for j in range(2):
                    cols = slice(j * SEQ, (j + 1) * SEQ)
                    for k in range(TT):
                        pe.matmul(U[:, cols], lhsT=cs[:, k, :], rhs=PT[0][:, s % 2, 2 * k + j, :],
                                  start=k == 0, stop=False, skip_group_check=True)
                        last = pe.matmul(U[0:KVL, cols], lhsT=cs[:, k, 0:KVL], rhs=PT[1][:, s % 2, 2 * k + j, :],
                                         start=False, stop=k == TT - 1, skip_group_check=True)
                last.then_inc(u_full, 1)

            def output(t, s):
                p = (s - 3) % PAIRS
                t.need(pe, u_lo, 8, s - 2)
                if p == 0:
                    t.need(pe, x_added, 1, 0)
                for i in range(TT):
                    rows = slice(i * P, (i + 1) * P)
                    last = f32r_matmul3(pe, O[:, i * HID:(i + 1) * HID], Us[0][:, (s - 3) % 2, rows],
                                        Us[1][:, (s - 3) % 2, rows], Bo[0][:, p, :], Bo[1][:, p, :],
                                        p == 0 and i == 0, p == PAIRS - 1)
                last.then_inc(o_added, 1)

            def turn_unit(u):
                w, r = UNITS[u]
                pe.wait_ge(rows_kept, 16 * (2 * r + 2))
                if u == 0:
                    pe.wait_ge(rope_mul, LAST)
                if u == 2:
                    pe.wait_ge(qT_lo, LAST)
                if u >= 3:
                    pe.wait_ge(sw_lo, u - 2)
                for k in range(KT):
                    for i in range(2):
                        c = (2 * k + i) * P
                        last = turn(ps[:, SWB[u % 3], c:c + P], Wn[:, w, 2 * r + i, k * P:(k + 1) * P])
                last.then_inc(sw_turned, 1)

            def entry(b, least):
                t = Step(b, least)
                for s in range(8 if least < NB else 3):
                    n = PAIRS * least + s
                    if s == 3 and least + 1 < NB:
                        turn_k(t, 1)
                    if n < LAST:
                        scores(t, s, 0)
                        scores(t, s, 1)
                    if s == 6 and least + 2 < NB:
                        latents(t, 2, 0)
                    if 1 <= n <= LAST:
                        turn_probs(t, s, 0)
                    if 2 <= n <= LAST + 1:
                        values(t, s)
                    if n + LEAD < LAST:
                        query(t, s + LEAD)
                    if 3 <= n <= LAST + 2:
                        output(t, s)
                    if 1 <= n <= LAST:
                        turn_probs(t, s, 1)
                    if s == 3 and least + 1 < NB:
                        turn_q(t, 1)
                    if s == 4 and least + 2 < NB:
                        turn_x(t, 2)
                    if n + LEAD - 1 < LAST:
                        turn_query(t, s + LEAD - 1)
                    if s == 7 and least + 2 < NB:
                        latents(t, 2, 1)
                    for u in units_at(least, s):
                        turn_unit(u)
                    if least == NB and s == 0:
                        pe.wait_ge(exp_done, 2 * LAST)
                        turn_mx(Step(0, 0), 0)

            def turn_mx(t, gc):
                t.need(pe, m_xn, 1, gc + 1)
                t.need(pe, xt_lo, KT, KT * gc)
                for k in range(KT):
                    for i in range(CT):
                        last = turn(mXT[:, k, i * P:(i + 1) * P], xnm[:, i, k * P:(k + 1) * P])
                    last.then_inc(xt_full, 1)

            def inner(t, j, W, bank, full):
                cols = bass.ds(t.b * CHUNK, CHUNK)
                for k in range(KT):
                    last = f32r_matmul3(pe, bank, W[0][:, k, j * P:(j + 1) * P], W[1][:, k, j * P:(j + 1) * P],
                                        xT[0][:, k, cols], xT[1][:, k, cols], k == 0, k == KT - 1)
                last.then_inc(full, 1)

            def down(t, nf, m, j, f, W, closes, before=None):
                t.need(pe, h_lo, nf, m - 1)
                if before is not None:
                    t.need(pe, m_added, 1, before)
                for i in range(CT):
                    rows = slice(i * P, (i + 1) * P)
                    last = f32r_matmul3(pe, mO[:, i // 2, (i % 2) * HID:(i % 2 + 1) * HID],
                                        H[0][:, (j - 2) % 4, rows], H[1][:, (j - 2) % 4, rows],
                                        W[0][:, f, :], W[1][:, f, :],
                                        f == 0 and i % 2 == 0, closes)
                last.then_inc(down_done, 1)

            def chunk(k, c, least):
                t = Step(c, least)
                if k == len(BLOCKS):
                    _, _, pd, pnf, pc0, pm0 = BLOCKS[k - 1]
                    for j in range(2):
                        down(t, 0, M_ALL + j, j, pnf - 2 + j, pd, j == 1)
                    return
                Wa_, Wb_, Wc_, nf, c0, m0 = BLOCKS[k]
                for j in range(nf):
                    m = m0 + j
                    if j == 0:
                        t.need(pe, xt_lo, KT, KT * (c0 + 1))
                    if k == 1 and least == 0 and j == 0:
                        pe.wait_ge(cw_lo, 1)
                    if k == 0 and least == 0 and j < 3:
                        pe.wait_ge(sw_lo, (2, 11, 12)[j])
                    if k == 0 and least == 0 and j == 0:
                        pe.wait_ge(u_summed, LAST)
                    t.need(pe, silu_done, nf, m - 1)
                    inner(t, j, Wa_, mG[:, j % 2, :], gate_full)
                    if k == 0 and least == 0 and j == 0:
                        pe.wait_ge(x_added, NB)
                    t.need(pe, h_done, nf, m - 1)
                    inner(t, j, Wb_, mUP[:, j % 2, :], up_full)
                    if j >= 2:
                        down(t, nf, m, j, j - 2, Wc_, False, c0 if j == 2 else None)
                    elif least >= 1:
                        down(t, nf, m, j, nf - 2 + j, Wc_, j == 1)
                    elif k >= 1:
                        down(t, nf, m, j, BLOCKS[k - 1][3] - 2 + j, BLOCKS[k - 1][2], j == 1)
                    if j == 2 and not (k == len(BLOCKS) - 1 and least == NCH - 1):
                        turn_mx(t, c0 + 1)
                    if k == 0 and least == NCH - 1 and j == 4:
                        join_conv()

            def join_conv():
                pe.wait_ge(cw_loaded, 16 * 5)
                pe.wait_ge(xt_lo, KT * (NCH + 1))
                for m in range(KT):
                    for k in range(4):
                        last = pe.matmul(mXT[:, m, :], lhsT=winx_s[:, k, m * P:(m + 1) * P], rhs=wconv_s[:, k, :],
                                         start=k == 0, stop=k == 3)
                    last.then_inc(cw_joined, 1)

            t0 = Step(0, 0)
            pe.wait_ge(zeroed, 1)
            keep_warm(24)
            pe.wait_ge(ident_loaded, 16)
            turn_x(t0, 0)
            pe.wait_ge(qa_loaded, 32)
            join_query(0, 0, 2)
            pe.wait_ge(wa_lo, 1)
            latents(t0, 0, 0)
            join_query(0, 2, 5)
            latents(t0, 0, 1)
            join_query(0, 7, 1)
            pe.wait_ge(qb_loaded, 32)
            join_query(1, 0, HG)
            keep_warm(16)
            turn_k(t0, 0)
            turn_q(t0, 0)
            pe.wait_ge(o_loaded, 32)
            join_output(0)
            turn_x(t0, 1)
            join_output(1)
            join_output(2)
            for q in range(LEAD):
                query(t0, q)
                if q == 1:
                    pe.wait_ge(bo_lo, 2)
                for s in ([3], [4], [5, 6], [7])[q]:
                    join_output(s)
                if q in (1, 3):
                    latents(t0, 1, q // 2)
                if q >= 1:
                    turn_query(t0, q - 1)
            pe.wait_ge(bo_lo, PAIRS)
            entries(pe, entry)
            chunks(pe, chunk)

        @block.scalar
        def _(act):
            def copy(dst, src, **kw):
                return act.activation(dst, src, ACT.Copy, **kw)

            def split_x(t, dj):
                t.need(act, f_full, 5, 5 * dj + 1)
                copy(xaT[0][:].rearrange("p k c -> p (k c)"), F).then_inc(f_hi, 1)

            def split_k(t, dj):
                t.need(act, f_full, 5, 5 * dj + 4)
                copy(kT[0][:, bass.ds((t.b + dj) * SEQ, SEQ)], F[:, 0:SEQ]).then_inc(f_hi, 1)

            def split_q(t, dj):
                t.need(act, f_full, 5, 5 * dj + 5)
                if dj:
                    t.need(act, q_full, 8, 8)
                copy(ql1[0][:], F[:, 0:SEQ])
                copy(ql2[0:QK2, :], F[0:QK2, SEQ:2 * SEQ]).then_inc(f_hi, 1)

            def query_weights_rope(g):
                heads = slice(g * HG, (g + 1) * HG)
                copy(Wq1[0][:, heads, KVL:P], wqr1_s[:, heads, :], scale=SCALE)
                for rows in (slice(0, QK2), slice(QK2, P)):
                    last = copy(Wq2s[rows, heads, KVL:P], wqr2_s[:, heads, :], scale=SCALE)
                last.then_inc(wqr_hi, 1)

            def query_weights(g):
                heads = slice(g * HG, (g + 1) * HG)
                act.wait_ge(join_q, g + 1)
                copy(Wq1[0][:, heads, 0:KVL], ps[:, 2 * g, :].rearrange("p (h c) -> p h c", c=KVL), scale=SCALE)
                for rows in (slice(0, QK2), slice(QK2, P)):
                    last = copy(Wq2s[rows, heads, 0:KVL],
                                ps[0:QK2, 2 * g + 1, :].rearrange("p (h c) -> p h c", c=KVL), scale=SCALE)
                last.then_inc(wq_hi, 1)

            def output_weights(s):
                act.wait_ge(join_o, s + 1)
                for j in range(2):
                    last = copy(Bo[0][j * KVL:(j + 1) * KVL, s, :], ps[0:KVL, OB[s], j * HID:(j + 1) * HID])
                last.then_inc(bo_hi, 1)

            def probs(t, s, i):
                t.need(act, et_full, 16, 2 * (s - 1) + i + 1)
                t.need(act, u_full, 8, s - 2)
                copy(PT[0][:, (s - 1) % 2, :, i * P:(i + 1) * P], ET.rearrange("p (a q) -> p a q", q=P)) \
                    .then_inc(pt_hi, 1)

            def exps(t, s, i):
                par = s % 2
                t.need(act, max_done, 16, 2 * s + i + 1)
                t.need(act, et_full, 16, 2 * (s - 2) + i + 1)
                t.need(act, rinv_done, 16, 2 * (s - 2) + i + 1)
                for j in range(2):
                    a = 2 * i + j
                    last = act.activation(E[:, par, a, :], S[:, i, j * SEQ:(j + 1) * SEQ], ACT.Exp,
                                          bias=negmax[:, par, a:a + 1], accum_out=rowsum[:, par, a:a + 1])
                last.then_inc(exp_done, 1)

            def u_lower(t, s):
                t.need(act, u_full, 8, s - 1)
                t.need(act, u_lo, 8, s - 2)
                for j in range(2):
                    last = copy(usum[j * KVL:(j + 1) * KVL, :], U[KVL:2 * KVL, j * SEQ:(j + 1) * SEQ])
                last.then_inc(u_copied, 1)

            def u_split(t, s):
                t.need(act, u_summed, 8, s - 1)
                t.need(act, o_added, 8, s - 3)
                copy(Us[0][:, s % 2, :], usum[:]).then_inc(u_hi, 1)

            def tap_products(t, m):
                if m == 0:
                    t.need(act, basis_loaded, 32, 32)
                    t.need(act, rows_kept, 16, 0)
                if m >= 2:
                    t.need(act, tap_add, TAPS - 1, m - 1)
                for w in range(3):
                    last = copy((rows_s if m == 0 else sprod)[:, w, :], basis_s[:, m, :], scale=ctrl_s[:, w, m:m + 1])
                last.then_inc(tap_mul, 1)

            def q_nope(t, dq):
                t.need(act, q_full, 8, dq + 1)
                t.need(act, qt_full, 8, dq - 1)
                copy(Qt[:, dq % 2, :, 0:KVL], Q.rearrange("p (h f) -> p h f", f=P)[:, :, 0:KVL]) \
                    .then_inc(qnope_done, 1)

            def q_turned(t, dq):
                idx = dq % 8
                g, i = idx // 2, idx % 2
                t.need(act, qt_full, 8, dq + 1)
                t.need(act, scores_full, 16, 16 * (dq // 8 - 1) + 4 * g + 2 + i + 1)
                copy(QT[0][:, g * G4:(g + 1) * G4, i * P:(i + 1) * P], QTp.rearrange("p (h q) -> p h q", q=P)) \
                    .then_inc(qT_hi, 1)

            def unit_hi(u):
                act.wait_ge(sw_turned, u + 1)
                if u == 6:
                    act.wait_ge(scores_full, 2 * LAST)
                for src, (hi, lo) in unit_views(u):
                    last = copy(hi, src)
                last.then_inc(sw_hi, 1)

            def entry(b, least):
                t = Step(b, least)
                for s in range(8 if least < NB else 3):
                    n = PAIRS * least + s
                    if s in (0, 3) and least < NB:
                        tap_products(t, s)
                    if s == 3 and least + 1 < NB:
                        split_k(t, 1)
                    if 1 <= n <= LAST:
                        probs(t, s, 0)
                    if n < LAST:
                        exps(t, s, 0)
                    if 2 <= n <= LAST + 1:
                        u_lower(t, s)
                    if n + LEAD < LAST:
                        q_nope(t, s + LEAD)
                    if s == 1 and least < NB:
                        t.need(act, u_full, 8, 0)
                        t.need(act, z_done, 2, 2)
                        copy(cs[:, :, 0:KVL],
                             zc[:, bass.ds(b * TT * KVL, TT * KVL)].rearrange("p (i f) -> p i f", f=KVL)) \
                            .then_inc(c_hi, 1)
                    if n < LAST:
                        exps(t, s, 1)
                    if 1 <= n <= LAST:
                        probs(t, s, 1)
                    if s == 3 and least + 1 < NB:
                        split_q(t, 1)
                    if 2 <= n <= LAST + 1:
                        u_split(t, s)
                    if s in (0, 1) and least < NB:
                        tap_products(t, s + 1)
                    if s == 4 and least + 2 < NB:
                        split_x(t, 2)
                    if n + LEAD - 1 < LAST:
                        q_turned(t, s + LEAD - 1)
                    for u in units_at(least, s):
                        unit_hi(u)
                    if s in (4, 5) and least < NB:
                        tap_products(t, s)
                    if least == NB and s == 0:
                        split_mx(Step(0, 0), 0, 0)

            def split_mx(t, gc, slot):
                for k in range(KT):
                    t.need(act, xt_full, KT, KT * gc + k + 1)
                    copy(xT[0][:, k, bass.ds(slot * CHUNK, CHUNK)], mXT[:, k, :]).then_inc(xt_hi, 1)

            def chunk(k, c, least):
                if k == len(BLOCKS):
                    return
                t = Step(c, least)
                nf, c0, m0 = BLOCKS[k][3:]
                for j in range(nf):
                    m = m0 + j
                    t.need(act, gate_full, nf, m + 1)
                    t.need(act, h_done, nf, m - 1)
                    act.activation(silu[:, j % 2, :], mG[:, j % 2, :], ACT.Silu).then_inc(silu_done, 1)
                    t.need(act, h_done, nf, m + 1)
                    t.need(act, down_done, nf, m - 3)
                    copy(H[0][:, j % 4, :], htmp[:, j % 2, :]).then_inc(h_hi, 1)
                    if j == 2 and not (k == len(BLOCKS) - 1 and least == NCH - 1):
                        split_mx(t, c0 + 1, 0 if least == NCH - 1 else c + 1)

            act.dma_start(wa_s[:], wa).then_inc(wa_loaded, 16)
            t0 = Step(0, 0)
            act.wait_ge(half_set, 1)
            act.activation(scratch[:], half[:], ACT.Exp)
            act.wait_ge(wa_loaded, 16)
            copy(Wa[0][:], wa_s[:]).then_inc(wa_hi, 1)
            split_x(t0, 0)
            act.wait_ge(r_loaded, 32)
            query_weights_rope(0)
            query_weights_rope(1)
            query_weights(0)
            split_k(t0, 0)
            split_q(t0, 0)
            output_weights(0)
            split_x(t0, 1)
            output_weights(1)
            for q in range(LEAD):
                q_nope(t0, q)
                if q == 0:
                    query_weights(1)
                for s in ([2, 3], [4], [5, 6], [7])[q]:
                    output_weights(s)
                if q >= 1:
                    q_turned(t0, q - 1)
            entries(act, entry)
            chunks(act, chunk)

        @block.vector
        def _(dve):
            def minus(dst, src, hi):
                return dve.tensor_tensor(dst, src, hi.bitcast(F32), ALU.subtract)

            def x_stats(t, dj):
                for i in range(TT):
                    last = dve.bn_stats(st6[:, i, :], X[:, bass.ds((t.b + dj) * TT * HID + i * HID, HID)])
                last.then_inc(fe_chain, 1)

            def x_aggregate(t, dj, between):
                t.need(dve, fe_chain, FE_LINKS, FE_LINKS * dj + 1)
                if between is not None:
                    between()
                for i in range(TT):
                    last = dve.bn_aggr(mv[:, i, :], st6[:, i, :])
                last.then_inc(fe_chain, 1)
                t.need(dve, fe_chain, FE_LINKS, FE_LINKS * dj + 2)
                t.need(dve, xrstd_done, 1, dj)
                dve.tensor_scalar(vare[:], mv[:, :, 1], EPS, None, ALU.add).then_inc(xvar_done, 1)

            def x_norm(t, dj):
                t.need(dve, xrstd_done, 1, dj + 1)
                t.need(dve, z_done, 2, 2 * dj)
                for i in range(TT):
                    last = dve.tensor_scalar(xn[:, i, :], X[:, bass.ds((t.b + dj) * TT * HID + i * HID, HID)],
                                             mv[:, i, 0:1], rstd[:, i:i + 1], ALU.subtract, ALU.mult)
                last.then_inc(xn_done, 1)

            def split_x(t, dj):
                t.need(dve, f_hi, 3, 3 * dj + 1)
                minus(xaT[1][:].rearrange("p k c -> p (k c)"), F, xaT[0][:].rearrange("p k c -> p (k c)")) \
                    .then_inc(f_lo, 1)

            def z_stats(t, dj, i):
                c0 = FE_LINKS * dj + FE_X + FE_Z * i
                t.need(dve, f_full, 5, 5 * dj + 2 + i)
                dve.bn_stats(zst6[:, 0, :], F[:, 0:QL])
                dve.bn_stats(zst6[:, 1, :], F[:, QL:QL + KVL]).then_inc(fe_chain, 1)
                t.need(dve, z_done, 2, 2 * dj + i)
                t.need(dve, fe_chain, FE_LINKS, c0 + 1)
                dve.tensor_tensor(krtmp, F[:, QL + KVL:QL + P], cosT[:, i, :], ALU.mult)
                for a in range(2):
                    last = dve.bn_aggr(zmv[:, a, :], zst6[:, a, :])
                last.then_inc(fe_chain, 1)
                t.need(dve, fe_chain, FE_LINKS, c0 + 2)
                dve.tensor_scalar(zvare[:], zmv[:, :, 1], EPS, None, ALU.add).then_inc(zvar_done, 1)

            def z_norm(t, dj, i):
                t.need(dve, zrstd_done, 2, 2 * dj + i + 1)
                for a, cols in enumerate((slice(0, QL), slice(QL, QL + KVL))):
                    dve.tensor_scalar(ztmp[:, cols], F[:, cols], zmv[:, a, 0:1], zrstd[:, a:a + 1],
                                      ALU.subtract, ALU.mult)
                dve.tensor_tensor(krtmp2.rearrange("p (z e) -> p z e", z=2),
                                  F[:, QL + KVL:QL + P].rearrange("p (z e) -> p z e", z=2)[:, ::-1, :],
                                  sinT[:, i, :].rearrange("p (z e) -> p z e", z=2), ALU.mult).then_inc(f_lo, 1)

            def split_k(t, dj):
                t.need(dve, f_hi, 3, 3 * dj + 2)
                cols = bass.ds((t.b + dj) * SEQ, SEQ)
                minus(kT[1][:, cols], F[:, 0:SEQ], kT[0][:, cols]).then_inc(f_lo, 1)

            def split_q(t, dj):
                t.need(dve, f_hi, 3, 3 * dj + 3)
                minus(ql1[1][:], F[:, 0:SEQ], ql1[0][:])
                minus(ql2[QK2:P, :], F[0:QK2, SEQ:2 * SEQ], ql2[0:QK2, :]).then_inc(f_lo, 1)

            def query_weights_rope(g):
                heads = slice(g * HG, (g + 1) * HG)
                dve.wait_ge(wqr_hi, g + 1)
                for dst, hi, src in (
                        (Wq1[1][:, heads, KVL:P], Wq1[0][:, heads, KVL:P], wqr1_s[:, heads, :]),
                        (Wq2l[:, heads, KVL:P], Wq2s[0:QK2, heads, KVL:P], wqr2_s[:, heads, :])):
                    dve.scalar_tensor_tensor(dst, src, SCALE, hi.bitcast(F32), ALU.mult, ALU.subtract)

            def query_weights(g):
                heads = slice(g * HG, (g + 1) * HG)
                dve.wait_ge(wq_hi, g + 1)
                for dst, hi, src in (
                        (Wq1[1][:, heads, 0:KVL], Wq1[0][:, heads, 0:KVL],
                         ps[:, 2 * g, :].rearrange("p (h c) -> p h c", c=KVL)),
                        (Wq2l[:, heads, 0:KVL], Wq2s[0:QK2, heads, 0:KVL],
                         ps[0:QK2, 2 * g + 1, :].rearrange("p (h c) -> p h c", c=KVL))):
                    last = dve.scalar_tensor_tensor(dst, src, SCALE, hi.bitcast(F32), ALU.mult, ALU.subtract)
                last.then_inc(wq_lo, 1)

            def output_weights(s):
                dve.wait_ge(bo_hi, s + 1)
                for j in range(2):
                    rows = slice(j * KVL, (j + 1) * KVL)
                    last = minus(Bo[1][rows, s, :], ps[0:KVL, OB[s], j * HID:(j + 1) * HID], Bo[0][rows, s, :])
                last.then_inc(bo_lo, 1)

            def maxima(t, s, i):
                t.need(dve, scores_full, 16, 2 * s + i + 1)
                t.need(dve, exp_done, 16, 2 * (s - 2) + i + 1)
                dve.tensor_reduce(negmax[:, s % 2, 2 * i:2 * i + 2], S[:, i, :].rearrange("p (j k) -> p j k", k=SEQ),
                                  AX.X, ALU.max, negate=True).then_inc(max_done, 1)

            def inverse(t, s, i):
                t.need(dve, exp_done, 16, 2 * s + i + 1)
                t.need(dve, norm_done, 16, 2 * (s - 2) + i + 1)
                dve.reciprocal(rinv[:, s % 2, 2 * i:2 * i + 2], rowsum[:, s % 2, 2 * i:2 * i + 2]) \
                    .then_inc(rinv_done, 1)

            def probs(t, s, i):
                t.need(dve, pt_hi, 16, 2 * (s - 1) + i + 1)
                cols = slice(i * P, (i + 1) * P)
                minus(PT[1][:, (s - 1) % 2, :, cols], ET.rearrange("p (a q) -> p a q", q=P),
                      PT[0][:, (s - 1) % 2, :, cols]).then_inc(pt_lo, 1)

            def u_sum(t, s):
                t.need(dve, u_copied, 8, s - 1)
                for j in range(2):
                    rows = slice(j * KVL, (j + 1) * KVL)
                    last = dve.tensor_tensor(usum[rows, :], U[0:KVL, j * SEQ:(j + 1) * SEQ], usum[rows, :], ALU.add)
                last.then_inc(u_summed, 1)

            def rope(t, dq):
                i = (dq % 8) % 2
                t.need(dve, qnope_done, 8, dq + 1)
                t.need(dve, qtok_done, 8, dq)
                r = Q.rearrange("p (h f) -> p h f", f=P)[:, :, KVL:P]
                dve.tensor_tensor(Qt[:, dq % 2, :, KVL:P], r,
                                  cosT[:, i, :].unsqueeze(1).broadcast_to([P, G4, ROPE]), ALU.mult)
                dve.tensor_tensor(rtmp[:].rearrange("p h (z e) -> p h z e", z=2),
                                  r.rearrange("p h (z e) -> p h z e", z=2)[:, :, ::-1, :],
                                  sinT[:, i, :].rearrange("p (z e) -> p z e", z=2).unsqueeze(1)
                                  .broadcast_to([P, G4, 2, ROPE // 2]), ALU.mult).then_inc(rope_mul, 1)

            def q_turned(t, dq):
                idx = dq % 8
                g, i = idx // 2, idx % 2
                t.need(dve, qT_hi, 8, dq + 1)
                heads, cols = slice(g * G4, (g + 1) * G4), slice(i * P, (i + 1) * P)
                minus(QT[1][:, heads, cols], QTp.rearrange("p (h q) -> p h q", q=P), QT[0][:, heads, cols]) \
                    .then_inc(qT_lo, 1)

            def unit_lo(u):
                dve.wait_ge(sw_hi, u + 1)
                for src, (hi, lo) in unit_views(u):
                    last = minus(lo, src, hi)
                last.then_inc(sw_lo, 1)

            def entry(b, least):
                t = Step(b, least)
                for s in range(8 if least < NB else 3):
                    n = PAIRS * least + s
                    more = least + 2 < NB
                    if s == 3 and least >= 1:
                        t.need(dve, o_added, 8, 0)
                        rows = X[:, bass.ds(b * TT * HID - TT * HID, TT * HID)]
                        dve.tensor_tensor(rows, O, rows, ALU.add).then_inc(x_added, 1)
                    if n < LAST:
                        maxima(t, s, 0)
                    if s == 5 and more:
                        split_x(t, 2)
                    if s == 2 and more:
                        x_norm(t, 2)
                    if s == 7 and more:
                        z_norm(t, 2, 0)
                    if s == 0 and least + 1 < NB:
                        z_norm(t, 1, 1)
                    if s == 1 and more:
                        x_stats(t, 2)
                        x_aggregate(t, 2, lambda: maxima(t, 1, 1))
                    elif n < LAST:
                        maxima(t, s, 1)
                    if s == 6 and more:
                        z_stats(t, 2, 0)
                    if s == 3 and least + 1 < NB:
                        split_k(t, 1)
                    if 1 <= n <= LAST:
                        probs(t, s, 0)
                    if n + LEAD - 2 < LAST:
                        q_turned(t, s + LEAD - 2)
                    if n < LAST:
                        inverse(t, s, 0)
                    if 2 <= n <= LAST + 1:
                        u_sum(t, s)
                    if n + LEAD < LAST:
                        rope(t, s + LEAD)
                    if n < LAST:
                        inverse(t, s, 1)
                    if 1 <= n <= LAST:
                        probs(t, s, 1)
                    if s == 7 and more:
                        z_stats(t, 2, 1)
                    if s == 3 and least + 1 < NB:
                        split_q(t, 1)
                    if s == 1 and least < NB:
                        t.need(dve, c_hi, 1, 1)
                        minus(cs[:, :, KVL:2 * KVL],
                              zc[:, bass.ds(b * TT * KVL, TT * KVL)].rearrange("p (i f) -> p i f", f=KVL),
                              cs[:, :, 0:KVL]).then_inc(c_lo, 1)
                    if least == NB and s == 2:
                        t.need(dve, o_added, 8, 0)
                        rows = X[:, bass.ds(b * TT * HID - TT * HID, TT * HID)]
                        dve.tensor_tensor(rows, O, rows, ALU.add).then_inc(x_added, 1)
                    if least == NB - 1:
                        if s in (0, 1):
                            mx_stats(Step(0, 0), 0, 0, range(2 * s, 2 * s + 2))
                        if s == 2:
                            mx_aggregate(Step(0, 0), 0, None)
                        if s in (3, 4):
                            mx_norm(Step(0, 0), 0, 0, range(2 * (s - 3), 2 * (s - 3) + 2))
                    for u in units_at(least, s):
                        unit_lo(u)
                    if least == NB and s == 0:
                        split_mx(Step(0, 0), 0, 0)

            def mx_stats(t, gc, slot, tiles=range(CT)):
                for i in tiles:
                    last = dve.bn_stats(mst6[:, i, :], X[:, bass.ds(slot * CT * HID + i * HID, HID)])
                if CT - 1 in tiles:
                    last.then_inc(m_chain, 1)

            def mx_aggregate(t, gc, between):
                t.need(dve, m_chain, 2, 2 * gc + 1)
                if between is not None:
                    between()
                for i in range(CT):
                    last = dve.bn_aggr(mmv[:, i, :], mst6[:, i, :])
                last.then_inc(m_chain, 1)
                t.need(dve, m_chain, 2, 2 * gc + 2)
                t.need(dve, m_rstd, 1, gc)
                dve.tensor_scalar(mvare[:], mmv[:, :, 1], EPS, None, ALU.add).then_inc(m_var, 1)

            def mx_norm(t, gc, slot, tiles=range(CT)):
                if 0 in tiles:
                    t.need(dve, m_rstd, 1, gc + 1)
                    t.need(dve, xt_full, KT, KT * gc)
                for i in tiles:
                    last = dve.tensor_scalar(xnm[:, i, :], X[:, bass.ds(slot * CT * HID + i * HID, HID)],
                                             mmv[:, i, 0:1], mrstd[:, i:i + 1], ALU.subtract, ALU.mult)
                if CT - 1 in tiles:
                    last.then_inc(m_xn, 1)

            def split_mx(t, gc, slot):
                for k in range(KT):
                    t.need(dve, xt_hi, KT, KT * gc + k + 1)
                    cols = bass.ds(slot * CHUNK, CHUNK)
                    minus(xT[1][:, k, cols], mXT[:, k, :], xT[0][:, k, cols]).then_inc(xt_lo, 1)

            def product(t, nf, m, j, scalar):
                t.need(dve, silu_done, nf, m + 1)
                t.need(dve, up_full, nf, m + 1)
                t.need(dve, h_lo, nf, m - 1)
                dve.scalar_tensor_tensor(htmp[:, j % 2, :], mUP[:, j % 2, :], scalar, silu[:, j % 2, :],
                                         ALU.mult, ALU.mult).then_inc(h_done, 1)

            def h_split(t, nf, m, j):
                t.need(dve, h_hi, nf, m)
                minus(H[1][:, (j - 1) % 4, :], htmp[:, (j - 1) % 2, :], H[0][:, (j - 1) % 4, :]).then_inc(h_lo, 1)

            def add_output(t, nf, m, gc, slot):
                t.need(dve, down_done, nf, m)
                rows = X[:, bass.ds(slot * CT * HID, CT * HID)]
                dve.tensor_tensor(rows, mO.rearrange("p a b -> p (a b)"), rows, ALU.add).then_inc(m_added, 1)

            def chunk(k, c, least):
                t = Step(c, least)
                if k == len(BLOCKS):
                    h_split(t, 0, M_ALL, 0)
                    add_output(t, 0, M_ALL, 0, NCH - 1)
                    return
                nf, c0, m0 = BLOCKS[k][3:]
                more = not (k == len(BLOCKS) - 1 and least == NCH - 1)
                slot = 0 if least == NCH - 1 else c + 1
                for j in range(nf):
                    m = m0 + j
                    scalar = d_s[:, j:j + 1] if k == 1 else 1.0
                    if j == 0 and more:
                        mx_stats(t, c0 + 1, slot)
                        mx_aggregate(t, c0 + 1, lambda: product(t, nf, m, j, scalar))
                    else:
                        product(t, nf, m, j, scalar)
                    if j > 0 or k > 0 or least > 0:
                        h_split(t, nf, m, j)
                    if j == 1 and (k > 0 or least > 0):
                        add_output(t, nf, m0, c0, NCH - 1 if least == 0 else c - 1)
                    if more:
                        if j == 1:
                            mx_norm(t, c0 + 1, slot)
                        if j == 2:
                            split_mx(t, c0 + 1, slot)
                    if k == 0 and least == NCH - 1:
                        if j == 5:
                            dve.wait_ge(cw_joined, KT)
                            dve.tensor_copy(Cz[0][:], winz_s[:])
                            dve.tensor_copy(Co[0][:], wout_s[:])
                            dve.tensor_copy(Cx[0][:], mXT).then_inc(cw_hi, 1)
                        if j == 6:
                            dve.wait_ge(cw_hi, 1)
                            minus(Cz[1][:], winz_s[:], Cz[0][:])
                            minus(Co[1][:], wout_s[:], Co[0][:])
                            minus(Cx[1][:], mXT, Cx[0][:]).then_inc(cw_lo, 1)

            t0 = Step(0, 0)
            dve.wait_ge(x0_loaded, 16)
            x_stats(t0, 0)
            x_aggregate(t0, 0, None)
            x_norm(t0, 0)
            dve.wait_ge(wa_hi, 1)
            minus(Wa[1][:], wa_s[:], Wa[0][:]).then_inc(wa_lo, 1)
            split_x(t0, 0)
            dve.wait_ge(first_loaded, 16 * 4)
            z_stats(t0, 0, 0)
            z_norm(t0, 0, 0)
            z_stats(t0, 0, 1)
            z_norm(t0, 0, 1)
            dve.wait_ge(x1_loaded, 16)
            x_stats(t0, 1)
            x_aggregate(t0, 1, None)
            query_weights_rope(0)
            x_norm(t0, 1)
            split_k(t0, 0)
            query_weights_rope(1)
            query_weights(0)
            split_q(t0, 0)
            output_weights(0)
            split_x(t0, 1)
            output_weights(1)
            for q in range(LEAD):
                rope(t0, q)
                if q == 0:
                    query_weights(1)
                if q == 2:
                    z_norm(t0, 1, 0)
                for s in ([2, 3], [4], [5, 6], [7])[q]:
                    output_weights(s)
                if q in (1, 3):
                    z_stats(t0, 1, q // 2)
                if 1 <= q < LEAD - 1:
                    q_turned(t0, q - 1)
            dve.wait_ge(x_loaded, 16)
            entries(dve, entry)
            chunks(dve, chunk)

        @block.gpsimd
        def _(pool):
            def x_rsqrt(t, dj):
                t.need(pool, xvar_done, 1, dj + 1)
                t.need(pool, xn_done, 1, dj)
                pool.tensor_tensor(rstd[:], vare[:], half[:, 0:TT], ALU.pow).then_inc(xrstd_done, 1)

            def z_rsqrt(t, dj, i):
                t.need(pool, zvar_done, 2, 2 * dj + i + 1)
                pool.tensor_tensor(zrstd[:], zvare[:], half[:, 0:2], ALU.pow).then_inc(zrstd_done, 1)

            def z_affine(t, dj, i):
                t.need(pool, f_lo, 5, 5 * dj + 2 + i)
                pool.tensor_tensor(ztmp, ztmp, lnws[:], ALU.mult).then_inc(zscaled, 1)
                if i == 0:
                    t.need(pool, f_full, 5, 5 * dj)
                pool.tensor_tensor(zkn[:, i, KVL:P], krtmp, krtmp2, ALU.add)
                t.need(pool, zscaled, 2, 2 * dj + i + 1)
                pool.tensor_tensor(zkn[:, i, 0:KVL], ztmp[:, QL:], lnbs[:, QL:], ALU.add)
                pool.tensor_tensor(zc[:, bass.ds((t.b + dj) * TT * KVL + i * KVL, KVL)], ztmp[:, QL:], lnbs[:, QL:],
                                   ALU.add)
                pool.tensor_tensor(zq[:, i, :], ztmp[:, 0:QL], lnbs[:, 0:QL], ALU.add).then_inc(z_done, 1)

            def rope_sum(t, dq):
                t.need(pool, rope_mul, 8, dq + 1)
                dst = Qt[:, dq % 2, :, KVL:P]
                pool.tensor_tensor(dst, dst, rtmp[:], ALU.add).then_inc(qtok_done, 1)

            def normalise(t, s, i):
                t.need(pool, rinv_done, 16, 2 * s + i + 1)
                e = E[:, s % 2, 2 * i:2 * i + 2, :]
                pool.tensor_tensor(e, e, rinv[:, s % 2, 2 * i:2 * i + 2].unsqueeze(2).broadcast_to([P, 2, SEQ]),
                                   ALU.mult).then_inc(norm_done, 1)

            def u_rest(t, s):
                t.need(pool, u_hi, 8, s - 1)
                pool.tensor_tensor(Us[1][:, s % 2, :], usum[:], Us[0][:, s % 2, :].bitcast(F32), ALU.subtract) \
                    .then_inc(u_lo, 1)

            def tap_sum(t, m):
                t.need(pool, tap_mul, TAPS, m + 1)
                if m >= 2:
                    t.need(pool, tap_add, TAPS - 1, m - 1)
                pool.tensor_tensor(rows_s[:], rows_s[:], sprod[:], ALU.add).then_inc(tap_add, 1)

            def entry(b, least):
                t = Step(b, least)
                for s in range(8 if least < NB else 2):
                    n = PAIRS * least + s
                    more = least + 2 < NB
                    if s in (1, 2, 3) and least < NB:
                        tap_sum(t, s)
                    if s in (5, 6) and least < NB:
                        tap_sum(t, s - 1)
                    if s == 1 and more:
                        x_rsqrt(t, 2)
                    if s == 7 and more:
                        z_affine(t, 2, 0)
                    if s == 0 and least + 1 < NB:
                        z_affine(t, 1, 1)
                    if n < LAST:
                        normalise(t, s, 0)
                    if s == 6 and more:
                        z_rsqrt(t, 2, 0)
                    if n + LEAD < LAST:
                        rope_sum(t, s + LEAD)
                    if 2 <= n <= LAST + 1:
                        u_rest(t, s)
                    if s == 7 and more:
                        z_rsqrt(t, 2, 1)
                    if n < LAST:
                        normalise(t, s, 1)
                    if least == NB - 1 and s == 2:
                        m_rsqrt(Step(0, 0), 0)

            def m_rsqrt(t, gc):
                t.need(pool, m_var, 1, gc + 1)
                t.need(pool, m_xn, 1, gc)
                pool.tensor_tensor(mrstd[:], mvare[:], half[:, 0:CT], ALU.pow).then_inc(m_rstd, 1)

            t0 = Step(0, 0)
            pool.memset(half[:], -0.5).then_inc(half_set, 1)
            pool.memset(cs[:].bitcast(F32), 0.0).then_inc(zeroed, 1)
            pool.wait_ge(zeroed, 1)
            x_rsqrt(t0, 0)
            z_rsqrt(t0, 0, 0)
            z_affine(t0, 0, 0)
            z_rsqrt(t0, 0, 1)
            z_affine(t0, 0, 1)
            x_rsqrt(t0, 1)
            for q in range(LEAD):
                rope_sum(t0, q)
                if q == 1:
                    z_rsqrt(t0, 1, 0)
                if q == 2:
                    z_affine(t0, 1, 0)
            z_rsqrt(t0, 1, 1)
            entries(pool, entry)
            for gc in range(1, NCH * len(BLOCKS)):
                m_rsqrt(t0, gc)

        @block.sync
        def _(sp):
            HALF_X = 2 * TT
            xd = x.rearrange("t p d -> p t d")
            xs = X[:, :].rearrange("p (t d) -> p t d", d=HID)
            sp.dma_start(xs[:, 0:TT, :], xd[:, 0:TT, :]).then_inc(x0_loaded, 16)
            sp.dma_start(ident[:], ident_in).then_inc(ident_loaded, 16)
            for g in range(NH // HG):
                if g == 1:
                    for dst, src in ((cosT, cos), (sinT, sin), (lnws, lnw), (lnbs, lnb)):
                        sp.dma_start(dst[:], src).then_inc(first_loaded, 16)
                    sp.dma_start(xs[:, TT:HALF_X, :], xd[:, TT:HALF_X, :]).then_inc(x1_loaded, 16)
                heads, loaded = slice(g * HG, (g + 1) * HG), (qa_loaded, qb_loaded)[g]
                sp.dma_start(wk_s[:, heads, :], wk[:, heads, :]).then_inc(loaded, 16)
                sp.dma_start(wqb_s[:, heads, :], wqb[:, heads, :]).then_inc(loaded, 16)
            for dst, src in ((wqr1_s, wqr1), (wqr2_s, wqr2)):
                sp.dma_start(dst[:], src).then_inc(r_loaded, 16)
            for dst, src in ((wv_s, wv), (wo_s, wo)):
                sp.dma_start(dst[:], src).then_inc(o_loaded, 16)
            sp.dma_start(xs[:, HALF_X:, :], xd[:, HALF_X:, :]).then_inc(x_loaded, 16)
            for b in range(NB):
                if b == 1:
                    sp.wait_ge(bo_lo, PAIRS)
                if b >= 1:
                    sp.wait_ge(tap_add, b * (TAPS - 1))
                    sp.dma_start(Wn[:, :, b - 1, :], rows_s[:]).then_inc(rows_kept, 16)
                sp.dma_start(basis_s[:].rearrange("p m c -> p (m c)"), basis[b]).then_inc(basis_loaded, 16)
                sp.dma_start(ctrl_s[:], ctrl[b]).then_inc(basis_loaded, 16)
            sp.wait_ge(tap_add, NB * (TAPS - 1))
            sp.dma_start(Wn[:, :, NB - 1, :], rows_s[:]).then_inc(rows_kept, 16)
            sp.wait_ge(x_added, NB)
            for dst, src in ((wconv_s, w_conv), (winx_s, w_inx), (winz_s, w_inz), (wout_s, w_out), (d_s, d_in)):
                sp.dma_start(dst[:], src).then_inc(cw_loaded, 16)
            for c in range(NCH):
                sp.wait_ge(m_added, 2 * NCH + c + 1)
                sp.dma_start(out[c * CT:(c + 1) * CT].rearrange("t p d -> p t d"),
                             xs[:, c * CT:(c + 1) * CT, :]).then_inc(stored, 16)
            sp.wait_ge(stored, 16 * NCH)


def spline_basis():
    n = ROWS * HID
    t = np.linspace(0.0, CTRL - 1.0, n, dtype=np.float64)
    i = np.clip(np.floor(t).astype(np.int64), 0, CTRL - 2)
    f = (t - i).astype(np.float32).astype(np.float64)
    first = np.clip(i.reshape(ROWS, HID)[:, 0] - 1, 0, CTRL - TAPS)
    f2, f3 = f * f, f * f * f
    parts = [0.5 * (-f + 2 * f2 - f3), 0.5 * (2 - 5 * f2 + 3 * f3), 0.5 * (f + 4 * f2 - 3 * f3), 0.5 * (f3 - f2)]
    basis = np.zeros((ROWS, TAPS, HID))
    row, col = np.divmod(np.arange(n), HID)
    for k, part in enumerate(parts):
        tap = np.clip(i + k - 1, 0, CTRL - 1) - first[row]
        np.add.at(basis, (row, tap, col), part)
    return basis.astype(np.float32).reshape(RT, P, TAPS * HID), first


def rope_tables():
    inv = 1.0 / 10000.0 ** (np.arange(0, ROPE, 2, dtype=np.float32) / ROPE)
    a = np.outer(np.arange(SEQ, dtype=np.float32), inv)
    cos = np.concatenate([np.cos(a), np.cos(a)], 1).astype(np.float32)
    sin = np.concatenate([-np.sin(a), np.sin(a)], 1).astype(np.float32)
    return [t.reshape(TT, P, ROPE).transpose(1, 0, 2) for t in (cos, sin)]


def kernel(**inputs):
    import concourse.bacc as bacc
    from concourse.bass_utils import run_bass_kernel_spmd

    a = {k: np.asarray(w) for k, w in inputs.items()}
    A, C, FN = "L0_attn_a_", "L0_attn_b_", "L0_ffn_"
    kvb = a[A + "kv_b_w"].reshape(NH, NOPE + DV, KVL)
    qr = a[A + "q_rope_w"].T
    basis, first = spline_basis()
    cos, sin = rope_tables()
    win = first[:, None] + np.arange(TAPS)
    ctrl = np.stack([a[FN + n][win].reshape(RT, P, TAPS) for n in ("gate_cp", "up_cp", "down_cp")], 2)
    w_in = a[C + "W_in"]
    wide = lambda w: np.broadcast_to(w, (P, w.shape[0]))
    arrays = {
        "x": a[A + "hidden_states"].reshape(NTILE, P, HID),
        "wa": np.concatenate([a[A + "q_a_w"], a[A + "kv_a_w"]], 0).T.reshape(KT, P, QL + P).transpose(1, 0, 2),
        "lnw": wide(np.concatenate([a[A + "q_a_ln_w"], a[A + "kv_a_ln_w"]])),
        "lnb": wide(np.concatenate([a[A + "q_a_ln_b"], a[A + "kv_a_ln_b"]])),
        "wqb": a[A + "q_b_w"].reshape(NH, NOPE, QL).transpose(1, 0, 2),
        "wk": kvb[:, :NOPE].transpose(1, 0, 2),
        "wv": kvb[:, NOPE:].transpose(1, 0, 2),
        "wqr1": qr[:P].reshape(P, NH, ROPE),
        "wqr2": qr[P:].reshape(QK2, NH, ROPE),
        "wo": a[A + "o_w"].T.reshape(NH, DV, HID).transpose(1, 0, 2),
        "cos": cos, "sin": sin, "ident_in": np.eye(P, dtype=np.float32),
        "basis": basis, "ctrl": ctrl,
        "w_inx": w_in[:CONV].reshape(4, P, HID).transpose(1, 0, 2),
        "w_inz": w_in[CONV:].T.reshape(KT, P, CONV).transpose(1, 0, 2),
        "w_conv": a[C + "conv_w"].T.reshape(4, P, CONV).transpose(1, 0, 2),
        "w_out": a[C + "W_out"].T.reshape(4, P, HID).transpose(1, 0, 2),
        "d_in": a[C + "D"].reshape(4, P).T,
    }
    nc = bacc.Bacc("TRN2", target_bir_lowering=False, num_devices=1)
    feeds, aps = {}, {}
    for name, w in arrays.items():
        w = np.ascontiguousarray(w)
        feeds["in_" + name] = w
        aps[name] = nc.dram_tensor("in_" + name, w.shape, mybir.dt.from_np(w.dtype), kind="ExternalInput").ap()
    aps["out"] = nc.dram_tensor("out_x", (NTILE, P, HID), F32, kind="ExternalOutput").ap()
    build(nc, **aps)
    r = run_bass_kernel_spmd(nc, [feeds], core_ids=[0])
    return r.results[0]["out_x"].reshape(NB, SEQ, HID)
```
